# Optimizing a Trainium2 kernel written in Bass

```python
import numpy as np
import jax
import jax.numpy as jnp

def _softmax(x, axis=-1):
    return jax.nn.softmax(x, axis=axis)

def _gelu(x):
    return jax.nn.gelu(x, approximate=True)

def _silu(x):
    return jax.nn.silu(x)

def _sigmoid(x):
    return jax.nn.sigmoid(x)

def _layernorm(x, axis=-1, eps=1e-05):
    m = jnp.mean(x, axis=axis, keepdims=True)
    v = jnp.var(x, axis=axis, keepdims=True)
    return (x - m) / jnp.sqrt(v + eps)

def _scatter_add(tgt, idx, src, axis=0):
    return tgt.at[idx].add(src)

def _segment_sum(src, seg, n):
    return jax.ops.segment_sum(src, seg, n)
kernel_name = 'mk_early_fusion_d1_tok_img768_r4_316690'

def setup_inputs(seed: int=0):
    np.random.seed(seed)
    _w = jnp.asarray

    def _rec_inputs():
        import jax
        import jax.numpy as jnp
        _rk = jax.random.key(seed)
        x = 7.57192e-06 + 1.00007 * jax.random.normal(jax.random.fold_in(_rk, 1), (16, 3, 112, 112), jnp.float32)
        txt = -6.31349e-07 + 0.985278 * jax.random.normal(jax.random.fold_in(_rk, 2), (16, 128, 192), jnp.float32)
        return (x, txt)
    x, txt = _rec_inputs()

    def _L0_tok_setup():
        import jax, jax.numpy as jnp
        import numpy as np
        B, IN, IMG = (64, 3, 224)
        PATCH, LEVELS, D = (16, 4, 192)
        ISQ2 = 0.7071067811865476
        DN = ('NCHW', 'OIHW', 'NCHW')

        def conv(x, w, b=None, stride=1, pad=((0, 0), (0, 0)), groups=1):
            y = jax.lax.conv_general_dilated(x, w, (stride, stride), pad, dimension_numbers=DN, feature_group_count=groups)
            return y if b is None else y + b[None, :, None, None]

        def dwconv(x, wd, wp, bp):
            y = conv(x, wd, pad=((1, 1), (1, 1)), groups=x.shape[1])
            return conv(y, wp, bp)

        def haar_dwt2(x):
            xe, xo = (x[..., ::2], x[..., 1::2])
            lo_w, hi_w = ((xe + xo) * ISQ2, (xe - xo) * ISQ2)

            def split_h(t):
                te, to = (t[..., ::2, :], t[..., 1::2, :])
                return ((te + to) * ISQ2, (te - to) * ISQ2)
            ll, lh = split_h(lo_w)
            hl, hh = split_h(hi_w)
            return (ll, lh, hl, hh)

        def wavelet_packet(x):
            f = x
            for _ in range(LEVELS):
                b, k, h, w = f.shape
                ll, lh, hl, hh = haar_dwt2(f)
                bands = jnp.stack([ll, lh, hl, hh], axis=1)
                bands = bands.reshape(b, 4, k // IN, IN, h // 2, w // 2)
                f = jnp.transpose(bands, (0, 2, 1, 3, 4, 5)).reshape(b, 4 * k, h // 2, w // 2)
            return f

        def gelu(x):
            return jax.nn.gelu(x, approximate=False)

        def forward(x, pl_w, pl_b, pl_dw, pl_pw, pl_pwb, pg_w1, pg_b1, pg_dw, pg_pw, pg_pwb, pg_w2, pg_b2, alpha, f1_dw, f1_pw, f1_pwb, f2_dw, f2_pw, f2_pwb, f3_dw, f3_pw, f3_pwb, ln_g, ln_b, cls):
            loc = conv(x, pl_w, pl_b, stride=PATCH)
            loc = dwconv(gelu(loc), pl_dw, pl_pw, pl_pwb)
            g = wavelet_packet(x)
            g = gelu(conv(g, pg_w1, pg_b1))
            g = gelu(dwconv(g, pg_dw, pg_pw, pg_pwb))
            glob = conv(g, pg_w2, pg_b2)
            gate = 0.5 * (jnp.tanh(alpha) + 1.0)
            h = (1.0 - gate) * loc + gate * glob
            h = jax.nn.relu(dwconv(h, f1_dw, f1_pw, f1_pwb))
            h = jax.nn.relu(dwconv(h, f2_dw, f2_pw, f2_pwb))
            h = dwconv(loc + h, f3_dw, f3_pw, f3_pwb)
            t = jnp.transpose(h.reshape(h.shape[0], D, -1), (0, 2, 1))
            mu = jnp.mean(t, -1, keepdims=True)
            var = jnp.mean((t - mu) ** 2, -1, keepdims=True)
            t = (t - mu) / jnp.sqrt(var + 1e-05) * ln_g + ln_b
            cls_tok = jnp.broadcast_to(cls, (t.shape[0], 1, D))
            return jnp.concatenate([cls_tok, t], axis=1)
        key = jax.random.key(seed)
        ks = jax.random.split(key, 32)

        def rn(i, shape, s=0.02):
            return jax.random.normal(ks[i], shape, jnp.float32) * s
        KW = IN * 4 ** LEVELS
        return {'x': jax.random.normal(ks[0], (B, IN, IMG, IMG), jnp.float32), 'pl_w': rn(1, (D, IN, PATCH, PATCH)), 'pl_b': rn(2, (D,)), 'pl_dw': rn(3, (D, 1, 3, 3)), 'pl_pw': rn(4, (D, D, 1, 1)), 'pl_pwb': rn(5, (D,)), 'pg_w1': rn(6, (D, KW, 1, 1)), 'pg_b1': rn(7, (D,)), 'pg_dw': rn(8, (D, 1, 3, 3)), 'pg_pw': rn(9, (D, D, 1, 1)), 'pg_pwb': rn(10, (D,)), 'pg_w2': rn(11, (D, D, 1, 1)), 'pg_b2': rn(12, (D,)), 'alpha': jnp.zeros((1, D, 1, 1), jnp.float32), 'f1_dw': rn(13, (D, 1, 3, 3)), 'f1_pw': rn(14, (D, D, 1, 1)), 'f1_pwb': rn(15, (D,)), 'f2_dw': rn(16, (D, 1, 3, 3)), 'f2_pw': rn(17, (D, D, 1, 1)), 'f2_pwb': rn(18, (D,)), 'f3_dw': rn(19, (D, 1, 3, 3)), 'f3_pw': rn(20, (D, D, 1, 1)), 'f3_pwb': rn(21, (D,)), 'ln_g': jnp.ones((D,), jnp.float32), 'ln_b': jnp.zeros((D,), jnp.float32), 'cls': rn(22, (1, 1, D))}
    _L0_tok_all = _L0_tok_setup()
    _L0_tok_in = {k: v for k, v in _L0_tok_all.items() if k in ('pl_w', 'pl_b', 'pl_dw', 'pl_pw', 'pl_pwb', 'pg_w1', 'pg_b1', 'pg_dw', 'pg_pw', 'pg_pwb', 'pg_w2', 'pg_b2', 'alpha', 'f1_dw', 'f1_pw', 'f1_pwb', 'f2_dw', 'f2_pw', 'f2_pwb', 'f3_dw', 'f3_pw', 'f3_pwb', 'ln_g', 'ln_b', 'cls')}
    del _L0_tok_all

    def _L0_attn_setup():
        import jax, jax.numpy as jnp
        import numpy as np
        B, N, C = (32, 577, 192)
        H = 12
        D = C // H
        key = jax.random.key(seed)
        ks = jax.random.split(key, 4)
        x = jax.random.normal(ks[0], (B, N, C), dtype=jnp.float32)
        w_qkv = jax.random.normal(ks[1], (C, 3 * C), dtype=jnp.float32) * C ** (-0.5)
        b_qkv = jnp.zeros((3 * C,), dtype=jnp.float32)
        scale = jnp.ones((H,), dtype=jnp.float32) * D ** (-0.5)
        w_proj = jax.random.normal(ks[2], (C, C), dtype=jnp.float32) * C ** (-0.5)
        b_proj = jnp.zeros((C,), dtype=jnp.float32)
        return {'x': x, 'w_qkv': w_qkv, 'b_qkv': b_qkv, 'scale': scale, 'w_proj': w_proj, 'b_proj': b_proj}
    _L0_attn_all = _L0_attn_setup()
    _L0_attn_in = {k: v for k, v in _L0_attn_all.items() if k in ('w_qkv', 'b_qkv', 'scale', 'w_proj', 'b_proj')}
    del _L0_attn_all

    def _L0_ffn_setup():
        import jax, jax.numpy as jnp
        import numpy as np
        NHEAD = 12
        EPS_Z = 1e-05
        EPS_LN = 1e-05

        def _zscore_last(t, n):
            m = t.mean(axis=-1, keepdims=True)
            var = ((t - m) ** 2).sum(axis=-1, keepdims=True) / (n - 1)
            return (t - m) / (jnp.sqrt(var) + EPS_Z)

        def _layernorm(x, g, b):
            m = x.mean(axis=-1, keepdims=True)
            v = ((x - m) ** 2).mean(axis=-1, keepdims=True)
            return (x - m) * jax.lax.rsqrt(v + EPS_LN) * g + b
        key = jax.random.key(seed)
        ks = jax.random.split(key, 20)
        B, T, D, FF, E = (2, 256, 192, 768, 4)
        p = lambda k, shape: jax.random.normal(k, shape, jnp.float32) * 0.02
        return {'src': jax.random.normal(ks[0], (B, T, D), jnp.float32), 'frac': jax.random.uniform(ks[1], (B, T), jnp.float32), 'Wq': p(ks[2], (D, D)), 'bq': jnp.zeros((D,), jnp.float32), 'Wk': p(ks[3], (D, D)), 'bk': jnp.zeros((D,), jnp.float32), 'Wv': p(ks[4], (D, D)), 'bv': jnp.zeros((D,), jnp.float32), 'Wo': p(ks[5], (D, D)), 'bo': jnp.zeros((D,), jnp.float32), 'gamma': jnp.float32(1.0), 'ln1_g': jnp.ones((D,), jnp.float32), 'ln1_b': jnp.zeros((D,), jnp.float32), 'ln2_g': jnp.ones((D,), jnp.float32), 'ln2_b': jnp.zeros((D,), jnp.float32), 'Wg': p(ks[6], (E, D)), 'bg': jnp.zeros((E,), jnp.float32), 'W1': p(ks[7], (E, D, FF)), 'b1': jnp.zeros((E, FF), jnp.float32), 'W2': p(ks[8], (E, FF, D)), 'b2': jnp.zeros((E, D), jnp.float32)}
    _L0_ffn_all = _L0_ffn_setup()
    _L0_ffn_in = {k: v for k, v in _L0_ffn_all.items() if k in ('frac', 'Wq', 'bq', 'Wk', 'bk', 'Wv', 'bv', 'Wo', 'bo', 'gamma', 'ln1_g', 'ln1_b', 'ln2_g', 'ln2_b', 'Wg', 'bg', 'W1', 'b1', 'W2', 'b2')}
    del _L0_ffn_all
    return {'x': x, 'txt': txt, 'L0_tok_pl_w': _L0_tok_in['pl_w'], 'L0_tok_pl_b': _L0_tok_in['pl_b'], 'L0_tok_pl_dw': _L0_tok_in['pl_dw'], 'L0_tok_pl_pw': _L0_tok_in['pl_pw'], 'L0_tok_pl_pwb': _L0_tok_in['pl_pwb'], 'L0_tok_pg_w1': _L0_tok_in['pg_w1'], 'L0_tok_pg_b1': _L0_tok_in['pg_b1'], 'L0_tok_pg_dw': _L0_tok_in['pg_dw'], 'L0_tok_pg_pw': _L0_tok_in['pg_pw'], 'L0_tok_pg_pwb': _L0_tok_in['pg_pwb'], 'L0_tok_pg_w2': _L0_tok_in['pg_w2'], 'L0_tok_pg_b2': _L0_tok_in['pg_b2'], 'L0_tok_alpha': _L0_tok_in['alpha'], 'L0_tok_f1_dw': _L0_tok_in['f1_dw'], 'L0_tok_f1_pw': _L0_tok_in['f1_pw'], 'L0_tok_f1_pwb': _L0_tok_in['f1_pwb'], 'L0_tok_f2_dw': _L0_tok_in['f2_dw'], 'L0_tok_f2_pw': _L0_tok_in['f2_pw'], 'L0_tok_f2_pwb': _L0_tok_in['f2_pwb'], 'L0_tok_f3_dw': _L0_tok_in['f3_dw'], 'L0_tok_f3_pw': _L0_tok_in['f3_pw'], 'L0_tok_f3_pwb': _L0_tok_in['f3_pwb'], 'L0_tok_ln_g': _L0_tok_in['ln_g'], 'L0_tok_ln_b': _L0_tok_in['ln_b'], 'L0_tok_cls': _L0_tok_in['cls'], 'L0_attn_w_qkv': _L0_attn_in['w_qkv'], 'L0_attn_b_qkv': _L0_attn_in['b_qkv'], 'L0_attn_scale': _L0_attn_in['scale'], 'L0_attn_w_proj': _L0_attn_in['w_proj'], 'L0_attn_b_proj': _L0_attn_in['b_proj'], 'L0_ffn_frac': _L0_ffn_in['frac'], 'L0_ffn_Wq': _L0_ffn_in['Wq'], 'L0_ffn_bq': _L0_ffn_in['bq'], 'L0_ffn_Wk': _L0_ffn_in['Wk'], 'L0_ffn_bk': _L0_ffn_in['bk'], 'L0_ffn_Wv': _L0_ffn_in['Wv'], 'L0_ffn_bv': _L0_ffn_in['bv'], 'L0_ffn_Wo': _L0_ffn_in['Wo'], 'L0_ffn_bo': _L0_ffn_in['bo'], 'L0_ffn_gamma': _L0_ffn_in['gamma'], 'L0_ffn_ln1_g': _L0_ffn_in['ln1_g'], 'L0_ffn_ln1_b': _L0_ffn_in['ln1_b'], 'L0_ffn_ln2_g': _L0_ffn_in['ln2_g'], 'L0_ffn_ln2_b': _L0_ffn_in['ln2_b'], 'L0_ffn_Wg': _L0_ffn_in['Wg'], 'L0_ffn_bg': _L0_ffn_in['bg'], 'L0_ffn_W1': _L0_ffn_in['W1'], 'L0_ffn_b1': _L0_ffn_in['b1'], 'L0_ffn_W2': _L0_ffn_in['W2'], 'L0_ffn_b2': _L0_ffn_in['b2']}

def reference(x, txt, L0_tok_pl_w, L0_tok_pl_b, L0_tok_pl_dw, L0_tok_pl_pw, L0_tok_pl_pwb, L0_tok_pg_w1, L0_tok_pg_b1, L0_tok_pg_dw, L0_tok_pg_pw, L0_tok_pg_pwb, L0_tok_pg_w2, L0_tok_pg_b2, L0_tok_alpha, L0_tok_f1_dw, L0_tok_f1_pw, L0_tok_f1_pwb, L0_tok_f2_dw, L0_tok_f2_pw, L0_tok_f2_pwb, L0_tok_f3_dw, L0_tok_f3_pw, L0_tok_f3_pwb, L0_tok_ln_g, L0_tok_ln_b, L0_tok_cls, L0_attn_w_qkv, L0_attn_b_qkv, L0_attn_scale, L0_attn_w_proj, L0_attn_b_proj, L0_ffn_frac, L0_ffn_Wq, L0_ffn_bq, L0_ffn_Wk, L0_ffn_bk, L0_ffn_Wv, L0_ffn_bv, L0_ffn_Wo, L0_ffn_bo, L0_ffn_gamma, L0_ffn_ln1_g, L0_ffn_ln1_b, L0_ffn_ln2_g, L0_ffn_ln2_b, L0_ffn_Wg, L0_ffn_bg, L0_ffn_W1, L0_ffn_b1, L0_ffn_W2, L0_ffn_b2):
    import jax
    import jax.numpy as jnp

    def _L0_tok_ref(x, pl_w, pl_b, pl_dw, pl_pw, pl_pwb, pg_w1, pg_b1, pg_dw, pg_pw, pg_pwb, pg_w2, pg_b2, alpha, f1_dw, f1_pw, f1_pwb, f2_dw, f2_pw, f2_pwb, f3_dw, f3_pw, f3_pwb, ln_g, ln_b, cls):
        import jax, jax.numpy as jnp
        import numpy as np
        B, IN, IMG = (64, 3, 224)
        PATCH, LEVELS, D = (16, 4, 192)
        ISQ2 = 0.7071067811865476
        DN = ('NCHW', 'OIHW', 'NCHW')

        def conv(x, w, b=None, stride=1, pad=((0, 0), (0, 0)), groups=1):
            y = jax.lax.conv_general_dilated(x, w, (stride, stride), pad, dimension_numbers=DN, feature_group_count=groups)
            return y if b is None else y + b[None, :, None, None]

        def dwconv(x, wd, wp, bp):
            y = conv(x, wd, pad=((1, 1), (1, 1)), groups=x.shape[1])
            return conv(y, wp, bp)

        def haar_dwt2(x):
            xe, xo = (x[..., ::2], x[..., 1::2])
            lo_w, hi_w = ((xe + xo) * ISQ2, (xe - xo) * ISQ2)

            def split_h(t):
                te, to = (t[..., ::2, :], t[..., 1::2, :])
                return ((te + to) * ISQ2, (te - to) * ISQ2)
            ll, lh = split_h(lo_w)
            hl, hh = split_h(hi_w)
            return (ll, lh, hl, hh)

        def wavelet_packet(x):
            f = x
            for _ in range(LEVELS):
                b, k, h, w = f.shape
                ll, lh, hl, hh = haar_dwt2(f)
                bands = jnp.stack([ll, lh, hl, hh], axis=1)
                bands = bands.reshape(b, 4, k // IN, IN, h // 2, w // 2)
                f = jnp.transpose(bands, (0, 2, 1, 3, 4, 5)).reshape(b, 4 * k, h // 2, w // 2)
            return f

        def gelu(x):
            return jax.nn.gelu(x, approximate=False)

        def forward(x, pl_w, pl_b, pl_dw, pl_pw, pl_pwb, pg_w1, pg_b1, pg_dw, pg_pw, pg_pwb, pg_w2, pg_b2, alpha, f1_dw, f1_pw, f1_pwb, f2_dw, f2_pw, f2_pwb, f3_dw, f3_pw, f3_pwb, ln_g, ln_b, cls):
            loc = conv(x, pl_w, pl_b, stride=PATCH)
            loc = dwconv(gelu(loc), pl_dw, pl_pw, pl_pwb)
            g = wavelet_packet(x)
            g = gelu(conv(g, pg_w1, pg_b1))
            g = gelu(dwconv(g, pg_dw, pg_pw, pg_pwb))
            glob = conv(g, pg_w2, pg_b2)
            gate = 0.5 * (jnp.tanh(alpha) + 1.0)
            h = (1.0 - gate) * loc + gate * glob
            h = jax.nn.relu(dwconv(h, f1_dw, f1_pw, f1_pwb))
            h = jax.nn.relu(dwconv(h, f2_dw, f2_pw, f2_pwb))
            h = dwconv(loc + h, f3_dw, f3_pw, f3_pwb)
            t = jnp.transpose(h.reshape(h.shape[0], D, -1), (0, 2, 1))
            mu = jnp.mean(t, -1, keepdims=True)
            var = jnp.mean((t - mu) ** 2, -1, keepdims=True)
            t = (t - mu) / jnp.sqrt(var + 1e-05) * ln_g + ln_b
            cls_tok = jnp.broadcast_to(cls, (t.shape[0], 1, D))
            return jnp.concatenate([cls_tok, t], axis=1)
        return forward(x, pl_w, pl_b, pl_dw, pl_pw, pl_pwb, pg_w1, pg_b1, pg_dw, pg_pw, pg_pwb, pg_w2, pg_b2, alpha, f1_dw, f1_pw, f1_pwb, f2_dw, f2_pw, f2_pwb, f3_dw, f3_pw, f3_pwb, ln_g, ln_b, cls)

    def _L0_attn_ref(x, w_qkv, b_qkv, scale, w_proj, b_proj):
        import jax, jax.numpy as jnp
        import numpy as np
        B, N, C = (32, 577, 192)
        H = 12
        D = C // H
        b, n, c = x.shape
        h = scale.shape[0]
        d = c // h
        qkv = (x @ w_qkv + b_qkv).reshape(b, n, 3, h, d)
        q = qkv[:, :, 0]
        k = qkv[:, :, 1]
        v = qkv[:, :, 2]
        attn = jnp.einsum('bihd,bjhd->bhij', q, k) * scale[None, :, None, None]
        if n > 1:
            mask = jnp.zeros((n, n), dtype=bool).at[1:, 1:].set(jnp.eye(n - 1, dtype=bool))
            attn = jnp.where(mask[None, None], -jnp.inf, attn)
        attn = jax.nn.softmax(attn, axis=-1)
        out = jnp.einsum('bhij,bjhd->bihd', attn, v).reshape(b, n, c)
        return out @ w_proj + b_proj

    def _L0_ffn_ref(src, frac, Wq, bq, Wk, bk, Wv, bv, Wo, bo, gamma, ln1_g, ln1_b, ln2_g, ln2_b, Wg, bg, W1, b1, W2, b2):
        import jax, jax.numpy as jnp
        import numpy as np
        NHEAD = 12
        EPS_Z = 1e-05
        EPS_LN = 1e-05

        def _zscore_last(t, n):
            m = t.mean(axis=-1, keepdims=True)
            var = ((t - m) ** 2).sum(axis=-1, keepdims=True) / (n - 1)
            return (t - m) / (jnp.sqrt(var) + EPS_Z)

        def _layernorm(x, g, b):
            m = x.mean(axis=-1, keepdims=True)
            v = ((x - m) ** 2).mean(axis=-1, keepdims=True)
            return (x - m) * jax.lax.rsqrt(v + EPS_LN) * g + b
        B, T, D = src.shape
        H = NHEAD
        hd = D // H
        scale = hd ** (-0.5)
        Q = (src @ Wq.T + bq).reshape(B, T, H, hd)
        K = (src @ Wk.T + bk).reshape(B, T, H, hd)
        V = (src @ Wv.T + bv).reshape(B, T, H, hd)
        logits = jnp.einsum('bqhd,bkhd->bhqk', Q, K) * scale
        logits = gamma * _zscore_last(logits, T)
        probs = jax.nn.softmax(logits, axis=-1)
        attn = jnp.einsum('bhqk,bkhd->bqhd', probs, V).reshape(B, T, D)
        attn = attn @ Wo.T + bo
        x = _layernorm(src + attn, ln1_g, ln1_b)
        E = Wg.shape[0]
        gate_scores = jax.nn.softmax(x @ Wg.T + bg, axis=-1)
        top2_val, top2_idx = jax.lax.top_k(gate_scores, 2)
        combine = (jax.nn.one_hot(top2_idx, E, dtype=x.dtype) * top2_val[..., None]).sum(axis=-2)
        h = jax.nn.relu(jnp.einsum('btd,edf->ebtf', x, W1) + b1[:, None, None, :])
        y = jnp.einsum('ebtf,efd->ebtd', h, W2) + b2[:, None, None, :]
        ff = jnp.einsum('ebtd,bte->btd', y, combine)
        return _layernorm(x + ff, ln2_g, ln2_b)
    h = _L0_tok_ref(x, L0_tok_pl_w, L0_tok_pl_b, L0_tok_pl_dw, L0_tok_pl_pw, L0_tok_pl_pwb, L0_tok_pg_w1, L0_tok_pg_b1, L0_tok_pg_dw, L0_tok_pg_pw, L0_tok_pg_pwb, L0_tok_pg_w2, L0_tok_pg_b2, L0_tok_alpha, L0_tok_f1_dw, L0_tok_f1_pw, L0_tok_f1_pwb, L0_tok_f2_dw, L0_tok_f2_pw, L0_tok_f2_pwb, L0_tok_f3_dw, L0_tok_f3_pw, L0_tok_f3_pwb, L0_tok_ln_g, L0_tok_ln_b, L0_tok_cls)
    h = jnp.concatenate([h, txt], axis=1)
    h = h + _L0_attn_ref(_layernorm(h, axis=-1), L0_attn_w_qkv, L0_attn_b_qkv, L0_attn_scale, L0_attn_w_proj, L0_attn_b_proj)
    h = h + _L0_ffn_ref(_layernorm(h, axis=-1), L0_ffn_frac, L0_ffn_Wq, L0_ffn_bq, L0_ffn_Wk, L0_ffn_bk, L0_ffn_Wv, L0_ffn_bv, L0_ffn_Wo, L0_ffn_bo, L0_ffn_gamma, L0_ffn_ln1_g, L0_ffn_ln1_b, L0_ffn_ln2_g, L0_ffn_ln2_b, L0_ffn_Wg, L0_ffn_bg, L0_ffn_W1, L0_ffn_b1, L0_ffn_W2, L0_ffn_b2)
    return h

_drawn_inputs = setup_inputs


def setup_inputs(seed=0):
    import zlib

    import numpy as np

    out = dict(_drawn_inputs(seed))
    spreads = {'L0_tok_alpha': (0.0, 0.8),
     'L0_tok_ln_g': (1.0, 0.2),
     'L0_tok_ln_b': (0.0, 0.1),
     'L0_attn_b_qkv': (0.0, 0.1),
     'L0_attn_scale': (0.25, 0.538),
     'L0_attn_b_proj': (0.0, 0.1),
     'L0_ffn_bq': (0.0, 2.0),
     'L0_ffn_bk': (0.0, 2.0),
     'L0_ffn_bv': (0.0, 0.581),
     'L0_ffn_bo': (0.0, 0.1),
     'L0_ffn_ln1_g': (1.0, 0.2),
     'L0_ffn_ln1_b': (0.0, 0.1),
     'L0_ffn_ln2_g': (1.0, 0.2),
     'L0_ffn_ln2_b': (0.0, 0.1),
     'L0_ffn_bg': (0.0, 0.8),
     'L0_ffn_b1': (0.0, 0.8),
     'L0_ffn_b2': (0.0, 0.42)}
    factors = {'x': 8.0,
     'L0_tok_pl_w': 8.0,
     'L0_tok_pl_b': 189.151,
     'L0_tok_pl_dw': 8.0,
     'L0_tok_pl_pw': 8.0,
     'L0_tok_pl_pwb': 50.776,
     'L0_tok_pg_w1': 8.0,
     'L0_tok_pg_b1': 200.0,
     'L0_tok_pg_dw': 8.0,
     'L0_tok_pg_pw': 8.0,
     'L0_tok_pg_pwb': 200.0,
     'L0_tok_pg_w2': 8.0,
     'L0_tok_pg_b2': 200.0,
     'L0_tok_f1_dw': 8.0,
     'L0_tok_f1_pw': 8.0,
     'L0_tok_f1_pwb': 200.0,
     'L0_tok_f2_dw': 8.0,
     'L0_tok_f2_pw': 8.0,
     'L0_tok_f2_pwb': 178.797,
     'L0_tok_f3_dw': 4.296,
     'L0_tok_f3_pw': 5.201,
     'L0_ffn_Wq': 8.0,
     'L0_ffn_Wk': 8.0,
     'L0_ffn_Wv': 3.834,
     'L0_ffn_Wo': 2.829,
     'L0_ffn_W1': 2.884,
     'L0_tok_f3_pwb': 33.029}
    for name, (base, spread) in spreads.items():
        noise = np.random.default_rng([zlib.crc32(name.encode()), seed]).standard_normal(out[name].shape)
        drawn = base * np.exp(spread * noise) if base else spread * noise
        out[name] = jnp.asarray(drawn.astype(out[name].dtype))
    for name, factor in factors.items():
        out[name] = (out[name] * factor).astype(out[name].dtype)
    return out
```

```python
from contextlib import ExitStack

import numpy as np
import concourse.bass as bass
from concourse import mybir

F32 = mybir.dt.float32
BF16 = mybir.dt.bfloat16
ALU = mybir.AluOpType
ACT = mybir.ActivationFunctionType
AX = mybir.AxisListType

B, D, HEADS, HD = 16, 192, 12, 16
HC = D // 2
HH = HEADS // 2
IMG, PATCH, CIN = 112, 16, 3
G7 = IMG // PATCH
NI = G7 * G7
NTXT = 128
NB = NI + 1
T = NTXT + NB
T2 = 2 * T
TP = NTXT + 64
PAIRS = B // 2
KC = CIN * PATCH * PATCH // 128
NPOS = B * NI
NH = NPOS // 2
PITCH = G7 + 1
CELLS = B * PITCH * PITCH
GUARD = 16
E, FF = 4, 768
FT = FF // 128
UNITS = E * FT
TERMS = 6
SROWS = TERMS * HD
XW = 3 * 128
XN = 2 * NTXT + 64 + NB
BIG = -1.0e30
EPS = 1e-5
NCONV = 5

(C_PLB, C_PGB, C_PLP, C_PGP, C_PGB2, C_ALPHA, C_F1, C_F2, C_BQ, C_BK, C_SCALE, C_FBQ, C_GAMMA) = range(0, 26, 2)
C_DW = 26
NCH = C_DW + NCONV * 2 * 9
(R_F3B, R_TG, R_TB, R_BV, R_BP, R_FBV, R_BO, R_L1G, R_L1B, R_L2G, R_L2B, R_B2) = range(12)
NROW = R_B2 + E
Q_PART = (0, 0, 0, 1, 1, 2)
K_PART = (0, 1, 2, 0, 1, 0)

CHAIN_STEPS = {"dve_attn": 73, "act_attn": 6, "dve_moe": 12, "pool_moe": 6}
FILL = {
    (0, "norm"): 1, (0, "qkv"): 2, (0, "stack"): 2, (0, "max"): 1, (0, "rows"): 1, (0, "exp"): 1, (0, "out"): 1, (0, "turn"): 1,
    (1, "norm"): 1, (1, "qkv"): 2, (1, "stats"): 1, (1, "stack"): 2, (1, "max"): 1, (1, "rows"): 1, (1, "exp"): 1, (1, "out"): 1,
    (1, "turn"): 1,
}


class Chain:

    def __init__(self, eng, sem, per_round, this_round):
        self.eng, self.sem, self.per, self.base, self.n = eng, sem, per_round, this_round * per_round, 0

    def link(self, ins):
        self.n += 1
        ins.then_inc(self.sem, 1)
        self.eng.wait_ge(self.sem, self.base + self.n)

    def end(self):
        assert self.n == self.per, (self.sem, self.n, self.per)


def build(nc, a):
    ctx = ExitStack()
    with ctx:
        def sb(name, shape, dt=F32):
            return ctx.enter_context(nc.sbuf_tensor(name, shape, dt))

        sems = {}

        def sem(name):
            sems[name] = ctx.enter_context(nc.semaphore(name))
            return sems[name]

        def newton(ch, sc):
            ch.link(nc.vector.tensor_tensor(sc[:, 3, :], sc[:, 2, :], sc[:, 2, :], ALU.mult))
            ch.link(nc.vector.tensor_tensor(sc[:, 3, :], sc[:, 3, :], sc[:, 0, :], ALU.mult))
            ch.link(nc.vector.tensor_scalar(sc[:, 3, :], sc[:, 3, :], -0.5, 1.5, ALU.mult, ALU.add))
            ch.link(nc.vector.tensor_tensor(sc[:, 3, :], sc[:, 3, :], sc[:, 2, :], ALU.mult))

        ident = sb("ident", [128, 128])
        ident_bf = sb("ident_bf", [128, 128], BF16)
        masks_f = sb("masks_f", [128, 2, T2])
        masks = sb("masks", [128, 2, T2], BF16)
        same_head = sb("same_head", [HC, HC])
        lower = sb("lower", [128, E * E])
        chan = sb("chan", [HC, NCH])
        rows = sb("rows", [128, NROW, D])
        bg = sb("bg", [128, E])
        gate_w = sb("gate_w", [HC, 2, E])
        b1 = sb("b1", [128, UNITS])
        w_at = sb("w_at", [HC, 8, 2, D])
        w1 = sb("w1", [HC, 2, E * FF])
        w2 = sb("w2", [128, UNITS, D])
        gate = sb("gate", [HC, 2])
        qbias = sb("qbias", [HC, 2])
        img_tok = sb("img_tok", [128, PAIRS, D])

        PS = ctx.enter_context(nc.psum_tensor("PS", [128, 8, 512], F32))
        scr_q = nc.dram_tensor("scr_q", (3, 2, HD, HH * 2 * TP), BF16).ap()
        scr_k = nc.dram_tensor("scr_k", (3, 2, HD, HH * 2 * TP), BF16).ap()

        ld_haar, ld_cw, ld_const, ld_tok, ld_attn, ld_moe = (
            sem(n) for n in ("ld_haar", "ld_cw", "ld_const", "ld_tok", "ld_attn", "ld_moe"))
        ld_x = [sem(f"ld_x{k}") for k in range(KC)]
        casts = sem("casts")

        with ExitStack() as tk:
            def tsb(name, shape, dt=F32):
                return tk.enter_context(nc.sbuf_tensor(name, shape, dt))

            def tsem(name):
                return ctx.enter_context(nc.semaphore(name))

            cols = tsb("cols", [128, KC, NPOS])
            cw = tsb("cw", [128, KC, 2 * D])
            bands = tsb("bands", [128, KC, D])
            haar = tsb("haar", [128, 2, 256])
            w_pw = tsb("w_pw", [HC, NCONV + 1, 2, D])
            diag = tsb("diag", [HC, NCONV * 9, HC])
            pad_l = tsb("pad_l", [HC, 2, CELLS + 2 * GUARD])
            pad_g = tsb("pad_g", [HC, 2, CELLS + 2 * GUARD])
            dwo = tsb("dwo", [HC, 2, CELLS])
            flat = tsb("flat", [HC, 2, NPOS + 16])
            loc = tsb("loc", [HC, 2, NPOS])
            mid = tsb("mid", [HC, 2, NPOS])
            tstat = tsb("tstat", [128, PAIRS, 6])
            tmv = tsb("tmv", [128, PAIRS, 2])
            tsc = tsb("tsc", [128, 4, PAIRS])

            haar_psum, haar_ready, conv_psum, zeroed, diag_ready = (
                tsem(n) for n in ("haar_psum", "haar_ready", "conv_psum", "zeroed", "diag_ready"))
            pad_ready = [tsem(f"pad_ready{r}") for r in range(NCONV)]
            dw_vec = [tsem(f"dw_vec{r}") for r in range(NCONV)]
            dw_psum = [tsem(f"dw_psum{r}") for r in range(NCONV)]
            dw_pe = [tsem(f"dw_pe{r}") for r in range(NCONV)]
            pw_psum = [tsem(f"pw_psum{r}") for r in range(NCONV)]
            loc_ready, gg_ready, glob_psum, gate_ready, f2_relu, tok_var, tok_r0, tok_ready, cls_done, tdve, tact = (
                tsem(n) for n in ("loc_ready", "gg_ready", "glob_psum", "gate_ready", "f2_relu", "tok_var", "tok_r0",
                                  "tok_ready", "cls_done", "tdve", "tact"))

            def cells(t, lo, n):
                v = t[:, lo:lo + n * PITCH * PITCH].rearrange("p (b y x) -> p b y x", y=PITCH, x=PITCH)
                return v[:, :, 0:G7, 0:G7]

            def inner(pad, h, n):
                return cells(pad[:, h, :], GUARD + n * CELLS // 2, B // 2)

            def tap_offset(tap):
                return GUARD + (tap // 3 - 1) * PITCH + tap % 3 - 1

            def image_rows(t, lo):
                return t[:, lo:lo + CELLS].rearrange("p (r x) -> p r x", x=PITCH)[:, :, 0:G7]

            def grid(flat, n):
                return flat[:, NH * n:NH * n + NH].rearrange("p (b y x) -> p b y x", y=G7, x=G7)

            def col(c, h=0):
                return chan[:, c + h:c + h + 1]

            PAD_OF = [pad_l, pad_g, pad_l, pad_g, pad_l]

            with nc.Block() as block:
                @block.sync
                def _(sp):
                    sp.dma_start(haar[:], a["haar"]).then_inc(ld_haar, 16)
                    sp.dma_start(bands[:], a["pg_bands"]).then_inc(ld_haar, 16)
                    for k in range(KC):
                        sp.dma_start(cols[:, k, :], a["x_cols"][:, k, :]).then_inc(ld_x[k], 16)
                    sp.dma_start(w_at[:], a["w_at"]).then_inc(ld_attn, 16)
                    sp.dma_start(w1[:], a["w1"]).then_inc(ld_moe, 16)
                    sp.dma_start(w2[:], a["w2"]).then_inc(ld_moe, 16)
                    sp.wait_ge(tok_ready, 1)
                    for b in range(2):
                        sp.dma_start(img_tok[64 * b + NI:64 * b + NB, :, :], a["cls8"]).then_inc(cls_done, 16)
                    sp.wait_ge(cls_done, 32)

                @block.scalar
                def _(act):
                    act.dma_start(cw[:, :, 0:D], a["pl_cols"]).then_inc(ld_cw, 16)
                    act.dma_start(chan[:], a["chan"]).then_inc(ld_const, 16)
                    act.dma_start(ident[:], a["ident"]).then_inc(ld_const, 16)
                    act.dma_start(w_pw[:], a["w_pw"]).then_inc(ld_tok, 16)
                    act.dma_start(rows[:], a["rows"]).then_inc(ld_tok, 16)
                    act.dma_start(masks_f[:], a["masks"]).then_inc(ld_tok, 16)
                    act.dma_start(same_head[:], a["same_head"]).then_inc(ld_tok, 16)
                    act.dma_start(lower[:], a["lower"]).then_inc(ld_tok, 16)
                    act.dma_start(bg[:], a["bg"]).then_inc(ld_tok, 16)
                    act.dma_start(gate_w[:], a["gate_w"]).then_inc(ld_tok, 16)
                    act.dma_start(b1[:], a["b1"]).then_inc(ld_tok, 16)
                    act.wait_ge(ld_const, 32)
                    nc.scalar.activation(gate[:], chan[:, C_ALPHA:C_ALPHA + 2], ACT.Tanh).then_inc(gate_ready, 1)
                    act.wait_ge(haar_psum, 1)
                    nc.scalar.copy(cw[:, 0:KC, D:2 * D].rearrange("p (g k) d -> p g k d", k=2),
                                   PS[:, 0:3, 0:2 * D].rearrange("p g (k d) -> p g k d", k=2)).then_inc(haar_ready, 1)
                    act.wait_ge(conv_psum, 1)
                    act.wait_ge(zeroed, 1)
                    for m in range(4):
                        pad, bias = (pad_l, C_PLB) if m < 2 else (pad_g, C_PGB)
                        for n in range(2):
                            ins = nc.scalar.activation(inner(pad, m % 2, n), grid(PS[0:HC, 2 * m + n, :], 0), ACT.Gelu,
                                                       bias=col(bias, m % 2))
                        if m % 2:
                            ins.then_inc(pad_ready[m // 2], 1)

                    def evac_dw(r):
                        act.wait_ge(dw_psum[r], 1)
                        if r == NCONV - 1:
                            nc.scalar.copy(flat[:, 1, 0:NPOS].rearrange("p (n c) -> p n c", n=2), PS[0:HC, 0:2, 0:NH])
                            act.wait_ge(dw_vec[r], 1)
                            nc.scalar.copy(flat[:, 0, 0:NPOS].rearrange("p (b y x) -> p b y x", y=G7, x=G7),
                                           cells(dwo[:, 0, :], 0, B)).then_inc(dw_pe[r], 1)
                            return
                        for n in range(2):
                            ins = nc.scalar.copy(cells(dwo[:, 1, :], n * CELLS // 2, B // 2), grid(PS[0:HC, n, :], 0))
                        ins.then_inc(dw_pe[r], 1)

                    def evac_pw(r, out, func, bias, done):
                        act.wait_ge(pw_psum[r], 1)
                        for h in range(2):
                            for n in range(2):
                                ins = nc.scalar.activation(out(h, n), grid(PS[0:HC, 2 + 2 * h + n, :], 0), func,
                                                           bias=col(bias, h))
                        ins.then_inc(done, 1)

                    evac_dw(0)
                    evac_pw(0, lambda h, n: grid(loc[:, h, :], n), ACT.Identity, C_PLP, loc_ready)
                    evac_dw(1)
                    evac_pw(1, lambda h, n: grid(mid[:, h, :], n), ACT.Gelu, C_PGP, gg_ready)
                    evac_dw(2)
                    evac_pw(2, lambda h, n: inner(pad_g, h, n), ACT.Relu, C_F1, pad_ready[3])
                    evac_dw(3)
                    evac_pw(3, lambda h, n: grid(mid[:, h, :], n), ACT.Relu, C_F2, f2_relu)
                    evac_dw(4)
                    act.wait_ge(tok_var, 1)
                    nc.scalar.activation(tsc[:, 1, :], tsc[:, 0, :], ACT.Ln).then_inc(tact, 1)
                    act.wait_ge(tact, 1)
                    nc.scalar.activation(tsc[:, 2, :], tsc[:, 1, :], ACT.Exp, scale=-0.5).then_inc(tok_r0, 1)

                @block.gpsimd
                def _(pool):
                    nc.gpsimd.memset(pad_l[:], 0.0)
                    nc.gpsimd.memset(pad_g[:], 0.0)
                    nc.gpsimd.memset(flat[:, :, NPOS:NPOS + 16], 0.0).then_inc(zeroed, 1)
                    pool.wait_ge(ld_const, 32)
                    for r in range(NCONV):
                        for t in range(9):
                            ins = nc.gpsimd.tensor_scalar(diag[:, 9 * r + t, :], ident[0:HC, 0:HC],
                                                          col(C_DW + 18 * r + 9 + t), None, ALU.mult)
                        ins.then_inc(diag_ready, 1)

                @block.vector
                def _(dve):
                    ch = Chain(dve, tdve, 0, 0)
                    dve.wait_ge(ld_tok, 8 * 16)
                    nc.vector.tensor_copy(masks[:], masks_f[:])
                    dve.wait_ge(ld_const, 32)
                    nc.vector.tensor_copy(ident_bf[:], ident[:]).then_inc(casts, 1)
                    dve.wait_ge(gate_ready, 1)
                    ch.link(nc.vector.tensor_scalar(gate[:], gate[:], 1.0, 0.5, ALU.add, ALU.mult))
                    ch.link(nc.vector.tensor_tensor(qbias[:], chan[:, C_BQ:C_BQ + 2], chan[:, C_SCALE:C_SCALE + 2], ALU.mult))

                    def depthwise(r):
                        dve.wait_ge(pad_ready[r], 1)
                        if r:
                            dve.wait_ge(pw_psum[r - 1], 1)
                        out = image_rows(dwo[:, 0, :], 0)
                        for t in range(9):
                            w, src = col(C_DW + 18 * r + t), image_rows(PAD_OF[r][:, 0, :], tap_offset(t))
                            if t == 0:
                                ins = nc.vector.tensor_scalar(out, src, w, None, ALU.mult)
                            else:
                                ins = nc.vector.scalar_tensor_tensor(out=out, in0=src, scalar=w, in1=out,
                                                                     op0=ALU.mult, op1=ALU.add)
                            if t < 8:
                                ch.link(ins)
                        ins.then_inc(dw_vec[r], 1)

                    depthwise(0)
                    depthwise(1)
                    dve.wait_ge(loc_ready, 1)
                    dve.wait_ge(glob_psum, 1)
                    for h in range(2):
                        for n in range(2):
                            c = slice(NH * n, NH * n + NH)
                            ins = nc.vector.scalar_tensor_tensor(out=mid[:, h, c], in0=PS[0:HC, 2 + 2 * h + n, 0:NH],
                                                                 scalar=col(C_PGB2, h), in1=loc[:, h, c],
                                                                 op0=ALU.add, op1=ALU.subtract)
                    ch.link(ins)
                    for h in range(2):
                        ins = nc.vector.tensor_scalar(mid[:, h, :], mid[:, h, :], gate[:, h:h + 1], None, ALU.mult)
                    ch.link(ins)
                    for h in range(2):
                        for n in range(2):
                            ins = nc.vector.tensor_tensor(inner(pad_l, h, n), grid(mid[:, h, :], n), grid(loc[:, h, :], n),
                                                          ALU.add)
                    ins.then_inc(pad_ready[2], 1)
                    depthwise(2)
                    depthwise(3)
                    dve.wait_ge(f2_relu, 1)
                    for h in range(2):
                        for n in range(2):
                            ins = nc.vector.tensor_tensor(inner(pad_l, h, n), grid(mid[:, h, :], n), grid(loc[:, h, :], n),
                                                          ALU.add)
                    ins.then_inc(pad_ready[4], 1)
                    depthwise(4)
                    dve.wait_ge(pw_psum[4], 1)
                    ps = PS[:, 0:4, 0:2 * D].rearrange("p g (k d) -> p g k d", k=2)
                    for g in range(4):
                        ins = nc.vector.tensor_tensor(
                            img_tok[:, 2 * g:2 * g + 2, :], ps[:, g], rows[:, R_F3B:R_F3B + 1, :].to_broadcast([128, 2, D]),
                            ALU.add)
                    ch.link(ins)
                    for q in range(PAIRS):
                        ins = nc.vector.bn_stats(tstat[:, q, :], img_tok[:, q, :])
                    ch.link(ins)
                    for q in range(PAIRS):
                        ins = nc.vector.bn_aggr(tmv[:, q, :], tstat[:, q, :])
                    ch.link(ins)
                    nc.vector.tensor_scalar(tsc[:, 0, :], tmv[:, :, 1], EPS, None, ALU.add).then_inc(tok_var, 1)
                    dve.wait_ge(tok_var, 1)
                    dve.wait_ge(tok_r0, 1)
                    newton(ch, tsc)
                    for q in range(PAIRS):
                        ins = nc.vector.tensor_scalar(img_tok[:, q, :], img_tok[:, q, :], tmv[:, q, 0:1], tsc[:, 3, q:q + 1],
                                                      ALU.subtract, ALU.mult)
                    ch.link(ins)
                    ch.link(nc.vector.tensor_tensor(img_tok[:], img_tok[:], rows[:, R_TG:R_TG + 1, :].to_broadcast([128, PAIRS, D]), ALU.mult))
                    nc.vector.tensor_tensor(img_tok[:], img_tok[:], rows[:, R_TB:R_TB + 1, :].to_broadcast([128, PAIRS, D]),
                                            ALU.add).then_inc(tok_ready, 1)

                @block.tensor
                def _(pe):
                    pe.wait_ge(ld_haar, 32)
                    for c in range(CIN):
                        for m in range(2):
                            for k in range(2):
                                ins = nc.tensor.matmul(PS[:, c, D * m:D * m + D], haar[:, k, 128 * m:128 * m + 128],
                                                       bands[:, 2 * c + k, :], start=(k == 0), stop=(k == 1))
                    ins.then_inc(haar_psum, 1)
                    pe.wait_ge(ld_cw, 16)
                    pe.wait_ge(haar_ready, 1)
                    for k in range(KC):
                        pe.wait_ge(ld_x[k], 16)
                        for m in range(4):
                            for n in range(2):
                                ins = nc.tensor.matmul(PS[0:HC, 2 * m + n, 0:NH], cw[:, k, HC * m:HC * m + HC],
                                                       cols[:, k, NH * n:NH * n + NH], start=(k == 0), stop=(k == KC - 1))
                    ins.then_inc(conv_psum, 1)

                    def depthwise(r):
                        pe.wait_ge(pad_ready[r], 1)
                        pe.wait_ge(diag_ready, r + 1)
                        for n in range(2):
                            for t in range(9):
                                ins = nc.tensor.matmul(PS[0:HC, n, 0:NH], diag[:, 9 * r + t, :],
                                                       cells(PAD_OF[r][:, 1, :], tap_offset(t) + n * CELLS // 2, B // 2), start=(t == 0), stop=(t == 8))
                        ins.then_inc(dw_psum[r], 1)

                    def pointwise(w, src, done):
                        for m in range(2):
                            for n in range(2):
                                for k in range(2):
                                    ins = nc.tensor.matmul(PS[0:HC, 2 + 2 * m + n, 0:NH], w_pw[:, w, k, HC * m:HC * m + HC],
                                                           src(k, n), start=(k == 0), stop=(k == 1))
                        ins.then_inc(done, 1)

                    pe.wait_ge(ld_tok, 8 * 16)
                    pe.wait_ge(pad_ready[1], 1)
                    for r in range(NCONV):
                        depthwise(r)
                        pe.wait_ge(dw_vec[r], 1)
                        pe.wait_ge(dw_pe[r], 1)
                        if r == 1:
                            pe.wait_ge(loc_ready, 1)
                        if r < NCONV - 1:
                            pointwise(r, lambda k, n: cells(dwo[:, k, :], n * CELLS // 2, B // 2), pw_psum[r])
                        if r == 1:
                            pe.wait_ge(gg_ready, 1)
                            pointwise(NCONV, lambda k, n: mid[:, k, NH * n:NH * n + NH], glob_psum)
                    for q in range(PAIRS):
                        for b in range(2):
                            at = NI * (2 * q + b)
                            for k in range(2):
                                ins = nc.tensor.matmul(PS[64 * b:64 * b + 64, q // 2, D * (q % 2):D * (q % 2) + D],
                                                       flat[:, k, at:at + 64], w_pw[:, NCONV - 1, k, :],
                                                       start=(k == 0), stop=(k == 1), skip_group_check=True)
                    ins.then_inc(pw_psum[4], 1)

        h0 = sb("h0", [128, 3, D])
        h1 = sb("h1", [128, 3, D])
        xn = sb("xn", [128, 3, D])
        h1m = sb("h1m", [128, 3, D])
        x2 = sb("x2", [128, 3, D])
        x2m = sb("x2m", [128, 3, D])
        acc = sb("acc", [128, 3, D])
        b2c = sb("b2c", [128, 3, D])
        fin = sb("fin", [128, 3, D])
        stat = sb("stat", [128, 2, 3, 6])
        mv = sb("mv", [128, 2, 3, 2])
        lsc = [sb(f"lsc{i}", [128, 4, 3]) for i in range(2)]
        xT = sb("xT", [HC, 2, XW])
        xc = sb("xc", [HC, 2, XW])
        x2T = sb("x2T", [HC, 2, XW])
        x2Tm = sb("x2Tm", [HC, 2, XN])
        xbar = sb("xbar", [HC, 2, 2, 2])
        q32 = sb("q32", [HC, 2, 2, TP])
        k32 = sb("k32", [HC, 2, 2, TP])
        rem = sb("rem", [HC, 2, 2, TP])
        qs = sb("qs", [HC, 3, 2, 2 * TP], BF16)
        ks = sb("ks", [HC, 3, 2, 2 * TP], BF16)
        qst = sb("qst", [128, HEADS, 2 * TP], BF16)
        kst = sb("kst", [128, HEADS, 2 * TP], BF16)
        va = sb("va", [128, 4, HEADS, 32])
        kct = sb("kct", [128, 4, D])
        gsb = sb("gsb", [HC, 4, HC])
        mx = sb("mx", [128, 3, HEADS])
        mneg = sb("mneg", [128, 3, HEADS])
        mpart = sb("mpart", [128, 3, 3, HEADS])
        mbf = sb("mbf", [128, 3, HEADS], BF16)
        mrows = sb("mrows", [3 * HEADS, 2 * TP], BF16)
        probs = sb("probs", [128, HH, 3, T2])
        osb = sb("osb", [128, 3, XW])
        rs = sb("rs", [128, 3, HEADS])
        on = sb("on", [128, 3, D])
        oT = sb("oT", [HC, 2, XW])
        gl = sb("gl", [128, 3, E])
        gs = sb("gs", [128, 3, 2])
        cmp1 = sb("cmp1", [128, 3, E, E])
        cmp2 = sb("cmp2", [128, 3, E, E])
        comb = sb("comb", [128, 3, E])
        combm = sb("combm", [128, 3, E])
        hid = [sb(f"hid{i}", [128, XW]) for i in range(2)]

        names = ("preset txt_in img_in h0_free ln_var ln_r0 xn_ready xT_psum xT_ready xc_ready q_psum q_f32 k_psum k_f32 "
                 "v_psum v_ready kc_psum kc_ready g_psum g_ready u_psum prod_ready ss_psum qf_ready q_split k_split "
                 "q_stored k_stored q_stacked k_stacked s_psum s_used m_split mT_psum m_rows m_stacked e_psum e_done "
                 "pv_psum o_ready oT_psum on_ready oc_psum oc_ready pr_psum res_ready "
                 "x2_ready x2T_psum x2T_ready gate_psum gl_ready ge_ready comb_ready "
                 "m_x m_h1 m_x2 m_comb h_psum h_ready h_used y_psum y_used b2_ready fin_var fin_r0 fin_ready stored "
                 "passed dve_attn act_attn dve_moe pool_moe").split()
        S = {n: sem(n) for n in names}

        def plain_wait(eng):
            eng.sem_inc(S["passed"], 1)

        def at(n, per, k):
            return n * per + k

        def text(t):
            return t[:, :, 0:2 * NTXT].rearrange("p h (b j) -> p h b j", b=2)

        def images(t, n=NB):
            return t[:, :, 2 * NTXT:XW].rearrange("p h (b j) -> p h b j", b=2)[:, :, :, 0:n]

        def tile_cols(t, half, i):
            return t[:, half, 128 * i:128 * i + 128]

        def tile_psum(banks, i):
            return PS[:, banks[0], D * i:D * i + D] if i < 2 else PS[:, banks[1], 0:D]

        def row(r, n):
            return rows[:, r:r + 1, :].to_broadcast([128, n, D])


        class MoePe:

            def __init__(self, pe, m):
                self.pe, self.m, self.u = pe, m, 0

            def start(self):
                self.pe.wait_ge(S["m_x"], at(self.m, 1, 1))

            def second(self, u):
                pe, m = self.pe, self.m
                e, j = divmod(u, FT)
                pe.wait_ge(S["h_ready"], at(m, UNITS, u + 1))
                if j == 0 and e > 0:
                    pe.wait_ge(S["y_used"], at(m, E, e))
                for i in range(3):
                    ins = nc.tensor.matmul(tile_psum((5, 6), i), hid[u % 2][:, 128 * i:128 * i + 128], w2[:, u, :], start=(j == 0 and i != 1),
                                           stop=(j == FT - 1), skip_group_check=True)
                ins.then_inc(S["h_used"], 1)
                if j == FT - 1:
                    self.last = ins

            def units(self, n):
                pe, m = self.pe, self.m
                for u in range(self.u, min(self.u + n, UNITS)):
                    if u >= 2:
                        pe.wait_ge(S["h_ready"], at(m, UNITS, u - 1))
                    for k in range(2):
                        ins = nc.tensor.matmul(PS[:, 3 + u % 2, 0:XN], w1[:, k, 128 * u:128 * u + 128],
                                               x2Tm[:, k, :], start=(k == 0), stop=(k == 1))
                    ins.then_inc(S["h_psum"], 1)
                    if u:
                        self.second(u - 1)
                before, self.u = self.u, min(self.u + n, UNITS)
                if before < self.u == UNITS:
                    self.second(UNITS - 1)

        class MoeAct:

            def __init__(self, act, m):
                self.act, self.m, self.u = act, m, 0

            def start(self):
                pass

            def units(self, n):
                for u in range(self.u, min(self.u + n, UNITS)):
                    self.act.wait_ge(S["h_psum"], at(self.m, UNITS, u + 1))
                    if u >= 2:
                        self.act.wait_ge(S["h_used"], at(self.m, UNITS, u - 1))
                    nc.scalar.activation(hid[u % 2][:, 0:XN], PS[:, 3 + u % 2, 0:XN], ACT.Relu,
                                         bias=b1[:, u:u + 1]).then_inc(S["h_ready"], 1)
                self.u = min(self.u + n, UNITS)

        class MoeDve:

            def __init__(self, dve, m):
                self.dve, self.m, self.u = dve, m, 0
                self.ch = Chain(dve, S["dve_moe"], CHAIN_STEPS["dve_moe"], m)

            def start(self):
                self.dve.wait_ge(S["b2_ready"], at(self.m, 1, 1))

            def expert(self, e):
                dve, m = self.dve, self.m
                dve.wait_ge(S["h_used"], at(m, UNITS, FT * (e + 1)))
                for i in range(3):
                    ins = nc.vector.scalar_tensor_tensor(out=acc[:, i, :], in0=tile_psum((5, 6), i),
                                                         scalar=combm[:, i, e:e + 1], in1=acc[:, i, :],
                                                         op0=ALU.mult, op1=ALU.add)
                ins.then_inc(S["y_used"], 1)
                dve.wait_ge(S["y_used"], at(m, E, e + 1))

            def units(self, n):
                for u in range(self.u, min(self.u + n, UNITS)):
                    if u and u % FT == 0:
                        self.expert(u // FT - 1)
                before, self.u = self.u, min(self.u + n, UNITS)
                if before < self.u == UNITS:
                    self.expert(E - 1)

            def finish(self):
                dve, m, ch = self.dve, self.m, self.ch
                ch.link(nc.vector.tensor_tensor(acc[:], acc[:], x2m[:], ALU.add))
                for i in range(3):
                    ins = nc.vector.bn_stats(stat[:, 1, i, :], acc[:, i, :])
                ch.link(ins)
                plain_wait(dve)
                for i in range(3):
                    ins = nc.vector.bn_aggr(mv[:, 1, i, :], stat[:, 1, i, :])
                ch.link(ins)
                nc.vector.tensor_scalar(lsc[1][:, 0, :], mv[:, 1, :, 1], EPS, None, ALU.add).then_inc(S["fin_var"], 1)
                dve.wait_ge(S["fin_r0"], at(m, 1, 1))
                newton(ch, lsc[1])
                dve.wait_ge(S["stored"], at(m, 80, 1))
                for i in range(3):
                    ins = nc.vector.tensor_scalar(fin[:, i, :], acc[:, i, :], mv[:, 1, i, 0:1], lsc[1][:, 3, i:i + 1],
                                                  ALU.subtract, ALU.mult)
                    ch.link(ins)
                ch.link(nc.vector.tensor_tensor(fin[:], fin[:], row(R_L2G, 3), ALU.mult))
                ch.link(nc.vector.tensor_tensor(fin[:], fin[:], row(R_L2B, 3), ALU.add))
                nc.vector.tensor_tensor(fin[:], fin[:], h1m[:], ALU.add).then_inc(S["fin_ready"], 1)
                ch.end()

        class NoMoe:
            def start(self):
                pass

            def units(self, n):
                pass

            def finish(self):
                pass

        def attn_pe(pe, p, moe):
            for s in range(2):
                n = 2 * p + s
                w = 4 * s
                pe.wait_ge(S["xn_ready"], at(n, 1, 1))
                for h in range(2):
                    for i in range(3):
                        ins = nc.tensor.transpose(PS[0:HC, h, 128 * i:128 * i + 128], xn[:, i, HC * h:HC * h + HC], ident[:])
                ins.then_inc(S["xT_psum"], 1)
                moe.units(FILL[s, "norm"])
                pe.wait_ge(S["xT_ready"], at(n, 1, 1))
                for m in range(2):
                    for k in range(2):
                        ins = nc.tensor.matmul(PS[0:HC, m, 0:XN], w_at[:, w, k, HC * m:HC * m + HC], xT[:, k, 0:XN],
                                               start=(k == 0), stop=(k == 1))
                ins.then_inc(S["q_psum"], 1)
                kx = xc if s else xT
                if s:
                    pe.wait_ge(S["xc_ready"], at(p, 1, 1))
                for m in range(2):
                    for k in range(2):
                        ins = nc.tensor.matmul(PS[0:HC, (2, 7)[m], 0:XN], w_at[:, w + 1, k, HC * m:HC * m + HC],
                                               kx[:, k, 0:XN], start=(k == 0), stop=(k == 1))
                ins.then_inc(S["k_psum"], 1)
                moe.units(FILL[s, "qkv"])
                pe.wait_ge(S["q_f32"], at(n, 1, 1))
                for i in range(3):
                    for k in range(2):
                        ins = nc.tensor.matmul(tile_psum((0, 1), i), tile_cols(xT, k, i), w_at[:, w + 2, k, :],
                                               start=(k == 0), stop=(k == 1))
                ins.then_inc(S["v_psum"], 1)
                if s:
                    pe.wait_ge(S["k_f32"], at(n, 1, 1))
                    for i in range(3):
                        for k in range(2):
                            ins = nc.tensor.matmul(tile_psum((2, 7), i), tile_cols(xc, k, i), w_at[:, w + 1, k, :],
                                                   start=(k == 0), stop=(k == 1))
                    ins.then_inc(S["kc_psum"], 1)
                    moe.units(FILL[s, "stats"])
                    pe.wait_ge(S["kc_ready"], at(p, 1, 1))
                    pe.wait_ge(S["v_ready"], at(n, 1, 1))
                    for b in range(2):
                        for h in range(2):
                            for i in range(2):
                                x = kct[:, 2 * i + b, HC * h:HC * h + HC]
                                c = HC * (2 * h + b)
                                ins = nc.tensor.matmul(PS[0:HC, 0, c:c + HC], x, x, start=(i == 0), stop=(i == 1))
                    ins.then_inc(S["g_psum"], 1)
                    pe.wait_ge(S["g_ready"], at(p, 1, 1))
                    for h in range(2):
                        for b in range(2):
                            ins = nc.tensor.matmul(PS[0:HC, 1 + h, T * b:T * b + T], gsb[:, 2 * h + b, :],
                                                   q32[:, h, b, 0:T], start=True, stop=True)
                    ins.then_inc(S["u_psum"], 1)
                    pe.wait_ge(S["prod_ready"], at(p, 1, 1))
                    for h in range(2):
                        ins = nc.tensor.matmul(PS[0:HC, (0, 7)[h], 0:T2], same_head[:], rem[:, h, :, 0:T],
                                               start=True, stop=True)
                    ins.then_inc(S["ss_psum"], 1)
                    pe.wait_ge(S["qf_ready"], at(p, 1, 1))
                moe.units(FILL[s, "stack"])
                pe.wait_ge(S["v_ready"], at(n, 1, 1))
                pe.wait_ge(S["k_f32"], at(n, 1, 1))
                pe.wait_ge(S["q_stacked"], at(n, 16 * TERMS, 16 * TERMS))
                pe.wait_ge(S["k_stacked"], at(n, 16 * TERMS, 16 * TERMS))

                def logits(u, rows_, still, move):
                    if s == 0:
                        for bank in range(3):
                            nc.tensor.matmul(PS[:, bank, 0:T2], ident_bf[:], masks[:, bank // 2, :], start=True, stop=False,
                                             skip_group_check=True)
                    for g in range(2):
                        h = 2 * u + g
                        for b in range(2):
                            nc.tensor.matmul(PS[:, g, T * b:T * b + T], still[0:rows_, h, TP * b:TP * b + NTXT],
                                             move[0:rows_, h, TP * b:TP * b + T], start=(s == 1), stop=True,
                                             skip_group_check=True)
                    for g in range(2):
                        h = 2 * u + g
                        for b in range(2):
                            ins = nc.tensor.matmul(PS[64 * b:64 * b + 64, 2, T * g:T * g + T],
                                                   still[0:rows_, h, TP * b + NTXT:TP * b + TP],
                                                   move[0:rows_, h, TP * b:TP * b + T], start=(s == 1), stop=True,
                                                   skip_group_check=True)
                    return ins

                for u in range(HH):
                    if u:
                        pe.wait_ge(S["s_used"], at(n, HH, u))
                    logits(u, SROWS, qst, kst).then_inc(S["s_psum"], 1)
                    moe.units(FILL[s, "max"])
                pe.wait_ge(S["m_split"], at(n, 1, 1))
                plain_wait(pe)
                for i in range(3):
                    src = mpart[:, i, :, :].rearrange("p c h -> p (c h)")
                    if i < 2:
                        nc.tensor.transpose(PS[0:3 * HEADS, 7, TP * i:TP * i + NTXT], src, ident[:])
                    else:
                        ins = nc.tensor.transpose(PS[0:3 * HEADS, 7, 384:512], src, ident[:])
                ins.then_inc(S["mT_psum"], 1)
                moe.units(FILL[s, "rows"])
                pe.wait_ge(S["s_used"], at(n, HH, HH))
                pe.wait_ge(S["m_stacked"], at(n, 48, 48))
                for u in range(HH):
                    if u:
                        pe.wait_ge(S["e_done"], at(n, HH, u))
                    logits(u, SROWS + 3, kst, qst).then_inc(S["e_psum"], 1)
                    moe.units(FILL[s, "exp"])
                pe.wait_ge(S["e_done"], at(n, HH, HH))
                for g in range(3):
                    for b in range(2):
                        for i in range(2):
                            for q in range(4):
                                h = 4 * g + q
                                mv_ = probs[:, h // 2, h % 2, T * b:T * b + T] if i == 0 else \
                                    probs[:, h // 2, 2, T * (h % 2):T * (h % 2) + T]
                                ins = nc.tensor.matmul(PS[32 * q:32 * q + 32, g, T * b:T * b + T], va[:, 2 * i + b, h, :],
                                                       mv_, start=(i == 0), stop=(i == 1), skip_group_check=True)
                ins.then_inc(S["pv_psum"], 1)
                moe.units(FILL[s, "out"])
                pe.wait_ge(S["o_ready"], at(n, 1, 1))
                for i in range(3):
                    for g in range(3):
                        ins = nc.tensor.transpose(PS[:, i, 128 * g:128 * g + 128], osb[:, g, 128 * i:128 * i + 128],
                                                  ident[:])
                ins.then_inc(S["oT_psum"], 1)
                moe.units(FILL[s, "turn"])
                pe.wait_ge(S["on_ready"], at(n, 1, 1))
                for h in range(2):
                    for i in range(3):
                        ins = nc.tensor.transpose(PS[0:HC, h, 128 * i:128 * i + 128], on[:, i, HC * h:HC * h + HC], ident[:])
                ins.then_inc(S["oc_psum"], 1)
                pe.wait_ge(S["oc_ready"], at(n, 1, 1))
                for i in range(3):
                    for k in range(2):
                        ins = nc.tensor.matmul(tile_psum((2, 7), i), tile_cols(oT, k, i), w_at[:, w + 3, k, :],
                                               start=(k == 0), stop=(k == 1))
                ins.then_inc(S["pr_psum"], 1)
            pe.wait_ge(S["x2_ready"], at(p, 1, 1))
            for h in range(2):
                for i in range(3):
                    ins = nc.tensor.transpose(PS[0:HC, h, 128 * i:128 * i + 128], x2[:, i, HC * h:HC * h + HC], ident[:])
            ins.then_inc(S["x2T_psum"], 1)
            pe.wait_ge(S["x2T_ready"], at(p, 1, 1))
            for i in range(3):
                for k in range(2):
                    ins = nc.tensor.matmul(PS[:, 2, E * i:E * i + E], tile_cols(x2T, k, i), gate_w[:, k, :],
                                           start=(k == 0), stop=(k == 1))
            ins.then_inc(S["gate_psum"], 1)

        def by_token(bank, half=slice(0, HC)):
            return (PS[half, bank, 0:2 * NTXT].rearrange("p (b j) -> p b j", b=2),
                    PS[half, bank, 2 * NTXT:XW].rearrange("p (b j) -> p b j", b=2)[:, :, 0:NB])

        def attn_act(act, p, moe):
            ch = Chain(act, S["act_attn"], CHAIN_STEPS["act_attn"], p)
            for s in range(2):
                n = 2 * p + s
                act.wait_ge(S["ln_var"], at(n, 1, 1))
                ch.link(nc.scalar.activation(lsc[0][:, 1, :], lsc[0][:, 0, :], ACT.Ln))
                nc.scalar.activation(lsc[0][:, 2, :], lsc[0][:, 1, :], ACT.Exp, scale=-0.5).then_inc(S["ln_r0"], 1)
                act.wait_ge(S["xT_psum"], at(n, 1, 1))
                nc.scalar.copy(xT[:], PS[0:HC, 0:2, 0:XW]).then_inc(S["xT_ready"], 1)
                moe.units(FILL[s, "norm"])
                act.wait_ge(S["q_psum"], at(n, 1, 1))
                for h in range(2):
                    for src, c in zip(by_token(h), (slice(0, NTXT), slice(NTXT, T))):
                        if s == 0:
                            ins = nc.scalar.activation(q32[:, h, :, c], src, ACT.Identity, bias=qbias[:, h:h + 1],
                                                       scale=chan[:, C_SCALE + h:C_SCALE + h + 1])
                        else:
                            ins = nc.scalar.activation(q32[:, h, :, c], src, ACT.Identity,
                                                       bias=chan[:, C_FBQ + h:C_FBQ + h + 1])
                ins.then_inc(S["q_f32"], 1)
                act.wait_ge(S["k_psum"], at(n, 1, 1))
                for h in range(2):
                    for src, c in zip(by_token((2, 7)[h]), (slice(0, NTXT), slice(NTXT, T))):
                        if s == 0:
                            ins = nc.scalar.activation(k32[:, h, :, c], src, ACT.Identity,
                                                       bias=chan[:, C_BK + h:C_BK + h + 1])
                        else:
                            ins = nc.scalar.copy(k32[:, h, :, c], src)
                ins.then_inc(S["k_f32"], 1)
                moe.units(FILL[s, "qkv"])
                if s:
                    act.wait_ge(S["kc_psum"], at(p, 1, 1))
                    nc.scalar.copy(kct[:, 0:2, :].rearrange("p i d -> p (i d)"), PS[:, 2, 0:2 * D])
                    nc.scalar.copy(kct[0:NB, 2, :], PS[0:NB, 7, 0:D])
                    nc.scalar.copy(kct[64:64 + NB, 3, :], PS[64:64 + NB, 7, 0:D]).then_inc(S["kc_ready"], 1)
                    moe.units(FILL[s, "stats"])
                    act.wait_ge(S["ss_psum"], at(p, 1, 1))
                    for h in range(2):
                        ins = nc.scalar.activation(rem[:, h, :, 0:T], PS[0:HC, (0, 7)[h], 0:T2].rearrange("p (b j) -> p b j", b=2),
                                                   ACT.Ln, bias=1e-18, scale=1.0 / (T - 1))
                    ch.link(ins)
                    ch.link(nc.scalar.activation(rem[:, :, :, 0:T], rem[:, :, :, 0:T], ACT.Exp, scale=0.5))
                    ch.link(nc.scalar.activation(rem[:, :, :, 0:T], rem[:, :, :, 0:T], ACT.Ln, bias=EPS / HD ** -0.5))
                    nc.scalar.activation(rem[:, :, :, 0:T], rem[:, :, :, 0:T], ACT.Exp, scale=-1.0).then_inc(S["qf_ready"], 1)
                moe.units(FILL[s, "stack"])
                for u in range(HH):
                    moe.units(FILL[s, "max"])
                act.wait_ge(S["mT_psum"], at(n, 1, 1))
                v = mrows[:].rearrange("p (b j) -> p b j", b=2)
                nc.scalar.copy(v[:, :, 0:NTXT], PS[0:3 * HEADS, 7, 0:2 * TP].rearrange("p (b j) -> p b j", b=2)[:, :, 0:NTXT])
                nc.scalar.copy(v[:, :, NTXT:TP], PS[0:3 * HEADS, 7, 384:512].rearrange("p (b j) -> p b j", b=2))\
                    .then_inc(S["m_rows"], 1)
                moe.units(FILL[s, "rows"])
                for u in range(HH):
                    act.wait_ge(S["e_psum"], at(n, HH, u + 1))
                    nc.scalar.activation(probs[:, u, :, :], PS[:, 0:3, 0:T2], ACT.Exp).then_inc(S["e_done"], 1)
                    moe.units(FILL[s, "exp"])
                act.wait_ge(S["pv_psum"], at(n, 1, 1))
                o = PS[:, 0:3, 0:T2].rearrange("p g (b j) -> p g b j", b=2)
                nc.scalar.copy(text(osb), o[:, :, :, 0:NTXT])
                nc.scalar.copy(images(osb), o[:, :, :, NTXT:T]).then_inc(S["o_ready"], 1)
                moe.units(FILL[s, "out"])
                moe.units(FILL[s, "turn"])
                act.wait_ge(S["oc_psum"], at(n, 1, 1))
                nc.scalar.copy(oT[:], PS[0:HC, 0:2, 0:XW]).then_inc(S["oc_ready"], 1)
            act.wait_ge(S["x2_var"], at(p, 1, 1))
            ch.link(nc.scalar.activation(lsc[0][:, 1, :], lsc[0][:, 0, :], ACT.Ln))
            nc.scalar.activation(lsc[0][:, 2, :], lsc[0][:, 1, :], ACT.Exp, scale=-0.5).then_inc(S["x2_r0"], 1)
            act.wait_ge(S["x2T_psum"], at(p, 1, 1))
            nc.scalar.copy(x2T[:], PS[0:HC, 0:2, 0:XW]).then_inc(S["x2T_ready"], 1)
            act.wait_ge(S["gl_ready"], at(p, 1, 1))
            nc.scalar.activation(gl[:], gl[:], ACT.Exp).then_inc(S["ge_ready"], 1)
            ch.end()

        def attn_dve(dve, p, moe):
            ch = Chain(dve, S["dve_attn"], CHAIN_STEPS["dve_attn"], p)

            def norm(x, y, var_sem, r0_sem, var_n, done=None, gain=None):
                for i in range(3):
                    ins = nc.vector.bn_stats(stat[:, 0, i, :], x[:, i, :])
                ch.link(ins)
                plain_wait(dve)
                for i in range(3):
                    ins = nc.vector.bn_aggr(mv[:, 0, i, :], stat[:, 0, i, :])
                ch.link(ins)
                nc.vector.tensor_scalar(lsc[0][:, 0, :], mv[:, 0, :, 1], EPS, None, ALU.add).then_inc(S[var_sem], 1)
                dve.wait_ge(S[r0_sem], at(var_n, 1, 1))
                newton(ch, lsc[0])
                for i in range(3):
                    ins = nc.vector.tensor_scalar(y[:, i, :], x[:, i, :], mv[:, 0, i, 0:1], lsc[0][:, 3, i:i + 1],
                                                  ALU.subtract, ALU.mult)
                    if i < 2:
                        ch.link(ins)
                if gain is not None:
                    ch.link(ins)
                    ch.link(nc.vector.tensor_tensor(y[:], y[:], row(gain, 3), ALU.mult))
                    ins = nc.vector.tensor_tensor(y[:], y[:], row(gain + 1, 3), ALU.add)
                ins.then_inc(S[done], 1)

            def split(x, parts, done):
                v = [parts[:, c].rearrange("p h (b j) -> p h b j", b=2)[:, :, :, 0:T] for c in range(3)]
                ch.link(nc.vector.tensor_copy(v[0], x[:, :, :, 0:T]))
                ch.link(nc.vector.tensor_tensor(rem[:, :, :, 0:T], x[:, :, :, 0:T], v[0], ALU.subtract))
                ch.link(nc.vector.tensor_copy(v[1], rem[:, :, :, 0:T]))
                nc.vector.tensor_tensor(v[2], rem[:, :, :, 0:T], v[1], ALU.subtract).then_inc(done, 1)

            for s in range(2):
                n = 2 * p + s
                x_in = h1 if s else h0
                if s == 0:
                    dve.wait_ge(S["txt_in"], at(p, 32, 32))
                    dve.wait_ge(S["img_in"], at(p, 1, 1))
                else:
                    dve.wait_ge(S["res_ready"], at(2 * p, 1, 1))
                norm(x_in, xn, "ln_var", "ln_r0", n, "xn_ready")
                moe.units(FILL[s, "norm"])
                if s:
                    dve.wait_ge(S["xT_ready"], at(n, 1, 1))
                    nc.vector.tensor_reduce(xbar[:, 0], text(xT), AX.X, ALU.add)
                    ch.link(nc.vector.tensor_reduce(xbar[:, 1], images(xT), AX.X, ALU.add))
                    ch.link(nc.vector.tensor_tensor(xbar[:, 0], xbar[:, 0], xbar[:, 1], ALU.add))
                    ch.link(nc.vector.tensor_scalar(xbar[:, 0], xbar[:, 0], 1.0 / T, None, ALU.mult))
                    mean = xbar[:, 0].unsqueeze(3)
                    nc.vector.tensor_tensor(text(xc), text(xT), mean.to_broadcast([HC, 2, 2, NTXT]), ALU.subtract)
                    nc.vector.tensor_tensor(images(xc, 64), images(xT, 64), mean.to_broadcast([HC, 2, 2, 64]),
                                            ALU.subtract).then_inc(S["xc_ready"], 1)
                if s == 0:
                    dve.wait_ge(S["q_f32"], at(n, 1, 1))
                    split(q32, qs, S["q_split"])
                    dve.wait_ge(S["q_split"], at(n, 1, 1))
                dve.wait_ge(S["k_f32"], at(n, 1, 1))
                split(k32, ks, S["k_split"])
                moe.units(FILL[s, "qkv"])
                dve.wait_ge(S["v_psum"], at(n, 1, 1))
                bv = R_FBV if s else R_BV
                nc.vector.tensor_tensor(va[:, 0:2, :, 0:HD], PS[:, 0, 0:2 * D].rearrange("p (i h d) -> p i h d", i=2, d=HD),
                                        rows[:, bv:bv + 1, :].rearrange("p i (h d) -> p i h d", d=HD).to_broadcast([128, 2, HEADS, HD]),
                                        ALU.add)
                for b in range(2):
                    r = slice(64 * b, 64 * b + NB)
                    ins = nc.vector.tensor_tensor(va[r, 2 + b, :, 0:HD], PS[r, 1, 0:D].rearrange("p (h d) -> p h d", d=HD),
                                                  rows[r, bv, :].rearrange("p (h d) -> p h d", d=HD), ALU.add)
                ins.then_inc(S["v_ready"], 1)
                if s:
                    moe.units(FILL[s, "stats"])
                    dve.wait_ge(S["g_psum"], at(p, 1, 1))
                    nc.vector.tensor_tensor(gsb[:], PS[0:HC, 0, 0:4 * HC].rearrange("p (i c) -> p i c", i=4),
                                            same_head[:].unsqueeze(1).to_broadcast([HC, 4, HC]), ALU.mult).then_inc(S["g_ready"], 1)
                    dve.wait_ge(S["u_psum"], at(p, 1, 1))
                    dve.wait_ge(S["k_split"], at(n, 1, 1))
                    nc.vector.tensor_tensor(rem[:, :, :, 0:T], PS[0:HC, 1:3, 0:T2].rearrange("p h (b j) -> p h b j", b=2),
                                            q32[:, :, :, 0:T], ALU.mult).then_inc(S["prod_ready"], 1)
                    dve.wait_ge(S["qf_ready"], at(p, 1, 1))
                    ch.link(nc.vector.scalar_tensor_tensor(out=q32[:, :, :, 0:T], in0=q32[:, :, :, 0:T],
                                                           scalar=chan[:, C_GAMMA:C_GAMMA + 1], in1=rem[:, :, :, 0:T],
                                                           op0=ALU.mult, op1=ALU.mult))
                    split(q32, qs, S["q_split"])
                    dve.wait_ge(S["q_split"], at(n, 1, 1))
                moe.units(FILL[s, "stack"])
                for u in range(HH):
                    dve.wait_ge(S["s_psum"], at(n, HH, u + 1))
                    nc.vector.tensor_reduce(mx[:, 0:2, 2 * u:2 * u + 2].rearrange("p b g -> p g b"),
                                            PS[:, 0:2, 0:T2].rearrange("p g (b j) -> p g b j", b=2), AX.X, ALU.max)
                    nc.vector.tensor_reduce(mx[:, 2, 2 * u:2 * u + 2],
                                            PS[:, 2, 0:T2].rearrange("p (g j) -> p g j", g=2), AX.X, ALU.max)\
                        .then_inc(S["s_used"], 1)
                    moe.units(FILL[s, "max"])
                dve.wait_ge(S["s_used"], at(n, HH, HH))
                ch.link(nc.vector.tensor_scalar(mneg[:], mx[:], -1.0, None, ALU.mult))
                for c in range(3):
                    ch.link(nc.vector.tensor_copy(mbf[:], mneg[:]))
                    ins = nc.vector.tensor_copy(mpart[:, :, c, :], mbf[:])
                    if c < 2:
                        ch.link(ins)
                        ch.link(nc.vector.tensor_tensor(mneg[:], mneg[:], mbf[:], ALU.subtract))
                ins.then_inc(S["m_split"], 1)
                moe.units(FILL[s, "rows"])
                for u in range(HH):
                    moe.units(FILL[s, "exp"])
                moe.units(FILL[s, "out"])
                dve.wait_ge(S["oT_psum"], at(n, 1, 1))
                o = PS[:, 0:3, 0:384].rearrange("p i (h c) -> p i h c", c=32)
                ch.link(nc.vector.reciprocal(rs[:].unsqueeze(3), o[:, :, :, HD:HD + 1]))
                nc.vector.tensor_tensor(on[:].rearrange("p i (h d) -> p i h d", d=HD), o[:, :, :, 0:HD],
                                        rs[:].unsqueeze(3).to_broadcast([128, 3, HEADS, HD]), ALU.mult).then_inc(S["on_ready"], 1)
                moe.units(FILL[s, "turn"])
                dve.wait_ge(S["pr_psum"], at(n, 1, 1))
                out, res, bo = (x2, xn, R_BO) if s else (h1, h0, R_BP)
                for i, (lo, hi) in enumerate(((0, 2), (2, 3))):
                    src = PS[:, (2, 7)[i], 0:(hi - lo) * D].rearrange("p (i d) -> p i d", d=D)
                    ins = nc.vector.tensor_tensor(out[:, lo:hi, :], src, row(bo, hi - lo), ALU.add)
                ch.link(ins)
                nc.vector.tensor_tensor(out[:], out[:], res[:], ALU.add).then_inc(S["res_ready"], 1)
            dve.wait_ge(S["res_ready"], at(2 * p, 1, 2))
            norm(x2, x2, "x2_var", "x2_r0", p, "x2_ready", R_L1G)
            dve.wait_ge(S["gate_psum"], at(p, 1, 1))
            ch.link(nc.vector.tensor_tensor(gl[:], PS[:, 2, 0:3 * E].rearrange("p (i e) -> p i e", e=E),
                                            bg[:].unsqueeze(1).to_broadcast([128, 3, E]), ALU.add))
            ch.link(nc.vector.tensor_reduce(gs[:, :, 0], gl[:], AX.X, ALU.max))
            nc.vector.tensor_tensor(gl[:], gl[:], gs[:, :, 0:1].to_broadcast([128, 3, E]), ALU.subtract).then_inc(S["gl_ready"], 1)
            dve.wait_ge(S["ge_ready"], at(p, 1, 1))
            ch.link(nc.vector.tensor_reduce(gs[:, :, 0], gl[:], AX.X, ALU.add))
            ch.link(nc.vector.reciprocal(gs[:, :, 1], gs[:, :, 0]))
            ch.link(nc.vector.tensor_tensor(gl[:], gl[:], gs[:, :, 1:2].to_broadcast([128, 3, E]), ALU.mult))
            mine, other = gl[:].unsqueeze(3).to_broadcast([128, 3, E, E]), gl[:].unsqueeze(2).to_broadcast([128, 3, E, E])
            ch.link(nc.vector.tensor_tensor(cmp1[:], other, mine, ALU.is_gt))
            ch.link(nc.vector.tensor_tensor(cmp2[:], other, mine, ALU.is_equal))
            ch.link(nc.vector.tensor_tensor(cmp2[:], cmp2[:],
                                            lower[:].rearrange("p (i e) -> p i e", e=E).unsqueeze(1).to_broadcast([128, 3, E, E]),
                                            ALU.mult))
            ch.link(nc.vector.tensor_tensor(cmp1[:], cmp1[:], cmp2[:], ALU.add))
            ch.link(nc.vector.tensor_reduce(comb[:], cmp1[:], AX.X, ALU.add))
            ch.link(nc.vector.tensor_scalar(comb[:], comb[:], 1.5, None, ALU.is_lt))
            nc.vector.tensor_tensor(comb[:], comb[:], gl[:], ALU.mult).then_inc(S["comb_ready"], 1)
            ch.end()

        def hand_over(pool, p):
            pool.wait_ge(S["comb_ready"], at(p, 1, 1))
            pool.wait_ge(S["x2T_ready"], at(p, 1, 1))
            plain_wait(pool)
            nc.gpsimd.tensor_copy(combm[:], comb[:])
            nc.gpsimd.tensor_copy(x2m[:], x2[:])
            nc.gpsimd.tensor_copy(h1m[:], h1[:])
            nc.gpsimd.tensor_copy(x2Tm[:], x2T[:, :, 0:XN]).then_inc(S["m_x"], 1)

        def b2_sum(pool, m):
            pool.wait_ge(S["m_x"], at(m, 1, 1))
            ch = Chain(pool, S["pool_moe"], CHAIN_STEPS["pool_moe"], m)
            for e in range(E):
                b2e = rows[:, R_B2 + e:R_B2 + e + 1, :].to_broadcast([128, 3, D])
                c = combm[:, :, e:e + 1].to_broadcast([128, 3, D])
                ins = nc.gpsimd.tensor_tensor(b2c[:] if e else acc[:], b2e, c, ALU.mult)
                ch.link(ins)
                if e:
                    ins = nc.gpsimd.tensor_tensor(acc[:], acc[:], b2c[:], ALU.add)
                    if e < E - 1:
                        ch.link(ins)
            ins.then_inc(S["b2_ready"], 1)
            ch.end()

        def load_pair(sp, p):
            for b in range(2):
                sp.dma_start(h0[:, b, :], a["txt"][p, b]).then_inc(S["txt_in"], 16)

        def stack_sp(sp, p):
            for s in range(2):
                n = 2 * p + s
                for x, scr, st, part, split_, stored, stacked in (
                        (ks, scr_k, kst, K_PART, "k_split", "k_stored", "k_stacked"),
                        (qs, scr_q, qst, Q_PART, "q_split", "q_stored", "q_stacked")) if s else (
                        (qs, scr_q, qst, Q_PART, "q_split", "q_stored", "q_stacked"),
                        (ks, scr_k, kst, K_PART, "k_split", "k_stored", "k_stacked")):
                    sp.wait_ge(S[split_], at(n, 1, 1))
                    sp.dma_start(scr.rearrange("c h d (g j) -> (d g) c h j", g=HH), x[:]).then_inc(S[stored], 16)
                    sp.wait_ge(S[stored], at(n, 16, 16))
                    for t in range(TERMS):
                        sp.dma_start(st[HD * t:HD * t + HD, :, :].rearrange("d (h g) j -> d h (g j)", h=2),
                                     scr[part[t]].rearrange("h d x -> d h x")).then_inc(S[stacked], 16)
                sp.wait_ge(S["m_rows"], at(n, 1, 1))
                for c in range(3):
                    sp.dma_start(qst[SROWS + c:SROWS + c + 1, :, :], mrows[HEADS * c:HEADS * c + HEADS, :])\
                        .then_inc(S["m_stacked"], 16)

        def store_pair(sp, m):
            sp.wait_ge(S["fin_ready"], at(m, 1, 1))
            out = a["out"][m]
            sp.dma_start(out[:, NB:T, :].rearrange("b t d -> t b d"), fin[:, 0:2, :]).then_inc(S["stored"], 16)
            for b in range(2):
                sp.dma_start(out[b, 1:NB, :], fin[64 * b:64 * b + NI, 2, :]).then_inc(S["stored"], 16)
                sp.dma_start(out[b, 0:1, :], fin[64 * b + NI:64 * b + NB, 2, :]).then_inc(S["stored"], 16)

        def fin_act(act, m, moe):
            act.wait_ge(S["fin_var"], at(m, 1, 1))
            nc.scalar.activation(lsc[1][:, 1, :], lsc[1][:, 0, :], ACT.Ln).then_inc(S["fin_ln"], 1)
            act.wait_ge(S["fin_ln"], at(m, 1, 1))
            nc.scalar.activation(lsc[1][:, 2, :], lsc[1][:, 1, :], ACT.Exp, scale=-0.5).then_inc(S["fin_r0"], 1)

        for n_ in ("x2_var", "x2_r0", "fin_ln"):
            S[n_] = sem(n_)

        with nc.Block() as block:
            @block.sync
            def _(sp):
                sp.wait_ge(S["preset"], 2)
                load_pair(sp, 0)
                stack_sp(sp, 0)

                def next_load(p):
                    sp.wait_ge(S["res_ready"], at(2 * p, 1, -1))
                    load_pair(sp, p)

                with sp.Fori(1, PAIRS) as p:
                    next_load(p)
                    stack_sp(sp, p)
                    store_pair(sp, p - 1)
                store_pair(sp, PAIRS - 1)
                sp.wait_ge(S["stored"], at(PAIRS, 80, 1))

            @block.tensor
            def _(pe):
                pe.wait_ge(ld_attn, 16)
                pe.wait_ge(ld_moe, 32)
                pe.wait_ge(casts, 1)
                pe.wait_ge(S["preset"], 2)
                attn_pe(pe, 0, NoMoe())
                with pe.Fori(1, PAIRS) as p:
                    moe = MoePe(pe, p - 1)
                    moe.start()
                    attn_pe(pe, p, moe)
                    moe.units(UNITS - moe.u)
                moe = MoePe(pe, PAIRS - 1)
                moe.start()
                moe.units(UNITS)

            @block.scalar
            def _(act):
                attn_act(act, 0, NoMoe())
                with act.Fori(1, PAIRS) as p:
                    moe = MoeAct(act, p - 1)
                    attn_act(act, p, moe)
                    moe.units(UNITS - moe.u)
                    fin_act(act, p - 1, moe)
                moe = MoeAct(act, PAIRS - 1)
                moe.units(UNITS)
                fin_act(act, PAIRS - 1, moe)

            @block.vector
            def _(dve):
                nc.vector.memset(qs[:], 0.0)
                nc.vector.memset(ks[:], 0.0)
                nc.vector.memset(va[:], 0.0).then_inc(casts, 1)
                dve.wait_ge(casts, 2)
                nc.vector.memset(va[:, 0:2, :, HD:HD + 1], 1.0)
                for b in range(2):
                    nc.vector.memset(va[64 * b:64 * b + NB, 2 + b, :, HD:HD + 1], 1.0)
                nc.vector.memset(kst[SROWS:128, :, :], 1.0).then_inc(S["stored"], 1)
                nc.vector.memset(qst[SROWS:128, :, :], 0.0).then_inc(S["preset"], 1)
                dve.wait_ge(cls_done, 32)
                attn_dve(dve, 0, NoMoe())
                with dve.Fori(1, PAIRS) as p:
                    moe = MoeDve(dve, p - 1)
                    moe.start()
                    attn_dve(dve, p, moe)
                    moe.units(UNITS - moe.u)
                    moe.finish()
                moe = MoeDve(dve, PAIRS - 1)
                moe.start()
                moe.units(UNITS)
                moe.finish()

            @block.gpsimd
            def _(pool):
                nc.gpsimd.memset(kct[:], 0.0)
                nc.gpsimd.memset(osb[:, :, 2 * NTXT:XW], 1.0)
                nc.gpsimd.memset(hid[0][:, XN:XW], 0.0)
                nc.gpsimd.memset(hid[1][:, XN:XW], 0.0).then_inc(S["preset"], 1)

                def image(p):
                    nc.gpsimd.tensor_copy(h0[:, 2, :], img_tok[:, p, :]).then_inc(S["img_in"], 1)

                pool.wait_ge(cls_done, 32)
                image(0)
                hand_over(pool, 0)
                with pool.Fori(1, PAIRS) as p:
                    image(p)
                    b2_sum(pool, p - 1)
                    pool.wait_ge(S["fin_ready"], at(p, 1, 0))
                    hand_over(pool, p)
                b2_sum(pool, PAIRS - 1)



def _haar():
    isq2 = float(np.float32(0.7071067811865476))
    f = np.arange(256)
    y, x = np.divmod(np.arange(256), 16)
    h = np.full((256, 256), isq2 ** 8)
    for level in range(4):
        digit = (f >> (2 * (3 - level))) & 3
        w_hi, h_hi = digit >> 1, digit & 1
        h = h * np.where((w_hi[:, None] & (x[None] >> level) & 1) == 1, -1.0, 1.0)
        h = h * np.where((h_hi[:, None] & (y[None] >> level) & 1) == 1, -1.0, 1.0)
    return h.astype(np.float32)


def _layout(i):
    f = {k: np.asarray(v) for k, v in i.items()}

    def halves(v):
        return np.reshape(v, (2, HC)).T

    def chunk(m, r=HC):
        return np.reshape(m, (-1, r, m.shape[-1])).transpose(1, 0, 2)

    turn = np.arange(D).reshape(2, HH, HD).transpose(0, 2, 1).reshape(-1)
    o = {}
    o["x_cols"] = chunk(f["x"].reshape(B, CIN, G7, PATCH, G7, PATCH).transpose(1, 3, 5, 0, 2, 4).reshape(-1, NPOS), 128)
    o["pl_cols"] = chunk(f["L0_tok_pl_w"].reshape(D, -1).T, 128)
    o["pg_bands"] = chunk(f["L0_tok_pg_w1"].reshape(D, 256, CIN).transpose(2, 1, 0).reshape(-1, D), 128)
    o["haar"] = chunk(_haar(), 128)
    o["ident"] = np.eye(128, dtype=np.float32)
    t = {}
    chan = np.zeros((HC, NCH), np.float32)
    scale = np.repeat(f["L0_attn_scale"], HD)
    bqkv = f["L0_attn_b_qkv"].reshape(3, D)
    for c, v in ((C_PLB, f["L0_tok_pl_b"]), (C_PGB, f["L0_tok_pg_b1"]), (C_PLP, f["L0_tok_pl_pwb"]),
                 (C_PGP, f["L0_tok_pg_pwb"]), (C_PGB2, f["L0_tok_pg_b2"]), (C_ALPHA, f["L0_tok_alpha"].reshape(D)),
                 (C_F1, f["L0_tok_f1_pwb"]), (C_F2, f["L0_tok_f2_pwb"]), (C_BQ, bqkv[0][turn]), (C_BK, bqkv[1][turn]),
                 (C_SCALE, scale[turn]), (C_FBQ, f["L0_ffn_bq"][turn]),
                 (C_GAMMA, np.broadcast_to(f["L0_ffn_gamma"], (D,)))):
        chan[:, c:c + 2] = halves(v)
    for r, name in enumerate(("pl", "pg", "f1", "f2", "f3")):
        w = f[f"L0_tok_{name}_dw"].reshape(2, HC, 9).transpose(1, 0, 2).reshape(HC, 18)
        chan[:, C_DW + 18 * r:C_DW + 18 * r + 18] = w
    o["chan"] = chan
    pws = [f[f"L0_tok_{n}_pw"].reshape(D, D).T for n in ("pl", "pg", "f1", "f2", "f3")] + [f["L0_tok_pg_w2"].reshape(D, D).T]
    o["w_pw"] = np.stack([chunk(w) for w in pws], 1)
    wqkv = f["L0_attn_w_qkv"]
    ws = [wqkv[:, 0:D][:, turn], wqkv[:, D:2 * D][:, turn], wqkv[:, 2 * D:], f["L0_attn_w_proj"],
          f["L0_ffn_Wq"].T[:, turn], f["L0_ffn_Wk"].T[:, turn], f["L0_ffn_Wv"].T, f["L0_ffn_Wo"].T]
    o["w_at"] = np.stack([chunk(w) for w in ws], 1)
    rows = [f["L0_tok_f3_pwb"], f["L0_tok_ln_g"], f["L0_tok_ln_b"], bqkv[2], f["L0_attn_b_proj"], f["L0_ffn_bv"],
            f["L0_ffn_bo"], f["L0_ffn_ln1_g"], f["L0_ffn_ln1_b"], f["L0_ffn_ln2_g"], f["L0_ffn_ln2_b"], *f["L0_ffn_b2"]]
    o["rows"] = np.broadcast_to(np.stack(rows)[None], (128, NROW, D))
    masks = np.zeros((128, 2, 2, T), np.float32)
    for j in range(128):
        masks[j, 0, :, j] = BIG
    for b in range(2):
        for j in range(NI):
            masks[64 * b + j, 1, :, NTXT + j] = BIG
    o["masks"] = masks.reshape(128, 2, T2)
    head = np.arange(HC) % HH
    o["same_head"] = (head[:, None] == head[None]).astype(np.float32)
    low = np.tril(np.ones((E, E), np.float32), -1)
    o["lower"] = np.broadcast_to(low.reshape(1, -1), (128, E * E))
    o["bg"] = np.broadcast_to(f["L0_ffn_bg"][None], (128, E))
    o["gate_w"] = chunk(f["L0_ffn_Wg"].T)
    o["b1"] = f["L0_ffn_b1"].reshape(UNITS, 128).T
    o["w1"] = chunk(f["L0_ffn_W1"].transpose(1, 0, 2).reshape(D, E * FF))
    o["w2"] = chunk(f["L0_ffn_W2"].reshape(E * FF, D), 128)
    o["cls8"] = np.broadcast_to(f["L0_tok_cls"].reshape(1, 1, D), (1, PAIRS, D))
    o["txt"] = f["txt"].reshape(PAIRS, 2, NTXT, D)
    return {k: np.ascontiguousarray(v) for k, v in o.items()}


def kernel(**inputs):
    import concourse.bacc as _bacc
    from concourse.bass_utils import run_bass_kernel_spmd as _run

    nc = _bacc.Bacc("TRN2", target_bir_lowering=False, num_devices=1)
    arrays = _layout(inputs)
    aps = {k: nc.dram_tensor(f"in_{k}", v.shape, F32, kind="ExternalInput").ap() for k, v in arrays.items()}
    aps["out"] = nc.dram_tensor("out", (PAIRS, 2, T, D), F32, kind="ExternalOutput").ap()
    build(nc, aps)
    r = _run(nc, [{f"in_{k}": v for k, v in arrays.items()}], core_ids=[0])
    return r.results[0]["out"].reshape(B, T, D)
```

```python
from contextlib import ExitStack

import numpy as np
import concourse.bass as bass
from concourse import mybir

F32 = mybir.dt.float32
BF16 = mybir.dt.bfloat16
ALU = mybir.AluOpType
ACT = mybir.ActivationFunctionType
AX = mybir.AxisListType

B, D, HEADS, HD = 16, 192, 12, 16
HC = D // 2
HH = HEADS // 2
IMG, PATCH, CIN = 112, 16, 3
G7 = IMG // PATCH
NI = G7 * G7
NTXT = 128
NB = NI + 1
T = NTXT + NB
T2 = 2 * T
TP = NTXT + 64
PAIRS = B // 2
KC = CIN * PATCH * PATCH // 128
NPOS = B * NI
NH = NPOS // 2
PITCH = G7 + 1
CELLS = B * PITCH * PITCH
GUARD = 16
E, FF = 4, 768
FT = FF // 128
UNITS = E * FT
TERMS = 6
SROWS = TERMS * HD
XW = 3 * 128
XN = 2 * NTXT + 64 + NB
BIG = -1.0e30
EPS = 1e-5
NCONV = 5

(C_PLB, C_PGB, C_PLP, C_PGP, C_PGB2, C_ALPHA, C_F1, C_F2, C_BQ, C_BK, C_SCALE, C_FBQ, C_GAMMA) = range(0, 26, 2)
C_DW = 26
NCH = C_DW + NCONV * 2 * 9
(R_BV, R_BP, R_FBV, R_BO, R_L1G, R_L1B, R_L2G, R_L2B, R_B2) = range(9)
R_F3B, R_TG, R_TB = range(3)
NROW = R_B2 + E
Q_RUNS = ((0, 0, 1), (1, 0, 1), (2, 0, 1), (3, 1, 1), (4, 1, 1), (5, 2, 1))
K_RUNS = ((0, 0, 3), (3, 0, 2), (5, 0, 1))

PROB_UNITS = 4

CHAIN_STEPS = {"dve_front0": 12, "dve_front1": 16, "dve_max0": 8, "dve_max1": 8, "dve_out0": 1, "dve_out1": 1,
               "dve_x2": 18, "dve_moe": 9, "act_deviation": 2, "pool_moe": 7}
FILL = {
    "start": 2, "norm": 1, "query": 1, "key": 0, "value": 0, "kc": 1, "g": 1, "u": 1, "ss": 1,
    ("max", 0): (0, 0, 1, 0, 0, 0), ("split", 0): 1, ("rows", 0): 2, ("exp", 0): (0, 0, 0, 0, 1, 0), ("out", 0): 0,
    ("max", 1): (0, 1, 0, 1, 0, 0), ("split", 1): 1, ("turn", 0): 1, ("back", 0): 1, ("rows", 1): 1,
    ("exp", 1): (1, 0, 1, 0, 1, 0), ("out", 1): 0, ("turn", 1): 1, ("back", 1): 1,
}


class Chain:

    def __init__(self, eng, sem, per_round, this_round):
        self.eng, self.sem, self.per, self.base, self.n = eng, sem, per_round, this_round * per_round, 0

    def link(self, ins):
        self.n += 1
        ins.then_inc(self.sem, 1)
        self.eng.wait_ge(self.sem, self.base + self.n)

    def end(self):
        assert self.n == self.per, (self.sem, self.n, self.per)


def build(nc, a):
    ctx = ExitStack()
    with ctx:
        def sb(name, shape, dt=F32):
            return ctx.enter_context(nc.sbuf_tensor(name, shape, dt))

        sems = {}

        def sem(name):
            sems[name] = ctx.enter_context(nc.semaphore(name))
            return sems[name]

        def newton(ch, sc):
            ch.link(nc.vector.tensor_tensor(sc[:, 3, :], sc[:, 2, :], sc[:, 2, :], ALU.mult))
            ch.link(nc.vector.tensor_tensor(sc[:, 3, :], sc[:, 3, :], sc[:, 0, :], ALU.mult))
            ch.link(nc.vector.tensor_scalar(sc[:, 3, :], sc[:, 3, :], -0.5, 1.5, ALU.mult, ALU.add))
            ch.link(nc.vector.tensor_tensor(sc[:, 3, :], sc[:, 3, :], sc[:, 2, :], ALU.mult))

        ident = sb("ident", [128, 128])
        ident_bf = sb("ident_bf", [128, 128], BF16)
        masks = sb("masks", [128, 2, T2], BF16)
        same_head = sb("same_head", [HC, HC])
        lower = sb("lower", [128, E * E])
        chan = sb("chan", [HC, NCH])
        rows = sb("rows", [128, NROW, D])
        bg = sb("bg", [128, E])
        gate_w = sb("gate_w", [HC, 2, E])
        b1 = sb("b1", [128, UNITS])
        w_at = sb("w_at", [HC, 8, 2, D])
        w1 = sb("w1", [HC, 2, E * FF])
        w2 = sb("w2", [128, UNITS, D])
        gate = sb("gate", [HC, 2])
        qbias = sb("qbias", [HC, 2])
        img_tok = sb("img_tok", [128, PAIRS, D])

        PS = ctx.enter_context(nc.psum_tensor("PS", [128, 8, 512], F32))
        scr_q = [nc.dram_tensor(f"scr_q{s}", (2, 3, HD, HH * 2 * TP), BF16).ap() for s in range(2)]
        scr_k = [nc.dram_tensor(f"scr_k{s}", (2, 3, HD, HH * 2 * TP), BF16).ap() for s in range(2)]

        ld_haar, ld_cw, ld_const, ld_tok, ld_attn, ld_moe = (
            sem(n) for n in ("ld_haar", "ld_cw", "ld_const", "ld_tok", "ld_attn", "ld_moe"))
        ld_x = [sem(f"ld_x{k}") for k in range(KC)]
        casts = sem("casts")

        with ExitStack() as tk:
            def tsb(name, shape, dt=F32):
                return tk.enter_context(nc.sbuf_tensor(name, shape, dt))

            def tsem(name):
                return ctx.enter_context(nc.semaphore(name))

            masks_f = tsb("masks_f", [128, 2, T2])
            tok_rows = tsb("tok_rows", [128, 3, D])
            cols = tsb("cols", [128, KC, NPOS])
            cw = tsb("cw", [128, KC, 2 * D])
            bands = tsb("bands", [128, KC, D])
            haar = tsb("haar", [128, 2, 256])
            w_pw = tsb("w_pw", [HC, NCONV + 1, 2, D])
            diag = tsb("diag", [HC, NCONV * 9, HC])
            pad_l = tsb("pad_l", [HC, 2, CELLS + 2 * GUARD])
            pad_g = tsb("pad_g", [HC, 2, CELLS + 2 * GUARD])
            dwo = tsb("dwo", [HC, 2, CELLS])
            flat = tsb("flat", [HC, 2, NPOS + 16])
            loc = tsb("loc", [HC, 2, NPOS])
            mid = tsb("mid", [HC, 2, NPOS])
            tstat = tsb("tstat", [128, PAIRS, 6])
            tmv = tsb("tmv", [128, PAIRS, 2])
            tsc = tsb("tsc", [128, 4, PAIRS])

            haar_psum, haar_ready, conv_psum, zeroed, diag_ready = (
                tsem(n) for n in ("haar_psum", "haar_ready", "conv_psum", "zeroed", "diag_ready"))
            pad_ready, dw_vec, dw_psum, dw_pe, pw_psum = (
                tsem(n) for n in ("pad_ready", "dw_vec", "dw_psum", "dw_pe", "pw_psum"))
            loc_ready, gg_ready, glob_psum, gate_ready, f2_relu, tok_var, tok_r0, tok_ready, cls_done, tdve, tact = (
                tsem(n) for n in ("loc_ready", "gg_ready", "glob_psum", "gate_ready", "f2_relu", "tok_var", "tok_r0",
                                  "tok_ready", "cls_done", "tdve", "tact"))

            def cells(t, lo, n):
                v = t[:, lo:lo + n * PITCH * PITCH].rearrange("p (b y x) -> p b y x", y=PITCH, x=PITCH)
                return v[:, :, 0:G7, 0:G7]

            def inner(pad, h, n):
                return cells(pad[:, h, :], GUARD + n * CELLS // 2, B // 2)

            def tap_offset(tap):
                return GUARD + (tap // 3 - 1) * PITCH + tap % 3 - 1

            def image_rows(t, lo):
                return t[:, lo:lo + CELLS].rearrange("p (r x) -> p r x", x=PITCH)[:, :, 0:G7]

            def grid(flat, n):
                return flat[:, NH * n:NH * n + NH].rearrange("p (b y x) -> p b y x", y=G7, x=G7)

            def col(c, h=0):
                return chan[:, c + h:c + h + 1]

            PAD_OF = [pad_l, pad_g, pad_l, pad_g, pad_l]

            with nc.Block() as block:
                @block.sync
                def _(sp):
                    sp.dma_start(haar[:], a["haar"]).then_inc(ld_haar, 16)
                    sp.dma_start(bands[:], a["pg_bands"]).then_inc(ld_haar, 16)
                    for k in range(KC):
                        sp.dma_start(cols[:, k, :], a["x_cols"][:, k, :]).then_inc(ld_x[k], 16)
                    sp.dma_start(w_at[:], a["w_at"]).then_inc(ld_attn, 16)
                    sp.dma_start(w1[:], a["w1"]).then_inc(ld_moe, 16)
                    sp.dma_start(w2[:], a["w2"]).then_inc(ld_moe, 16)
                    sp.wait_ge(tok_ready, 1)
                    for b in range(2):
                        sp.dma_start(img_tok[64 * b + NI:64 * b + NB, :, :], a["cls8"]).then_inc(cls_done, 16)
                    sp.wait_ge(cls_done, 32)

                @block.scalar
                def _(act):
                    act.dma_start(cw[:, :, 0:D], a["pl_cols"]).then_inc(ld_cw, 16)
                    act.dma_start(chan[:], a["chan"]).then_inc(ld_const, 16)
                    act.dma_start(ident[:], a["ident"]).then_inc(ld_const, 16)
                    act.dma_start(w_pw[:], a["w_pw"]).then_inc(ld_tok, 16)
                    act.dma_start(rows[:], a["rows"]).then_inc(ld_tok, 16)
                    act.dma_start(tok_rows[:], a["tok_rows"]).then_inc(ld_tok, 16)
                    act.dma_start(masks_f[:], a["masks"]).then_inc(ld_tok, 16)
                    act.dma_start(same_head[:], a["same_head"]).then_inc(ld_tok, 16)
                    act.dma_start(lower[:], a["lower"]).then_inc(ld_tok, 16)
                    act.dma_start(bg[:], a["bg"]).then_inc(ld_tok, 16)
                    act.dma_start(gate_w[:], a["gate_w"]).then_inc(ld_tok, 16)
                    act.dma_start(b1[:], a["b1"]).then_inc(ld_tok, 16)
                    act.wait_ge(ld_const, 32)
                    nc.scalar.activation(gate[:], chan[:, C_ALPHA:C_ALPHA + 2], ACT.Tanh).then_inc(gate_ready, 1)
                    act.wait_ge(haar_psum, 1)
                    nc.scalar.copy(cw[:, 0:KC, D:2 * D].rearrange("p (g k) d -> p g k d", k=2),
                                   PS[:, 0:3, 0:2 * D].rearrange("p g (k d) -> p g k d", k=2)).then_inc(haar_ready, 1)
                    act.wait_ge(conv_psum, 1)
                    act.wait_ge(zeroed, 1)
                    for m in range(4):
                        pad, bias = (pad_l, C_PLB) if m < 2 else (pad_g, C_PGB)
                        for n in range(2):
                            ins = nc.scalar.activation(inner(pad, m % 2, n), grid(PS[0:HC, 2 * m + n, :], 0), ACT.Gelu,
                                                       bias=col(bias, m % 2))
                        if m % 2:
                            ins.then_inc(pad_ready, 1)

                    def evac_dw(r):
                        act.wait_ge(dw_psum, r + 1)
                        if r == NCONV - 1:
                            nc.scalar.copy(flat[:, 1, 0:NPOS].rearrange("p (n c) -> p n c", n=2), PS[0:HC, 0:2, 0:NH])
                            act.wait_ge(dw_vec, r + 1)
                            nc.scalar.copy(flat[:, 0, 0:NPOS].rearrange("p (b y x) -> p b y x", y=G7, x=G7),
                                           cells(dwo[:, 0, :], 0, B)).then_inc(dw_pe, 1)
                            return
                        for n in range(2):
                            ins = nc.scalar.copy(cells(dwo[:, 1, :], n * CELLS // 2, B // 2), grid(PS[0:HC, n, :], 0))
                        ins.then_inc(dw_pe, 1)

                    def evac_pw(r, out, func, bias, done):
                        act.wait_ge(pw_psum, r + 1)
                        for h in range(2):
                            for n in range(2):
                                ins = nc.scalar.activation(out(h, n), grid(PS[0:HC, 2 + 2 * h + n, :], 0), func,
                                                           bias=col(bias, h))
                        ins.then_inc(done, 1)

                    evac_dw(0)
                    evac_pw(0, lambda h, n: grid(loc[:, h, :], n), ACT.Identity, C_PLP, loc_ready)
                    evac_dw(1)
                    evac_pw(1, lambda h, n: grid(mid[:, h, :], n), ACT.Gelu, C_PGP, gg_ready)
                    evac_dw(2)
                    evac_pw(2, lambda h, n: inner(pad_g, h, n), ACT.Relu, C_F1, pad_ready)
                    evac_dw(3)
                    evac_pw(3, lambda h, n: grid(mid[:, h, :], n), ACT.Relu, C_F2, f2_relu)
                    evac_dw(4)
                    act.wait_ge(tok_var, 1)
                    nc.scalar.activation(tsc[:, 1, :], tsc[:, 0, :], ACT.Ln).then_inc(tact, 1)
                    act.wait_ge(tact, 1)
                    nc.scalar.activation(tsc[:, 2, :], tsc[:, 1, :], ACT.Exp, scale=-0.5).then_inc(tok_r0, 1)

                @block.gpsimd
                def _(pool):
                    nc.gpsimd.memset(pad_l[:], 0.0)
                    nc.gpsimd.memset(pad_g[:], 0.0)
                    nc.gpsimd.memset(flat[:, :, NPOS:NPOS + 16], 0.0).then_inc(zeroed, 1)
                    pool.wait_ge(ld_const, 32)
                    for r in range(NCONV):
                        for t in range(9):
                            ins = nc.gpsimd.tensor_scalar(diag[:, 9 * r + t, :], ident[0:HC, 0:HC],
                                                          col(C_DW + 18 * r + 9 + t), None, ALU.mult)
                        ins.then_inc(diag_ready, 1)

                @block.vector
                def _(dve):
                    ch = Chain(dve, tdve, 0, 0)
                    dve.wait_ge(ld_tok, 9 * 16)
                    nc.vector.tensor_copy(masks[:], masks_f[:])
                    dve.wait_ge(ld_const, 32)
                    nc.vector.tensor_copy(ident_bf[:], ident[:]).then_inc(casts, 1)
                    dve.wait_ge(gate_ready, 1)
                    ch.link(nc.vector.tensor_scalar(gate[:], gate[:], 1.0, 0.5, ALU.add, ALU.mult))
                    ch.link(nc.vector.tensor_tensor(qbias[:], chan[:, C_BQ:C_BQ + 2], chan[:, C_SCALE:C_SCALE + 2], ALU.mult))

                    def depthwise(r):
                        dve.wait_ge(pad_ready, r + 1)
                        if r:
                            dve.wait_ge(pw_psum, r)
                        out = image_rows(dwo[:, 0, :], 0)
                        for t in range(9):
                            w, src = col(C_DW + 18 * r + t), image_rows(PAD_OF[r][:, 0, :], tap_offset(t))
                            if t == 0:
                                ins = nc.vector.tensor_scalar(out, src, w, None, ALU.mult)
                            else:
                                ins = nc.vector.scalar_tensor_tensor(out=out, in0=src, scalar=w, in1=out,
                                                                     op0=ALU.mult, op1=ALU.add)
                            if t < 8:
                                ch.link(ins)
                        ins.then_inc(dw_vec, 1)

                    depthwise(0)
                    depthwise(1)
                    dve.wait_ge(loc_ready, 1)
                    dve.wait_ge(glob_psum, 1)
                    for h in range(2):
                        for n in range(2):
                            c = slice(NH * n, NH * n + NH)
                            ins = nc.vector.scalar_tensor_tensor(out=mid[:, h, c], in0=PS[0:HC, 2 + 2 * h + n, 0:NH],
                                                                 scalar=col(C_PGB2, h), in1=loc[:, h, c],
                                                                 op0=ALU.add, op1=ALU.subtract)
                    ch.link(ins)
                    for h in range(2):
                        ins = nc.vector.tensor_scalar(mid[:, h, :], mid[:, h, :], gate[:, h:h + 1], None, ALU.mult)
                    ch.link(ins)
                    for h in range(2):
                        for n in range(2):
                            ins = nc.vector.tensor_tensor(inner(pad_l, h, n), grid(mid[:, h, :], n), grid(loc[:, h, :], n),
                                                          ALU.add)
                    ins.then_inc(pad_ready, 1)
                    depthwise(2)
                    depthwise(3)
                    dve.wait_ge(f2_relu, 1)
                    for h in range(2):
                        for n in range(2):
                            ins = nc.vector.tensor_tensor(inner(pad_l, h, n), grid(mid[:, h, :], n), grid(loc[:, h, :], n),
                                                          ALU.add)
                    ins.then_inc(pad_ready, 1)
                    depthwise(4)
                    dve.wait_ge(pw_psum, NCONV)
                    ps = PS[:, 0:4, 0:2 * D].rearrange("p g (k d) -> p g k d", k=2)
                    for g in range(4):
                        ins = nc.vector.tensor_tensor(
                            img_tok[:, 2 * g:2 * g + 2, :], ps[:, g], tok_rows[:, R_F3B:R_F3B + 1, :].to_broadcast([128, 2, D]),
                            ALU.add)
                    ch.link(ins)
                    for q in range(PAIRS):
                        ins = nc.vector.bn_stats(tstat[:, q, :], img_tok[:, q, :])
                    ch.link(ins)
                    for q in range(PAIRS):
                        ins = nc.vector.bn_aggr(tmv[:, q, :], tstat[:, q, :])
                    ch.link(ins)
                    nc.vector.tensor_scalar(tsc[:, 0, :], tmv[:, :, 1], EPS, None, ALU.add).then_inc(tok_var, 1)
                    dve.wait_ge(tok_var, 1)
                    dve.wait_ge(tok_r0, 1)
                    newton(ch, tsc)
                    for q in range(PAIRS):
                        ins = nc.vector.tensor_scalar(img_tok[:, q, :], img_tok[:, q, :], tmv[:, q, 0:1], tsc[:, 3, q:q + 1],
                                                      ALU.subtract, ALU.mult)
                    ch.link(ins)
                    ch.link(nc.vector.tensor_tensor(img_tok[:], img_tok[:], tok_rows[:, R_TG:R_TG + 1, :].to_broadcast([128, PAIRS, D]), ALU.mult))
                    nc.vector.tensor_tensor(img_tok[:], img_tok[:], tok_rows[:, R_TB:R_TB + 1, :].to_broadcast([128, PAIRS, D]),
                                            ALU.add).then_inc(tok_ready, 1)

                @block.tensor
                def _(pe):
                    pe.wait_ge(ld_haar, 32)
                    for c in range(CIN):
                        for m in range(2):
                            for k in range(2):
                                ins = nc.tensor.matmul(PS[:, c, D * m:D * m + D], haar[:, k, 128 * m:128 * m + 128],
                                                       bands[:, 2 * c + k, :], start=(k == 0), stop=(k == 1))
                    ins.then_inc(haar_psum, 1)
                    pe.wait_ge(ld_cw, 16)
                    pe.wait_ge(haar_ready, 1)
                    for k in range(KC):
                        pe.wait_ge(ld_x[k], 16)
                        for m in range(4):
                            for n in range(2):
                                ins = nc.tensor.matmul(PS[0:HC, 2 * m + n, 0:NH], cw[:, k, HC * m:HC * m + HC],
                                                       cols[:, k, NH * n:NH * n + NH], start=(k == 0), stop=(k == KC - 1))
                    ins.then_inc(conv_psum, 1)

                    def depthwise(r):
                        pe.wait_ge(pad_ready, r + 1)
                        pe.wait_ge(diag_ready, r + 1)
                        for n in range(2):
                            for t in range(9):
                                ins = nc.tensor.matmul(PS[0:HC, n, 0:NH], diag[:, 9 * r + t, :],
                                                       cells(PAD_OF[r][:, 1, :], tap_offset(t) + n * CELLS // 2, B // 2), start=(t == 0), stop=(t == 8))
                        ins.then_inc(dw_psum, 1)

                    def pointwise(w, src, done):
                        for m in range(2):
                            for n in range(2):
                                for k in range(2):
                                    ins = nc.tensor.matmul(PS[0:HC, 2 + 2 * m + n, 0:NH], w_pw[:, w, k, HC * m:HC * m + HC],
                                                           src(k, n), start=(k == 0), stop=(k == 1))
                        ins.then_inc(done, 1)

                    pe.wait_ge(ld_tok, 9 * 16)
                    pe.wait_ge(pad_ready, 2)
                    for r in range(NCONV):
                        depthwise(r)
                        pe.wait_ge(dw_vec, r + 1)
                        pe.wait_ge(dw_pe, r + 1)
                        if r == 1:
                            pe.wait_ge(loc_ready, 1)
                        if r < NCONV - 1:
                            pointwise(r, lambda k, n: cells(dwo[:, k, :], n * CELLS // 2, B // 2), pw_psum)
                        if r == 1:
                            pe.wait_ge(gg_ready, 1)
                            pointwise(NCONV, lambda k, n: mid[:, k, NH * n:NH * n + NH], glob_psum)
                    for q in range(PAIRS):
                        for b in range(2):
                            at = NI * (2 * q + b)
                            for k in range(2):
                                ins = nc.tensor.matmul(PS[64 * b:64 * b + 64, q // 2, D * (q % 2):D * (q % 2) + D],
                                                       flat[:, k, at:at + 64], w_pw[:, NCONV - 1, k, :],
                                                       start=(k == 0), stop=(k == 1), skip_group_check=True)
                    ins.then_inc(pw_psum, 1)

        h0 = sb("h0", [128, 3, D])
        h1 = sb("h1", [128, 3, D])
        h1_keep = sb("h1_keep", [128, 3, D])
        h1_fin = sb("h1_fin", [128, 3, D])
        xn = [sb(f"xn{s}", [128, 3, D]) for s in range(2)]
        x2 = sb("x2", [128, 3, D])
        acc = sb("acc", [128, 3, D])
        fin = sb("fin", [128, 3, D])
        stat = sb("stat", [128, 2, 3, 6])
        mv = sb("mv", [128, 2, 3, 2])
        lsc = [sb(f"lsc{i}", [128, 4, 3]) for i in range(2)]
        xT = [sb(f"xT{s}", [HC, 2, XW]) for s in range(2)]
        x2T = sb("x2T", [HC, 2, XW])
        xbar = sb("xbar", [HC, 2, 2, 2])
        q32 = [sb(f"q32{s}", [HC, 2, 2, TP]) for s in range(2)]
        k32 = sb("k32", [HC, 2, 2, TP])
        rem = sb("rem", [HC, 2, 2, TP])
        qs = sb("qs", [HC, 2, 3, 2 * TP], BF16)
        ks = sb("ks", [HC, 2, 3, 2 * TP], BF16)
        qst = [sb(f"qst{s}", [128, HEADS, 2 * TP], BF16) for s in range(2)]
        kst = [sb(f"kst{s}", [128, HEADS, 2 * TP], BF16) for s in range(2)]
        va = [sb(f"va{s}", [128, 4, HEADS, 32]) for s in range(2)]
        kct = sb("kct", [128, 4, D])
        gsb = sb("gsb", [HC, 4, HC])
        mx = sb("mx", [128, 3, HEADS])
        mneg = sb("mneg", [128, 3, HEADS])
        mpart = sb("mpart", [128, 3, 3, HEADS])
        mbf = sb("mbf", [128, 3, HEADS], BF16)
        mrows = sb("mrows", [3 * HEADS, 2 * TP], BF16)
        probs = sb("probs", [128, PROB_UNITS, 3, T2])
        osb = sb("osb", [128, 3, XW])
        rs = sb("rs", [128, 3, HEADS])
        on = sb("on", [128, 3, D])
        oT = sb("oT", [HC, 2, XW])
        xc = oT
        gl = sb("gl", [128, 3, E])
        gs = sb("gs", [128, 3, 2])
        cmp1 = sb("cmp1", [128, 3, E, E])
        cmp2 = sb("cmp2", [128, 3, E, E])
        comb = sb("comb", [128, 3, E])
        hid = [sb(f"hid{i}", [128, XW]) for i in range(2)]

        both = ("ln_var ln_r0 xn_ready xT_psum xT_ready q_psum q_f32 k_psum k_f32 v_psum v_ready q_split k_split "
                "q_stored k_stored q_stacked k_stacked s_psum s_used m_split mT_psum m_rows m_stacked e_psum e_done "
                "pv_psum o_ready oT_psum on_ready oc_psum oc_ready pr_psum pr_read res_ready act_ln").split()
        S = {(n, s): sem(f"{n}{s}") for n in both for s in range(2)}
        names = ("preset txt_in img_in h1_kept xc_ready kc_psum kc_ready g_psum g_ready u_psum prod_ready ss_psum ss_read "
                 "qf_ready x2_var x2_ln x2_r0 x2_ready x2T_psum x2T_ready gate_psum gate_used gl_ready ge_ready comb_ready "
                 "h_psum h_ready h_used y_used b2_ready fin_var fin_ln fin_r0 fin_ready fin_h1 stored passed").split()
        S.update({n: sem(n) for n in names + list(CHAIN_STEPS)})

        def plain_wait(eng):
            eng.sem_inc(S["passed"], 1)

        def at(n, per, k):
            return n * per + k

        def chain(eng, name, r):
            return Chain(eng, S[name], CHAIN_STEPS[name], r)

        def text(t):
            return t[:, :, 0:2 * NTXT].rearrange("p h (b j) -> p h b j", b=2)

        def images(t, n=NB):
            return t[:, :, 2 * NTXT:XW].rearrange("p h (b j) -> p h b j", b=2)[:, :, :, 0:n]

        def tile_cols(t, half, i):
            return t[:, half, 128 * i:128 * i + 128]

        def tile_psum(banks, i):
            return PS[:, banks[0], D * i:D * i + D] if i < 2 else PS[:, banks[1], 0:D]

        def row(r, n):
            return rows[:, r:r + 1, :].to_broadcast([128, n, D])

        FRONT = ((0, 1), (2, 3))


        class MoePe:

            def __init__(self, pe, m):
                self.pe, self.m, self.u = pe, m, 0

            def second(self, u):
                pe, m = self.pe, self.m
                e, j = divmod(u, FT)
                pe.wait_ge(S["h_ready"], at(m, UNITS, u + 1))
                if j == 0 and e > 0:
                    pe.wait_ge(S["y_used"], at(m, E, e))
                for i in range(3):
                    ins = nc.tensor.matmul(tile_psum((6, 7), i), hid[u % 2][:, 128 * i:128 * i + 128], w2[:, u, :],
                                           start=(j == 0 and i != 1), stop=(j == FT - 1), skip_group_check=True)
                ins.then_inc(S["h_used"], 1)

            def units(self, n):
                pe, m = self.pe, self.m
                end = min(self.u + n, UNITS)
                for u in range(self.u, end):
                    if u >= 2:
                        pe.wait_ge(S["h_ready"], at(m, UNITS, u - 1))
                    for k in range(2):
                        ins = nc.tensor.matmul(PS[:, 4 + u % 2, 0:XN], w1[:, k, 128 * u:128 * u + 128],
                                               x2T[:, k, 0:XN], start=(k == 0), stop=(k == 1))
                    ins.then_inc(S["h_psum"], 1)
                    if u:
                        self.second(u - 1)
                before, self.u = self.u, end
                if before < end == UNITS:
                    self.second(UNITS - 1)

        class MoeAct:

            def __init__(self, act, m):
                self.act, self.m, self.u = act, m, 0

            def units(self, n):
                end = min(self.u + n, UNITS)
                for u in range(self.u, end):
                    self.act.wait_ge(S["h_psum"], at(self.m, UNITS, u + 1))
                    if u >= 2:
                        self.act.wait_ge(S["h_used"], at(self.m, UNITS, u - 1))
                    nc.scalar.activation(hid[u % 2][:, 0:XN], PS[:, 4 + u % 2, 0:XN], ACT.Relu,
                                         bias=b1[:, u:u + 1]).then_inc(S["h_ready"], 1)
                self.u = end

            def finish(self):
                act, m = self.act, self.m
                act.wait_ge(S["fin_var"], at(m, 1, 1))
                nc.scalar.activation(lsc[1][:, 1, :], lsc[1][:, 0, :], ACT.Ln).then_inc(S["fin_ln"], 1)
                act.wait_ge(S["fin_ln"], at(m, 1, 1))
                nc.scalar.activation(lsc[1][:, 2, :], lsc[1][:, 1, :], ACT.Exp, scale=-0.5).then_inc(S["fin_r0"], 1)

        class MoeDve:

            def __init__(self, dve, m):
                self.dve, self.m, self.u = dve, m, 0
                self.ch = chain(dve, "dve_moe", m)

            def expert(self, e):
                dve, m = self.dve, self.m
                if e == 0:
                    dve.wait_ge(S["b2_ready"], at(m, 1, 1))
                dve.wait_ge(S["h_used"], at(m, UNITS, FT * (e + 1)))
                for i in range(3):
                    ins = nc.vector.scalar_tensor_tensor(out=acc[:, i, :], in0=tile_psum((6, 7), i),
                                                         scalar=comb[:, i, e:e + 1], in1=acc[:, i, :],
                                                         op0=ALU.mult, op1=ALU.add)
                ins.then_inc(S["y_used"], 1)
                dve.wait_ge(S["y_used"], at(m, E, e + 1))

            def units(self, n):
                end = min(self.u + n, UNITS)
                for u in range(self.u, end):
                    if u and u % FT == 0:
                        self.expert(u // FT - 1)
                before, self.u = self.u, end
                if before < end == UNITS:
                    self.expert(E - 1)

            def finish(self):
                dve, m, ch = self.dve, self.m, self.ch
                for i in range(3):
                    ins = nc.vector.bn_stats(stat[:, 1, i, :], acc[:, i, :])
                ch.link(ins)
                plain_wait(dve)
                for i in range(3):
                    ins = nc.vector.bn_aggr(mv[:, 1, i, :], stat[:, 1, i, :])
                ch.link(ins)
                nc.vector.tensor_scalar(lsc[1][:, 0, :], mv[:, 1, :, 1], EPS, None, ALU.add).then_inc(S["fin_var"], 1)
                dve.wait_ge(S["fin_r0"], at(m, 1, 1))
                newton(ch, lsc[1])
                for i in range(3):
                    ins = nc.vector.tensor_scalar(fin[:, i, :], acc[:, i, :], mv[:, 1, i, 0:1], lsc[1][:, 3, i:i + 1],
                                                  ALU.subtract, ALU.mult)
                ch.link(ins)
                ch.link(nc.vector.tensor_tensor(fin[:], fin[:], row(R_L2G, 3), ALU.mult))
                ch.link(nc.vector.tensor_tensor(fin[:], fin[:], row(R_L2B, 3), ALU.add))
                dve.wait_ge(S["fin_h1"], at(m, 1, 1))
                nc.vector.tensor_tensor(fin[:], fin[:], h1_fin[:], ALU.add).then_inc(S["fin_ready"], 1)
                ch.end()

        class NoMoe:
            def units(self, n):
                pass

            def finish(self):
                pass

        def moe_of(cls, eng, m):
            return NoMoe() if m is None else cls(eng, m)


        def pe_turn_in(pe, s, r):
            pe.wait_ge(S["xn_ready", s], at(r, 1, 1))
            for h in range(2):
                for i in range(3):
                    ins = nc.tensor.transpose(PS[0:HC, FRONT[s][h], 128 * i:128 * i + 128], xn[s][:, i, HC * h:HC * h + HC],
                                              ident[:])
            ins.then_inc(S["xT_psum", s], 1)

        def pe_project(pe, s, w, x, done):
            for m in range(2):
                for k in range(2):
                    ins = nc.tensor.matmul(PS[0:HC, FRONT[s][m], 0:XN], w_at[:, w, k, HC * m:HC * m + HC], x[:, k, 0:XN],
                                           start=(k == 0), stop=(k == 1))
            ins.then_inc(done, 1)

        def pe_tokens(banks, w, x, done):
            for i in range(3):
                for k in range(2):
                    ins = nc.tensor.matmul(tile_psum(banks, i), tile_cols(x, k, i), w_at[:, w, k, :],
                                           start=(k == 0), stop=(k == 1))
            ins.then_inc(done, 1)

        def pe_query(pe, s, r):
            pe.wait_ge(S["xT_ready", s], at(r, 1, 1))
            pe_project(pe, s, 4 * s, xT[s], S["q_psum", s])

        def pe_key(pe, s, r):
            if s:
                pe.wait_ge(S["xc_ready"], at(r, 1, 1))
            pe.wait_ge(S["q_f32", s], at(r, 1, 1))
            pe_project(pe, s, 4 * s + 1, xc if s else xT[0], S["k_psum", s])

        def pe_value(pe, s, r):
            pe.wait_ge(S["k_f32", s], at(r, 1, 1))
            pe_tokens(FRONT[s], 4 * s + 2, xT[s], S["v_psum", s])

        def pe_logits(pe, s, r, u, rows_, still, move, read, filled):
            for bank in range(3):
                if u:
                    pe.wait_ge(read, at(r, 3 * HH, 3 * u - 2 + bank))
                if s == 0:
                    nc.tensor.matmul(PS[:, bank, 0:T2], ident_bf[:], masks[:, bank // 2, :], start=True, stop=False,
                                     skip_group_check=True)
                if bank < 2:
                    h = 2 * u + bank
                    for b in range(2):
                        ins = nc.tensor.matmul(PS[:, bank, T * b:T * b + T], still[0:rows_, h, TP * b:TP * b + NTXT],
                                               move[0:rows_, h, TP * b:TP * b + T], start=(s == 1), stop=True,
                                               skip_group_check=True)
                else:
                    for g in range(2):
                        for b in range(2):
                            ins = nc.tensor.matmul(PS[64 * b:64 * b + 64, 2, T * g:T * g + T],
                                                   still[0:rows_, 2 * u + g, TP * b + NTXT:TP * b + TP],
                                                   move[0:rows_, 2 * u + g, TP * b:TP * b + T], start=(s == 1), stop=True,
                                                   skip_group_check=True)
                ins.then_inc(filled, 1)

        def pe_max_pass(pe, s, r, moe):
            pe.wait_ge(S["q_stacked", s], at(r, 16 * len(Q_RUNS), 16 * len(Q_RUNS)))
            pe.wait_ge(S["k_stacked", s], at(r, 16 * len(K_RUNS), 16 * len(K_RUNS)))
            for u in range(HH):
                pe_logits(pe, s, r, u, SROWS, qst[s], kst[s], S["s_used", s], S["s_psum", s])
                moe.units(FILL["max", s][u])

        def pe_max_rows(pe, s, r):
            pe.wait_ge(S["m_split", s], at(r, 1, 1))
            plain_wait(pe)
            for i in range(3):
                src = mpart[:, i, :, :].rearrange("p c h -> p (c h)")
                ins = nc.tensor.transpose(PS[0:3 * HEADS, 3, 128 * i:128 * i + 128], src, ident[:])
            ins.then_inc(S["mT_psum", s], 1)

        def pe_exp_pass(pe, s, r, moe):
            pe.wait_ge(S["s_used", s], at(r, 3 * HH, 3 * HH))
            pe.wait_ge(S["m_stacked", s], at(r, 48, 48))
            for u in range(HH):
                pe_logits(pe, s, r, u, SROWS + 3, kst[s], qst[s], S["e_done", s], S["e_psum", s])
                moe.units(FILL["exp", s][u])
                if u % 2 == 0 and u:
                    pe_values(pe, s, r, u // 2 - 1)
            pe_values(pe, s, r, HH // 2 - 1)

        def pe_values(pe, s, r, g):
            pe.wait_ge(S["e_done", s], at(r, 3 * HH, 6 * g + 6))
            if g:
                pe.wait_ge(S["o_ready", s], at(r, 3, g))
            for b in range(2):
                for i in range(2):
                    for q in range(4):
                        h = 4 * g + q
                        slot = h // 2 % PROB_UNITS
                        pr = probs[:, slot, h % 2, T * b:T * b + T] if i == 0 else \
                            probs[:, slot, 2, T * (h % 2):T * (h % 2) + T]
                        ins = nc.tensor.matmul(PS[32 * q:32 * q + 32, 3, T * b:T * b + T], va[s][:, 2 * i + b, h, :],
                                               pr, start=(i == 0), stop=(i == 1), skip_group_check=True)
            ins.then_inc(S["pv_psum", s], 1)

        def pe_out(pe, s, r, moe):
            pe.wait_ge(S["o_ready", s], at(r, 3, 3))
            for i in range(3):
                for g in range(3):
                    ins = nc.tensor.transpose(PS[:, i, 128 * g:128 * g + 128], osb[:, g, 128 * i:128 * i + 128], ident[:])
            ins.then_inc(S["oT_psum", s], 1)
            moe.units(FILL["turn", s])
            pe.wait_ge(S["on_ready", s], at(r, 1, 1))
            for h in range(2):
                for i in range(3):
                    ins = nc.tensor.transpose(PS[0:HC, h, 128 * i:128 * i + 128], on[:, i, HC * h:HC * h + HC], ident[:])
            ins.then_inc(S["oc_psum", s], 1)
            moe.units(FILL["back", s])
            pe.wait_ge(S["oc_ready", s], at(r, 1, 1))
            pe_tokens((2, 3), 4 * s + 3, oT, S["pr_psum", s])

        def pe_deviation(pe, b, moe):
            pe_tokens((0, 1), 5, xc, S["kc_psum"])
            moe.units(FILL["kc"])
            pe.wait_ge(S["kc_ready"], at(b, 1, 1))
            pe.wait_ge(S["v_ready", 1], at(b, 1, 1))
            for c in range(2):
                for h in range(2):
                    for i in range(2):
                        x = kct[:, 2 * i + c, HC * h:HC * h + HC]
                        o = HC * (2 * h + c)
                        ins = nc.tensor.matmul(PS[0:HC, 2, o:o + HC], x, x, start=(i == 0), stop=(i == 1))
            ins.then_inc(S["g_psum"], 1)
            moe.units(FILL["g"])
            pe.wait_ge(S["g_ready"], at(b, 1, 1))
            for h in range(2):
                for c in range(2):
                    ins = nc.tensor.matmul(PS[0:HC, h, T * c:T * c + T], gsb[:, 2 * h + c, :], q32[1][:, h, c, 0:T],
                                           start=True, stop=True)
            ins.then_inc(S["u_psum"], 1)
            moe.units(FILL["u"])
            pe.wait_ge(S["prod_ready"], at(b, 1, 1))
            for h in range(2):
                ins = nc.tensor.matmul(PS[0:HC, (2, 3)[h], 0:T2], same_head[:], rem[:, h, :, 0:T], start=True, stop=True)
            ins.then_inc(S["ss_psum"], 1)

        def pe_round(pe, a, b, nxt, m):
            moe = moe_of(MoePe, pe, m)
            moe.units(FILL["start"])
            if b is not None:
                if m is not None:
                    pe.wait_ge(S["gate_used"], at(b, 1, 0))
                pe_turn_in(pe, 1, b)
                moe.units(FILL["norm"])
                pe_query(pe, 1, b)
                moe.units(FILL["query"])
                pe_key(pe, 1, b)
                moe.units(FILL["key"])
                pe_value(pe, 1, b)
                moe.units(FILL["value"])
                if a is not None:
                    pe.wait_ge(S["v_ready", 0], at(a, 1, 1))
                pe_deviation(pe, b, moe)
                moe.units(FILL["ss"])
                pe.wait_ge(S["ss_read"], at(b, 1, 1))
            if a is not None:
                if b is None:
                    pe.wait_ge(S["v_ready", 0], at(a, 1, 1))
                pe_max_pass(pe, 0, a, moe)
                moe.units(FILL["split", 0])
                pe_max_rows(pe, 0, a)
                moe.units(FILL["rows", 0])
                pe_exp_pass(pe, 0, a, moe)
                moe.units(FILL["out", 0])
                pe.wait_ge(S["e_done", 0], at(a, 3 * HH, 3 * HH))
            if b is not None:
                pe_max_pass(pe, 1, b, moe)
                moe.units(FILL["split", 1])
                if a is not None:
                    pe.wait_ge(S["o_ready", 0], at(a, 3, 3))
                pe_max_rows(pe, 1, b)
                pe.wait_ge(S["m_rows", 1], at(b, 1, 1))
            if a is not None:
                pe_out(pe, 0, a, moe)
                moe.units(FILL["rows", 1])
                pe.wait_ge(S["pr_read", 0], at(a, 1, 1))
            if b is not None:
                pe_exp_pass(pe, 1, b, moe)
                moe.units(FILL["out", 1])
                pe.wait_ge(S["e_done", 1], at(b, 3 * HH, 3 * HH))
                pe_out(pe, 1, b, moe)
            moe.units(UNITS)
            if nxt is not None:
                pe_turn_in(pe, 0, nxt)
                pe_query(pe, 0, nxt)
                pe_key(pe, 0, nxt)
            if b is not None:
                pe.wait_ge(S["x2_ready"], at(b, 1, 1))
                for h in range(2):
                    for i in range(3):
                        ins = nc.tensor.transpose(PS[0:HC, (2, 3)[h], 128 * i:128 * i + 128], x2[:, i, HC * h:HC * h + HC],
                                                  ident[:])
                ins.then_inc(S["x2T_psum"], 1)
            if nxt is not None:
                pe_value(pe, 0, nxt)
            if b is not None:
                pe.wait_ge(S["x2T_ready"], at(b, 1, 1))
                for i in range(3):
                    for k in range(2):
                        ins = nc.tensor.matmul(PS[:, 2, E * i:E * i + E], tile_cols(x2T, k, i), gate_w[:, k, :],
                                               start=(k == 0), stop=(k == 1))
                ins.then_inc(S["gate_psum"], 1)


        def by_token(bank, half=slice(0, HC)):
            return (PS[half, bank, 0:2 * NTXT].rearrange("p (b j) -> p b j", b=2),
                    PS[half, bank, 2 * NTXT:XW].rearrange("p (b j) -> p b j", b=2)[:, :, 0:NB])

        def act_root(act, sc, var, ln, r0, r):
            act.wait_ge(var, at(r, 1, 1))
            nc.scalar.activation(sc[:, 1, :], sc[:, 0, :], ACT.Ln).then_inc(ln, 1)
            act.wait_ge(ln, at(r, 1, 1))
            nc.scalar.activation(sc[:, 2, :], sc[:, 1, :], ACT.Exp, scale=-0.5).then_inc(r0, 1)

        def act_norm(act, s, r):
            act_root(act, lsc[0], S["ln_var", s], S["act_ln", s], S["ln_r0", s], r)

        def act_turn_in(act, s, r):
            act.wait_ge(S["xT_psum", s], at(r, 1, 1))
            src = PS[0:HC, 0:2, 0:XW] if s == 0 else PS[0:HC, 2:4, 0:XW]
            nc.scalar.copy(xT[s][:], src).then_inc(S["xT_ready", s], 1)

        def act_query(act, s, r):
            act.wait_ge(S["q_psum", s], at(r, 1, 1))
            for h in range(2):
                for src, c in zip(by_token(FRONT[s][h]), (slice(0, NTXT), slice(NTXT, T))):
                    if s == 0:
                        ins = nc.scalar.activation(q32[0][:, h, :, c], src, ACT.Identity, bias=qbias[:, h:h + 1],
                                                   scale=chan[:, C_SCALE + h:C_SCALE + h + 1])
                    else:
                        ins = nc.scalar.activation(q32[1][:, h, :, c], src, ACT.Identity,
                                                   bias=chan[:, C_FBQ + h:C_FBQ + h + 1])
            ins.then_inc(S["q_f32", s], 1)

        def act_key(act, s, r, before):
            act.wait_ge(S["k_psum", s], at(r, 1, 1))
            if before is not None:
                act.wait_ge(S["k_split", 1 - s], at(before, 1, 1))
            for h in range(2):
                for src, c in zip(by_token(FRONT[s][h]), (slice(0, NTXT), slice(NTXT, T))):
                    if s == 0:
                        ins = nc.scalar.activation(k32[:, h, :, c], src, ACT.Identity, bias=chan[:, C_BK + h:C_BK + h + 1])
                    else:
                        ins = nc.scalar.copy(k32[:, h, :, c], src)
            ins.then_inc(S["k_f32", s], 1)

        def act_max_rows(act, s, r):
            act.wait_ge(S["mT_psum", s], at(r, 1, 1))
            v = mrows[:].rearrange("p (b j) -> p b j", b=2)
            nc.scalar.copy(v[:, :, 0:NTXT], PS[0:3 * HEADS, 3, 0:256].rearrange("p (b j) -> p b j", b=2))
            nc.scalar.copy(v[:, :, NTXT:TP], PS[0:3 * HEADS, 3, 256:384].rearrange("p (b j) -> p b j", b=2))\
                .then_inc(S["m_rows", s], 1)

        def act_exp_pass(act, s, r, moe):
            for u in range(HH):
                if u == PROB_UNITS:
                    act.wait_ge(S["pv_psum", s], at(r, 3, 1))
                for bank in range(3):
                    act.wait_ge(S["e_psum", s], at(r, 3 * HH, 3 * u + bank + 1))
                    nc.scalar.activation(probs[:, u % PROB_UNITS, bank, :], PS[:, bank, 0:T2], ACT.Exp)\
                        .then_inc(S["e_done", s], 1)
                moe.units(FILL["exp", s][u])
                if u % 2 == 0 and u:
                    act_values(act, s, r, u // 2 - 1)
            act_values(act, s, r, HH // 2 - 1)

        def act_values(act, s, r, g):
            act.wait_ge(S["pv_psum", s], at(r, 3, g + 1))
            o = PS[:, 3, 0:T2].rearrange("p (b j) -> p b j", b=2)
            nc.scalar.copy(osb[:, g, 0:2 * NTXT].rearrange("p (b j) -> p b j", b=2), o[:, :, 0:NTXT])
            nc.scalar.copy(osb[:, g, 2 * NTXT:XW].rearrange("p (b j) -> p b j", b=2)[:, :, 0:NB], o[:, :, NTXT:T])\
                .then_inc(S["o_ready", s], 1)

        def act_out(act, s, r, moe):
            moe.units(FILL["turn", s])
            act.wait_ge(S["oc_psum", s], at(r, 1, 1))
            nc.scalar.copy(oT[:], PS[0:HC, 0:2, 0:XW]).then_inc(S["oc_ready", s], 1)
            moe.units(FILL["back", s])

        def act_deviation(act, b, moe):
            act.wait_ge(S["kc_psum"], at(b, 1, 1))
            nc.scalar.copy(kct[:, 0:2, :].rearrange("p i d -> p (i d)"), PS[:, 0, 0:2 * D])
            nc.scalar.copy(kct[0:NB, 2, :], PS[0:NB, 1, 0:D])
            nc.scalar.copy(kct[64:64 + NB, 3, :], PS[64:64 + NB, 1, 0:D]).then_inc(S["kc_ready"], 1)
            moe.units(FILL["kc"])
            moe.units(FILL["g"])
            moe.units(FILL["u"])
            act.wait_ge(S["ss_psum"], at(b, 1, 1))
            ch = chain(act, "act_deviation", b)
            z = rem[:, :, :, 0:T]
            nc.scalar.activation(z, PS[0:HC, 2:4, 0:T2].rearrange("p h (b j) -> p h b j", b=2), ACT.Ln, bias=1e-18,
                                 scale=1.0 / (T - 1)).then_inc(S["ss_read"], 1)
            act.wait_ge(S["ss_read"], at(b, 1, 1))
            ch.link(nc.scalar.activation(z, z, ACT.Exp, scale=0.5))
            ch.link(nc.scalar.activation(z, z, ACT.Ln, bias=EPS / HD ** -0.5))
            nc.scalar.activation(z, z, ACT.Exp, scale=-1.0).then_inc(S["qf_ready"], 1)
            ch.end()

        def act_round(act, a, b, nxt, m):
            moe = moe_of(MoeAct, act, m)
            moe.units(FILL["start"])
            if b is not None:
                act_norm(act, 1, b)
                act_turn_in(act, 1, b)
                moe.units(FILL["norm"])
                act_query(act, 1, b)
                moe.units(FILL["query"])
                act_key(act, 1, b, a)
                moe.units(FILL["key"])
                moe.units(FILL["value"])
                act_deviation(act, b, moe)
                moe.units(FILL["ss"])
            if a is not None:
                for u in range(HH):
                    moe.units(FILL["max", 0][u])
                moe.units(FILL["split", 0])
                act_max_rows(act, 0, a)
                moe.units(FILL["rows", 0])
                act_exp_pass(act, 0, a, moe)
                moe.units(FILL["out", 0])
            if b is not None:
                for u in range(HH):
                    moe.units(FILL["max", 1][u])
                moe.units(FILL["split", 1])
                act_max_rows(act, 1, b)
            if a is not None:
                act_out(act, 0, a, moe)
                moe.units(FILL["rows", 1])
            if b is not None:
                act_exp_pass(act, 1, b, moe)
                moe.units(FILL["out", 1])
            if nxt is not None:
                act_norm(act, 0, nxt)
            if b is not None:
                act_out(act, 1, b, moe)
            moe.units(UNITS)
            moe.finish()
            if nxt is not None:
                act_turn_in(act, 0, nxt)
                act_query(act, 0, nxt)
                act_key(act, 0, nxt, b)
            if b is not None:
                act_root(act, lsc[0], S["x2_var"], S["x2_ln"], S["x2_r0"], b)
                act.wait_ge(S["x2T_psum"], at(b, 1, 1))
                nc.scalar.copy(x2T[:], PS[0:HC, 2:4, 0:XW]).then_inc(S["x2T_ready"], 1)
                act.wait_ge(S["gl_ready"], at(b, 1, 1))
                nc.scalar.activation(gl[:], gl[:], ACT.Exp).then_inc(S["ge_ready"], 1)


        def dve_norm(dve, ch, x, y, var, r0, r, done, gain=None):
            for i in range(3):
                ins = nc.vector.bn_stats(stat[:, 0, i, :], x[:, i, :])
            ch.link(ins)
            plain_wait(dve)
            for i in range(3):
                ins = nc.vector.bn_aggr(mv[:, 0, i, :], stat[:, 0, i, :])
            ch.link(ins)
            nc.vector.tensor_scalar(lsc[0][:, 0, :], mv[:, 0, :, 1], EPS, None, ALU.add).then_inc(var, 1)
            dve.wait_ge(r0, at(r, 1, 1))
            newton(ch, lsc[0])
            for i in range(3):
                ins = nc.vector.tensor_scalar(y[:, i, :], x[:, i, :], mv[:, 0, i, 0:1], lsc[0][:, 3, i:i + 1],
                                              ALU.subtract, ALU.mult)
            if gain is not None:
                ch.link(ins)
                ch.link(nc.vector.tensor_tensor(y[:], y[:], row(gain, 3), ALU.mult))
                ins = nc.vector.tensor_tensor(y[:], y[:], row(gain + 1, 3), ALU.add)
            ins.then_inc(done, 1)

        def dve_split(ch, x, parts, done):
            v = [parts[:, :, c].rearrange("p h (b j) -> p h b j", b=2)[:, :, :, 0:T] for c in range(3)]
            ch.link(nc.vector.tensor_copy(v[0], x[:, :, :, 0:T]))
            ch.link(nc.vector.tensor_tensor(rem[:, :, :, 0:T], x[:, :, :, 0:T], v[0], ALU.subtract))
            ch.link(nc.vector.tensor_copy(v[1], rem[:, :, :, 0:T]))
            nc.vector.tensor_tensor(v[2], rem[:, :, :, 0:T], v[1], ALU.subtract).then_inc(done, 1)

        def dve_value(dve, s, r):
            dve.wait_ge(S["v_psum", s], at(r, 1, 1))
            bv = R_FBV if s else R_BV
            bias = rows[:, bv:bv + 1, :].rearrange("p i (h d) -> p i h d", d=HD)
            nc.vector.tensor_tensor(va[s][:, 0:2, :, 0:HD], PS[:, FRONT[s][0], 0:2 * D].rearrange("p (i h d) -> p i h d", i=2, d=HD),
                                    bias.to_broadcast([128, 2, HEADS, HD]), ALU.add)
            for b in range(2):
                t = slice(64 * b, 64 * b + NB)
                ins = nc.vector.tensor_tensor(va[s][t, 2 + b, :, 0:HD],
                                              PS[t, FRONT[s][1], 0:D].rearrange("p (h d) -> p h d", d=HD),
                                              rows[t, bv, :].rearrange("p (h d) -> p h d", d=HD), ALU.add)
            ins.then_inc(S["v_ready", s], 1)

        def dve_front0(dve, r):
            ch = chain(dve, "dve_front0", r)
            dve.wait_ge(S["txt_in"], at(r, 32, 32))
            dve.wait_ge(S["img_in"], at(r, 1, 1))
            dve_norm(dve, ch, h0, xn[0], S["ln_var", 0], S["ln_r0", 0], r, S["xn_ready", 0])

            def splits(before):
                dve.wait_ge(S["q_f32", 0], at(r, 1, 1))
                if before is not None:
                    dve.wait_ge(S["q_stored", 1], at(before, 16, 16))
                dve_split(ch, q32[0], qs, S["q_split", 0])
                dve.wait_ge(S["q_split", 0], at(r, 1, 1))
                dve.wait_ge(S["k_f32", 0], at(r, 1, 1))
                if before is not None:
                    dve.wait_ge(S["k_stored", 1], at(before, 16, 16))
                dve_split(ch, k32, ks, S["k_split", 0])
                ch.end()
            return splits

        def dve_front1(dve, r, a):
            ch = chain(dve, "dve_front1", r)
            dve.wait_ge(S["res_ready", 0], at(r, 1, 1))
            dve_norm(dve, ch, h1, xn[1], S["ln_var", 1], S["ln_r0", 1], r, S["xn_ready", 1])
            dve.wait_ge(S["xT_ready", 1], at(r, 1, 1))
            nc.vector.tensor_reduce(xbar[:, 0], text(xT[1]), AX.X, ALU.add)
            ch.link(nc.vector.tensor_reduce(xbar[:, 1], images(xT[1]), AX.X, ALU.add))
            ch.link(nc.vector.tensor_tensor(xbar[:, 0], xbar[:, 0], xbar[:, 1], ALU.add))
            ch.link(nc.vector.tensor_scalar(xbar[:, 0], xbar[:, 0], 1.0 / T, None, ALU.mult))
            mean = xbar[:, 0].unsqueeze(3)
            nc.vector.tensor_tensor(text(xc), text(xT[1]), mean.to_broadcast([HC, 2, 2, NTXT]), ALU.subtract)
            nc.vector.tensor_tensor(images(xc, 64), images(xT[1], 64), mean.to_broadcast([HC, 2, 2, 64]),
                                    ALU.subtract).then_inc(S["xc_ready"], 1)
            dve.wait_ge(S["k_f32", 1], at(r, 1, 1))
            if a is not None:
                dve.wait_ge(S["k_stored", 0], at(a, 16, 16))
            dve_split(ch, k32, ks, S["k_split", 1])
            dve_value(dve, 1, r)
            dve.wait_ge(S["g_psum"], at(r, 1, 1))
            nc.vector.tensor_tensor(gsb[:], PS[0:HC, 2, 0:4 * HC].rearrange("p (i c) -> p i c", i=4),
                                    same_head[:].unsqueeze(1).to_broadcast([HC, 4, HC]), ALU.mult).then_inc(S["g_ready"], 1)
            dve.wait_ge(S["u_psum"], at(r, 1, 1))
            dve.wait_ge(S["k_split", 1], at(r, 1, 1))
            nc.vector.tensor_tensor(rem[:, :, :, 0:T], PS[0:HC, 0:2, 0:T2].rearrange("p h (b j) -> p h b j", b=2),
                                    q32[1][:, :, :, 0:T], ALU.mult).then_inc(S["prod_ready"], 1)

            def query(a):
                dve.wait_ge(S["qf_ready"], at(r, 1, 1))
                ch.link(nc.vector.scalar_tensor_tensor(out=q32[1][:, :, :, 0:T], in0=q32[1][:, :, :, 0:T],
                                                       scalar=chan[:, C_GAMMA:C_GAMMA + 1], in1=rem[:, :, :, 0:T],
                                                       op0=ALU.mult, op1=ALU.mult))
                if a is not None:
                    dve.wait_ge(S["q_stored", 0], at(a, 16, 16))
                dve_split(ch, q32[1], qs, S["q_split", 1])
                ch.end()
            return query

        def dve_max_pass(dve, s, r, moe):
            for u in range(HH):
                for g in range(3):
                    dve.wait_ge(S["s_psum", s], at(r, 3 * HH, 3 * u + g + 1))
                    out = mx[:, 0:2, 2 * u + g] if g < 2 else mx[:, 2, 2 * u:2 * u + 2]
                    nc.vector.tensor_reduce(out, PS[:, g, 0:T2].rearrange("p (b j) -> p b j", b=2), AX.X, ALU.max)\
                        .then_inc(S["s_used", s], 1)
                moe.units(FILL["max", s][u])
            ch = chain(dve, f"dve_max{s}", r)
            dve.wait_ge(S["s_used", s], at(r, 3 * HH, 3 * HH))
            ch.link(nc.vector.tensor_scalar(mneg[:], mx[:], -1.0, None, ALU.mult))
            for c in range(3):
                ch.link(nc.vector.tensor_copy(mbf[:], mneg[:]))
                ins = nc.vector.tensor_copy(mpart[:, :, c, :], mbf[:])
                if c < 2:
                    ch.link(ins)
                    ch.link(nc.vector.tensor_tensor(mneg[:], mneg[:], mbf[:], ALU.subtract))
            ins.then_inc(S["m_split", s], 1)
            ch.end()

        def dve_out(dve, s, r, moe):
            ch = chain(dve, f"dve_out{s}", r)
            dve.wait_ge(S["oT_psum", s], at(r, 1, 1))
            o = PS[:, 0:3, 0:384].rearrange("p i (h c) -> p i h c", c=32)
            ch.link(nc.vector.reciprocal(rs[:].unsqueeze(3), o[:, :, :, HD:HD + 1]))
            nc.vector.tensor_tensor(on[:].rearrange("p i (h d) -> p i h d", d=HD), o[:, :, :, 0:HD],
                                    rs[:].unsqueeze(3).to_broadcast([128, 3, HEADS, HD]), ALU.mult)\
                .then_inc(S["on_ready", s], 1)
            moe.units(FILL["turn", s])
            moe.units(FILL["back", s])
            dve.wait_ge(S["pr_psum", s], at(r, 1, 1))
            out, res, bo = (x2, xn[1], R_BO) if s else (h1, h0, R_BP)
            if s == 0 and not (isinstance(r, int) and r == 0):
                dve.wait_ge(S["h1_kept"], at(r, 1, 0))
            for i, (lo, hi) in enumerate(((0, 2), (2, 3))):
                src = PS[:, (2, 3)[i], 0:(hi - lo) * D].rearrange("p (i d) -> p i d", d=D)
                ins = nc.vector.tensor_tensor(out[:, lo:hi, :], src, row(bo, hi - lo), ALU.add)
            ins.then_inc(S["pr_read", s], 1)
            dve.wait_ge(S["pr_read", s], at(r, 1, 1))
            nc.vector.tensor_tensor(out[:], out[:], res[:], ALU.add).then_inc(S["res_ready", s], 1)
            ch.end()

        def dve_gate(dve, b, ch):
            dve.wait_ge(S["gate_psum"], at(b, 1, 1))
            nc.vector.tensor_tensor(gl[:], PS[:, 2, 0:3 * E].rearrange("p (i e) -> p i e", e=E),
                                    bg[:].unsqueeze(1).to_broadcast([128, 3, E]), ALU.add).then_inc(S["gate_used"], 1)
            dve.wait_ge(S["gate_used"], at(b, 1, 1))
            ch.link(nc.vector.tensor_reduce(gs[:, :, 0], gl[:], AX.X, ALU.max))
            nc.vector.tensor_tensor(gl[:], gl[:], gs[:, :, 0:1].to_broadcast([128, 3, E]), ALU.subtract)\
                .then_inc(S["gl_ready"], 1)
            dve.wait_ge(S["ge_ready"], at(b, 1, 1))
            ch.link(nc.vector.tensor_reduce(gs[:, :, 0], gl[:], AX.X, ALU.add))
            ch.link(nc.vector.reciprocal(gs[:, :, 1], gs[:, :, 0]))
            ch.link(nc.vector.tensor_tensor(gl[:], gl[:], gs[:, :, 1:2].to_broadcast([128, 3, E]), ALU.mult))
            mine, other = gl[:].unsqueeze(3).to_broadcast([128, 3, E, E]), gl[:].unsqueeze(2).to_broadcast([128, 3, E, E])
            ch.link(nc.vector.tensor_tensor(cmp1[:], other, mine, ALU.is_gt))
            ch.link(nc.vector.tensor_tensor(cmp2[:], other, mine, ALU.is_equal))
            ch.link(nc.vector.tensor_tensor(cmp2[:], cmp2[:],
                                            lower[:].rearrange("p (i e) -> p i e", e=E).unsqueeze(1).to_broadcast([128, 3, E, E]),
                                            ALU.mult))
            ch.link(nc.vector.tensor_tensor(cmp1[:], cmp1[:], cmp2[:], ALU.add))
            ch.link(nc.vector.tensor_reduce(comb[:], cmp1[:], AX.X, ALU.add))
            ch.link(nc.vector.tensor_scalar(comb[:], comb[:], 1.5, None, ALU.is_lt))
            nc.vector.tensor_tensor(comb[:], comb[:], gl[:], ALU.mult).then_inc(S["comb_ready"], 1)
            ch.end()

        def dve_round(dve, a, b, nxt, m):
            moe = moe_of(MoeDve, dve, m)
            moe.units(FILL["start"])
            if b is not None:
                query = dve_front1(dve, b, a)
                for k in ("norm", "query", "key", "value", "kc", "g", "u", "ss"):
                    moe.units(FILL[k])
            if a is not None:
                dve_max_pass(dve, 0, a, moe)
                moe.units(FILL["split", 0])
            if b is not None:
                query(a)
            if a is not None:
                moe.units(FILL["rows", 0])
                for u in range(HH):
                    moe.units(FILL["exp", 0][u])
                moe.units(FILL["out", 0])
            if b is not None:
                dve_max_pass(dve, 1, b, moe)
                moe.units(FILL["split", 1])
            if a is not None:
                dve_out(dve, 0, a, moe)
                moe.units(FILL["rows", 1])
            if b is not None:
                for u in range(HH):
                    moe.units(FILL["exp", 1][u])
                moe.units(FILL["out", 1])
            if nxt is not None:
                splits = dve_front0(dve, nxt)
            if b is not None:
                dve_out(dve, 1, b, moe)
            moe.units(UNITS)
            moe.finish()
            if nxt is not None:
                splits(b)
            if b is not None:
                ch = chain(dve, "dve_x2", b)
                dve.wait_ge(S["res_ready", 1], at(b, 1, 1))
                dve_norm(dve, ch, x2, x2, S["x2_var"], S["x2_r0"], b, S["x2_ready"], R_L1G)
            if nxt is not None:
                dve_value(dve, 0, nxt)
            if b is not None:
                dve_gate(dve, b, ch)


        def image(r):
            nc.gpsimd.tensor_copy(h0[:, 2, :], img_tok[:, r, :]).then_inc(S["img_in"], 1)

        def pool_biases(pool, m):
            pool.wait_ge(S["comb_ready"], at(m, 1, 1))
            pool.wait_ge(S["stored"], at(m, 80, 1))
            ch = chain(pool, "pool_moe", m)
            for e in range(E):
                b2e = rows[:, R_B2 + e:R_B2 + e + 1, :].to_broadcast([128, 3, D])
                c = comb[:, :, e:e + 1].to_broadcast([128, 3, D])
                ch.link(nc.gpsimd.tensor_tensor(fin[:], b2e, c, ALU.mult))
                ins = nc.gpsimd.tensor_tensor(acc[:], acc[:] if e else x2[:], fin[:], ALU.add)
                if e < E - 1:
                    ch.link(ins)
            ins.then_inc(S["b2_ready"], 1)
            ch.end()

        def pool_round(pool, a, b, nxt, m):
            if m is not None:
                pool_biases(pool, m)
                pool.wait_ge(S["h1_kept"], at(m, 1, 1))
                plain_wait(pool)
                nc.gpsimd.tensor_copy(h1_fin[:], h1_keep[:]).then_inc(S["fin_h1"], 1)
            if b is not None:
                pool.wait_ge(S["res_ready", 0], at(b, 1, 1))
                if m is not None:
                    pool.wait_ge(S["fin_h1"], at(m, 1, 1))
                plain_wait(pool)
                nc.gpsimd.tensor_copy(h1_keep[:], h1[:]).then_inc(S["h1_kept"], 1)
            if nxt is not None:
                pool.wait_ge(S["res_ready", 0], at(a, 1, 1))
                plain_wait(pool)
                image(nxt)


        def load_text(sp, r):
            for b in range(2):
                sp.dma_start(h0[:, b, :], a["txt"][r, b]).then_inc(S["txt_in"], 16)

        def stack(sp, s, r, which):
            x, scr, st = (qs, scr_q[s], qst[s]) if which == "q" else (ks, scr_k[s], kst[s])
            sp.wait_ge(S[f"{which}_split", s], at(r, 1, 1))
            sp.dma_start(scr.rearrange("h c d (g j) -> (d g) h c j", g=HH), x[:]).then_inc(S[f"{which}_stored", s], 16)
            sp.wait_ge(S[f"{which}_stored", s], at(r, 16, 16))
            for t, c, n in K_RUNS if which == "k" else Q_RUNS:
                sp.dma_start(st[HD * t:HD * (t + n), :, :].rearrange("p (h g) j -> p h (g j)", h=2),
                             scr[:, c:c + n].rearrange("h c d x -> (c d) h x")).then_inc(S[f"{which}_stacked", s], 16)

        def stack_max(sp, s, r):
            sp.wait_ge(S["m_rows", s], at(r, 1, 1))
            for c in range(3):
                sp.dma_start(qst[s][SROWS + c:SROWS + c + 1, :, :], mrows[HEADS * c:HEADS * c + HEADS, :])\
                    .then_inc(S["m_stacked", s], 16)

        def store_pair(sp, m):
            sp.wait_ge(S["fin_ready"], at(m, 1, 1))
            out = a["out"][m]
            sp.dma_start(out[:, NB:T, :].rearrange("b t d -> t b d"), fin[:, 0:2, :]).then_inc(S["stored"], 16)
            for b in range(2):
                sp.dma_start(out[b, 1:NB, :], fin[64 * b:64 * b + NI, 2, :]).then_inc(S["stored"], 16)
                sp.dma_start(out[b, 0:1, :], fin[64 * b + NI:64 * b + NB, 2, :]).then_inc(S["stored"], 16)

        def sp_round(sp, a, b, nxt, m):
            if b is not None:
                stack(sp, 1, b, "k")
            if a is not None:
                stack_max(sp, 0, a)
            if b is not None:
                stack(sp, 1, b, "q")
                stack_max(sp, 1, b)
            if nxt is not None:
                sp.wait_ge(S["res_ready", 0], at(a, 1, 1))
                load_text(sp, nxt)
                stack(sp, 0, nxt, "q")
                stack(sp, 0, nxt, "k")
            if m is not None:
                store_pair(sp, m)

        def rounds(eng, one_round):
            one_round(eng, 0, None, 1, None)
            one_round(eng, 1, 0, 2, None)
            with eng.Fori(1, PAIRS - 2) as p:
                one_round(eng, p + 1, p, p + 2, p - 1)
            one_round(eng, PAIRS - 1, PAIRS - 2, None, PAIRS - 3)
            one_round(eng, None, PAIRS - 1, None, PAIRS - 2)
            one_round(eng, None, None, None, PAIRS - 1)

        with nc.Block() as block:
            @block.sync
            def _(sp):
                sp.wait_ge(S["preset"], 2)
                load_text(sp, 0)
                stack(sp, 0, 0, "q")
                stack(sp, 0, 0, "k")
                rounds(sp, sp_round)
                sp.wait_ge(S["stored"], at(PAIRS, 80, 1))

            @block.tensor
            def _(pe):
                pe.wait_ge(ld_attn, 16)
                pe.wait_ge(ld_moe, 32)
                pe.wait_ge(casts, 1)
                pe.wait_ge(S["preset"], 2)
                pe_turn_in(pe, 0, 0)
                pe_query(pe, 0, 0)
                pe_key(pe, 0, 0)
                pe_value(pe, 0, 0)
                rounds(pe, pe_round)

            @block.scalar
            def _(act):
                act_norm(act, 0, 0)
                act_turn_in(act, 0, 0)
                act_query(act, 0, 0)
                act_key(act, 0, 0, None)
                rounds(act, act_round)

            @block.vector
            def _(dve):
                nc.vector.memset(qs[:], 0.0)
                nc.vector.memset(ks[:], 0.0)
                for s in range(2):
                    ins = nc.vector.memset(va[s][:], 0.0)
                ins.then_inc(casts, 1)
                dve.wait_ge(casts, 2)
                for s in range(2):
                    nc.vector.memset(va[s][:, 0:2, :, HD:HD + 1], 1.0)
                    for b in range(2):
                        nc.vector.memset(va[s][64 * b:64 * b + NB, 2 + b, :, HD:HD + 1], 1.0)
                    nc.vector.memset(kst[s][SROWS:128, :, :], 1.0)
                    ins = nc.vector.memset(qst[s][SROWS:128, :, :], 0.0)
                ins.then_inc(S["preset"], 1)
                nc.vector.memset(rs[:], 0.0).then_inc(S["stored"], 1)
                dve.wait_ge(cls_done, 32)
                splits = dve_front0(dve, 0)
                splits(None)
                dve_value(dve, 0, 0)
                rounds(dve, dve_round)

            @block.gpsimd
            def _(pool):
                nc.gpsimd.memset(kct[:], 0.0)
                nc.gpsimd.memset(osb[:, :, 2 * NTXT:XW], 1.0)
                nc.gpsimd.memset(hid[0][:, XN:XW], 0.0)
                nc.gpsimd.memset(hid[1][:, XN:XW], 0.0).then_inc(S["preset"], 1)
                pool.wait_ge(cls_done, 32)
                image(0)
                rounds(pool, pool_round)



def _haar():
    isq2 = float(np.float32(0.7071067811865476))
    f = np.arange(256)
    y, x = np.divmod(np.arange(256), 16)
    h = np.full((256, 256), isq2 ** 8)
    for level in range(4):
        digit = (f >> (2 * (3 - level))) & 3
        w_hi, h_hi = digit >> 1, digit & 1
        h = h * np.where((w_hi[:, None] & (x[None] >> level) & 1) == 1, -1.0, 1.0)
        h = h * np.where((h_hi[:, None] & (y[None] >> level) & 1) == 1, -1.0, 1.0)
    return h.astype(np.float32)


def _layout(i):
    f = {k: np.asarray(v) for k, v in i.items()}

    def halves(v):
        return np.reshape(v, (2, HC)).T

    def chunk(m, r=HC):
        return np.reshape(m, (-1, r, m.shape[-1])).transpose(1, 0, 2)

    turn = np.arange(D).reshape(2, HH, HD).transpose(0, 2, 1).reshape(-1)
    o = {}
    o["x_cols"] = chunk(f["x"].reshape(B, CIN, G7, PATCH, G7, PATCH).transpose(1, 3, 5, 0, 2, 4).reshape(-1, NPOS), 128)
    o["pl_cols"] = chunk(f["L0_tok_pl_w"].reshape(D, -1).T, 128)
    o["pg_bands"] = chunk(f["L0_tok_pg_w1"].reshape(D, 256, CIN).transpose(2, 1, 0).reshape(-1, D), 128)
    o["haar"] = chunk(_haar(), 128)
    o["ident"] = np.eye(128, dtype=np.float32)
    t = {}
    chan = np.zeros((HC, NCH), np.float32)
    scale = np.repeat(f["L0_attn_scale"], HD)
    bqkv = f["L0_attn_b_qkv"].reshape(3, D)
    for c, v in ((C_PLB, f["L0_tok_pl_b"]), (C_PGB, f["L0_tok_pg_b1"]), (C_PLP, f["L0_tok_pl_pwb"]),
                 (C_PGP, f["L0_tok_pg_pwb"]), (C_PGB2, f["L0_tok_pg_b2"]), (C_ALPHA, f["L0_tok_alpha"].reshape(D)),
                 (C_F1, f["L0_tok_f1_pwb"]), (C_F2, f["L0_tok_f2_pwb"]), (C_BQ, bqkv[0][turn]), (C_BK, bqkv[1][turn]),
                 (C_SCALE, scale[turn]), (C_FBQ, f["L0_ffn_bq"][turn]),
                 (C_GAMMA, np.broadcast_to(f["L0_ffn_gamma"], (D,)))):
        chan[:, c:c + 2] = halves(v)
    for r, name in enumerate(("pl", "pg", "f1", "f2", "f3")):
        w = f[f"L0_tok_{name}_dw"].reshape(2, HC, 9).transpose(1, 0, 2).reshape(HC, 18)
        chan[:, C_DW + 18 * r:C_DW + 18 * r + 18] = w
    o["chan"] = chan
    pws = [f[f"L0_tok_{n}_pw"].reshape(D, D).T for n in ("pl", "pg", "f1", "f2", "f3")] + [f["L0_tok_pg_w2"].reshape(D, D).T]
    o["w_pw"] = np.stack([chunk(w) for w in pws], 1)
    wqkv = f["L0_attn_w_qkv"]
    ws = [wqkv[:, 0:D][:, turn], wqkv[:, D:2 * D][:, turn], wqkv[:, 2 * D:], f["L0_attn_w_proj"],
          f["L0_ffn_Wq"].T[:, turn], f["L0_ffn_Wk"].T[:, turn], f["L0_ffn_Wv"].T, f["L0_ffn_Wo"].T]
    o["w_at"] = np.stack([chunk(w) for w in ws], 1)
    rows = [f["L0_tok_f3_pwb"], f["L0_tok_ln_g"], f["L0_tok_ln_b"]]
    o["tok_rows"] = np.broadcast_to(np.stack(rows)[None], (128, 3, D))
    rows = [bqkv[2], f["L0_attn_b_proj"], f["L0_ffn_bv"],
            f["L0_ffn_bo"], f["L0_ffn_ln1_g"], f["L0_ffn_ln1_b"], f["L0_ffn_ln2_g"], f["L0_ffn_ln2_b"], *f["L0_ffn_b2"]]
    o["rows"] = np.broadcast_to(np.stack(rows)[None], (128, NROW, D))
    masks = np.zeros((128, 2, 2, T), np.float32)
    for j in range(128):
        masks[j, 0, :, j] = BIG
    for b in range(2):
        for j in range(NI):
            masks[64 * b + j, 1, :, NTXT + j] = BIG
    o["masks"] = masks.reshape(128, 2, T2)
    head = np.arange(HC) % HH
    o["same_head"] = (head[:, None] == head[None]).astype(np.float32)
    low = np.tril(np.ones((E, E), np.float32), -1)
    o["lower"] = np.broadcast_to(low.reshape(1, -1), (128, E * E))
    o["bg"] = np.broadcast_to(f["L0_ffn_bg"][None], (128, E))
    o["gate_w"] = chunk(f["L0_ffn_Wg"].T)
    o["b1"] = f["L0_ffn_b1"].reshape(UNITS, 128).T
    o["w1"] = chunk(f["L0_ffn_W1"].transpose(1, 0, 2).reshape(D, E * FF))
    o["w2"] = chunk(f["L0_ffn_W2"].reshape(E * FF, D), 128)
    o["cls8"] = np.broadcast_to(f["L0_tok_cls"].reshape(1, 1, D), (1, PAIRS, D))
    o["txt"] = f["txt"].reshape(PAIRS, 2, NTXT, D)
    return {k: np.ascontiguousarray(v) for k, v in o.items()}


def kernel(**inputs):
    import concourse.bacc as _bacc
    from concourse.bass_utils import run_bass_kernel_spmd as _run

    nc = _bacc.Bacc("TRN2", target_bir_lowering=False, num_devices=1)
    arrays = _layout(inputs)
    aps = {k: nc.dram_tensor(f"in_{k}", v.shape, F32, kind="ExternalInput").ap() for k, v in arrays.items()}
    aps["out"] = nc.dram_tensor("out", (PAIRS, 2, T, D), F32, kind="ExternalOutput").ap()
    build(nc, aps)
    r = _run(nc, [{f"in_{k}": v for k, v in arrays.items()}], core_ids=[0])
    return r.results[0]["out"].reshape(B, T, D)
```

```python
from contextlib import ExitStack

import numpy as np
import concourse.bass as bass
from concourse import mybir

F32 = mybir.dt.float32
BF16 = mybir.dt.bfloat16
I32 = mybir.dt.int32
ALU = mybir.AluOpType
ACT = mybir.ActivationFunctionType
AX = mybir.AxisListType

B, D, HEADS, HD = 16, 192, 12, 16
HC = D // 2
HH = HEADS // 2
IMG, PATCH, CIN = 112, 16, 3
G7 = IMG // PATCH
NI = G7 * G7
NTXT = 128
NB = NI + 1
T = NTXT + NB
T2 = 2 * T
TP = NTXT + 64
PAIRS = B // 2
KC = CIN * PATCH * PATCH // 128
NPOS = B * NI
NH = NPOS // 2
PITCH = G7 + 1
CELLS = B * PITCH * PITCH
GUARD = 16
E, FF = 4, 768
FT = FF // 128
UNITS = E * FT
MOE_STEPS = 2 * UNITS + 1
TERMS = 6
SROWS = TERMS * HD
XW = 3 * 128
XN = 2 * NTXT + 64 + NB
BIG = -1.0e30
EPS = 1e-5
ROOT_GUESS = 0x5f3759df
NCONV = 5
PE_TAP0 = 2

(C_PLB, C_PGB, C_PLP, C_PGP, C_PGB2, C_ALPHA, C_F1, C_F2, C_BQ, C_BK, C_SCALE, C_FBQ, C_GAMMA) = range(0, 26, 2)
C_DW = 26
NCH = C_DW + NCONV * 2 * 9
(R_BV, R_BP, R_FBV, R_BO, R_L1G, R_L1B, R_L2G, R_L2B, R_B2) = range(9)
NROW = R_B2 + E
Q_RUNS = ((0, 0, 1), (1, 0, 1), (2, 0, 1), (3, 1, 1), (4, 1, 1), (5, 2, 1))
K_RUNS = ((0, 0, 3), (3, 0, 2), (5, 0, 1))

PROB_UNITS = 4

CHAIN_STEPS = {"dve_tok": 16, "dve_front0": 20, "dve_front1": 10, "dve_norm1": 14, "dve_max0": 8, "dve_max1": 8,
               "dve_out0": 1, "dve_out1": 1, "dve_x2": 26, "dve_moe": 17, "act_deviation": 2, "dve_bias": 4}
FILL = {
    "start": 4, "norm": 1, "query": 4, "key": 3, "value": 0, "kc": 2, "g": 2, "u": 1, "ss": 2,
    ("max", 0): (0, 0, 0, 0, 0, 0), ("split", 0): 2, ("rows", 0): 4, ("exp", 0): (0, 0, 0, 0, 0, 0), ("out", 0): 0,
    ("max", 1): (0, 0, 0, 0, 0, 0), ("split", 1): 2, ("turn", 0): 2, ("back", 0): 1, ("rows", 1): 1,
    ("exp", 1): (1, 0, 1, 1, 0, 2), ("out", 1): 0, ("turn", 1): 2, ("back", 1): 1, "next turn": 0, "next norm": 3,
    "next query": 2,
}
FILL_A7 = {
    "start": 4, "norm": 4, "query": 4, "key": 0, "value": 0, "kc": 1, "g": 2, "u": 1, "ss": 2,
    ("max", 0): (0, 1, 0, 0, 0, 0), ("split", 0): 2, ("rows", 0): 4, ("exp", 0): (1, 0, 0, 0, 0, 0), ("out", 0): 0,
    ("max", 1): (0, 0, 1, 0, 0, 0), ("split", 1): 2, ("turn", 0): 2, ("back", 0): 1, ("rows", 1): 0,
    ("exp", 1): (1, 2, 0, 0, 0, 1), ("out", 1): 1, ("turn", 1): 2, ("back", 1): 0, "next turn": 0, "next norm": 4,
    "next query": 2,
}
FILL_B7 = {
    "start": 4, "norm": 1, "query": 3, "key": 4, "value": 0, "kc": 2, "g": 0, "u": 2, "ss": 14,
    ("max", 0): (0, 0, 0, 1, 1, 0), ("split", 0): 0, ("rows", 0): 0, ("exp", 0): (0, 0, 0, 0, 0, 0), ("out", 0): 1,
    ("max", 1): (0, 0, 0, 0, 0, 0), ("split", 1): 1, ("turn", 0): 1, ("back", 0): 2, ("rows", 1): 4,
    ("exp", 1): (1, 2, 0, 0, 0, 2), ("out", 1): 1, ("turn", 1): 2, ("back", 1): 0, "next turn": 0, "next norm": 3,
    "next query": 2,
}


class Chain:

    def __init__(self, eng, sem, per_round, this_round):
        self.eng, self.sem, self.per, self.base, self.n = eng, sem, per_round, this_round * per_round, 0

    def link(self, ins):
        self.n += 1
        ins.then_inc(self.sem, 1)
        self.eng.wait_ge(self.sem, self.base + self.n)

    def end(self):
        assert self.n == self.per, (self.sem, self.n, self.per)


def build(nc, a):
    ctx = ExitStack()
    with ctx:
        def sb(name, shape, dt=F32):
            return ctx.enter_context(nc.sbuf_tensor(name, shape, dt))

        sems = {}

        def sem(name):
            sems[name] = ctx.enter_context(nc.semaphore(name))
            return sems[name]

        def root(ch, sc):
            bits = sc.bitcast(I32)
            nc.vector.tensor_scalar(sc[:, 3, :], sc[:, 0, :], -0.5, None, ALU.mult)
            ch.link(nc.vector.tensor_scalar(bits[:, 1, :], bits[:, 0, :], 1, None, ALU.logical_shift_right))
            ch.link(nc.vector.tensor_scalar(bits[:, 2, :], bits[:, 1, :], -1, ROOT_GUESS, ALU.mult, ALU.add))
            for _ in range(3):
                ch.link(nc.vector.tensor_tensor(sc[:, 1, :], sc[:, 2, :], sc[:, 2, :], ALU.mult))
                ch.link(nc.vector.tensor_tensor(sc[:, 1, :], sc[:, 1, :], sc[:, 3, :], ALU.mult))
                ch.link(nc.vector.scalar_tensor_tensor(out=sc[:, 2, :], in0=sc[:, 1, :], scalar=1.5, in1=sc[:, 2, :],
                                                       op0=ALU.add, op1=ALU.mult))

        ident = sb("ident", [128, 128])
        ident_bf = sb("ident_bf", [128, 128], BF16)
        masks = sb("masks", [128, T2], BF16)
        same_head = sb("same_head", [HC, HC])
        lower = sb("lower", [128, E * E])
        chan = sb("chan", [HC, NCH])
        rows = sb("rows", [128, NROW, D])
        bg = sb("bg", [128, E])
        gate_w = sb("gate_w", [HC, 2, E])
        b1 = sb("b1", [128, UNITS])
        w_at = sb("w_at", [HC, 8, 2, D])
        w1 = sb("w1", [HC, 2, E * FF])
        w2 = sb("w2", [128, UNITS, D])
        gate = sb("gate", [HC, 2])
        qbias = sb("qbias", [HC, 2])
        tok_gain = sb("tok_gain", [128, 2, D])
        img_tok = sb("img_tok", [128, PAIRS, D])
        tstat = sb("tstat", [128, PAIRS, 6])
        tmv = sb("tmv", [128, PAIRS, 2])
        tsc = sb("tsc", [128, 4, PAIRS])
        kst = [sb(f"kst{s}", [128, HEADS, 2 * TP], BF16) for s in range(2)]
        va = [sb(f"va{s}", [128, 4, HEADS, 32]) for s in range(2)]

        PS = ctx.enter_context(nc.psum_tensor("PS", [128, 8, 512], F32))
        scr_q = [nc.dram_tensor(f"scr_q{s}", (2, 3, HD, HH * 2 * TP), BF16).ap() for s in range(2)]
        scr_k = [nc.dram_tensor(f"scr_k{s}", (2, 3, HD, HH * 2 * TP), BF16).ap() for s in range(2)]

        ld_haar, ld_cw, ld_const, ld_tok, ld_attn, ld_moe = (
            sem(n) for n in ("ld_haar", "ld_cw", "ld_const", "ld_tok", "ld_attn", "ld_moe"))
        ld_x = [sem(f"ld_x{k}") for k in range(KC)]
        casts = sem("casts")

        with ExitStack() as tk:
            def tsb(name, shape, dt=F32):
                return tk.enter_context(nc.sbuf_tensor(name, shape, dt))

            def tsem(name):
                return ctx.enter_context(nc.semaphore(name))

            masks_f = tsb("masks_f", [128, T2])
            f3_bias = tsb("f3_bias", [128, 1, D])
            cols = tsb("cols", [128, KC, NPOS])
            cw = tsb("cw", [128, KC, 2 * D])
            tap = cw[0:HC].rearrange("p k d -> p (k d)")[:, 0:2 * CELLS].rearrange("p (t c) -> p t c", t=2)
            bands = tsb("bands", [128, KC, D])
            haar = tsb("haar", [128, 2, 256])
            w_pw = tsb("w_pw", [HC, NCONV + 1, 2, D])
            diag = tsb("diag", [HC, NCONV * (9 - PE_TAP0), HC])
            pad_l = tsb("pad_l", [HC, 2, CELLS + 2 * GUARD])
            pad_g = tsb("pad_g", [HC, 2, CELLS + 2 * GUARD])
            dwo = tsb("dwo", [HC, 2, CELLS])
            flat = tsb("flat", [HC, 2, NPOS + 16])
            loc = tsb("loc", [HC, 2, NPOS])
            mid = tsb("mid", [HC, 2, NPOS])

            haar_psum, haar_ready, conv_psum, zeroed, diag_ready = (
                tsem(n) for n in ("haar_psum", "haar_ready", "conv_psum", "zeroed", "diag_ready"))
            pad_ready, taps_ready, taps_added, dw_ready, dw_psum, pw_psum = (
                tsem(n) for n in ("pad_ready", "taps_ready", "taps_added", "dw_ready", "dw_psum", "pw_psum"))
            loc_ready, gg_ready, glob_psum, gate_ready, f2_relu, flat_ready, f3_psum, tdve = (
                tsem(n) for n in ("loc_ready", "gg_ready", "glob_psum", "gate_ready", "f2_relu", "flat_ready", "f3_psum",
                                  "tdve"))

            def cells(t, lo, n):
                v = t[:, lo:lo + n * PITCH * PITCH].rearrange("p (b y x) -> p b y x", y=PITCH, x=PITCH)
                return v[:, :, 0:G7, 0:G7]

            def inner(pad, h, n):
                return cells(pad[:, h, :], GUARD + n * CELLS // 2, B // 2)

            def tap_offset(tap):
                return GUARD + (tap // 3 - 1) * PITCH + tap % 3 - 1

            def image_rows(t, lo, n):
                lo += n * CELLS // 2
                return t[:, lo:lo + CELLS // 2].rearrange("p (r x) -> p r x", x=PITCH)[:, 0:CELLS // 2 // PITCH - 1, 0:G7]

            def step(r, n):
                return 2 * r + n + 1

            def grid(flat, n):
                return flat[:, NH * n:NH * n + NH].rearrange("p (b y x) -> p b y x", y=G7, x=G7)

            def col(c, h=0):
                return chan[:, c + h:c + h + 1]

            PAD_OF = [pad_l, pad_g, pad_l, pad_g, pad_l]

            with nc.Block() as block:
                @block.sync
                def _(sp):
                    sp.dma_start(haar[:], a["haar"]).then_inc(ld_haar, 16)
                    sp.dma_start(bands[:], a["pg_bands"]).then_inc(ld_haar, 16)
                    for k in range(KC):
                        sp.dma_start(cols[:, k, :], a["x_cols"][:, k, :]).then_inc(ld_x[k], 16)
                    sp.dma_start(w_at[:], a["w_at"]).then_inc(ld_attn, 16)
                    sp.dma_start(w1[:], a["w1"]).then_inc(ld_moe, 16)
                    sp.dma_start(w2[:], a["w2"]).then_inc(ld_moe, 16)

                @block.scalar
                def _(act):
                    act.dma_start(cw[:, :, 0:D], a["pl_cols"]).then_inc(ld_cw, 16)
                    act.dma_start(chan[:], a["chan"]).then_inc(ld_const, 16)
                    act.dma_start(ident[:], a["ident"]).then_inc(ld_const, 16)
                    act.dma_start(w_pw[:], a["w_pw"]).then_inc(ld_tok, 16)
                    act.dma_start(rows[:], a["rows"]).then_inc(ld_tok, 16)
                    act.dma_start(f3_bias[:], a["f3_bias"]).then_inc(ld_tok, 16)
                    act.dma_start(tok_gain[:], a["tok_gain"]).then_inc(ld_tok, 16)
                    act.dma_start(masks_f[:], a["masks"]).then_inc(ld_tok, 16)
                    act.dma_start(same_head[:], a["same_head"]).then_inc(ld_tok, 16)
                    act.dma_start(lower[:], a["lower"]).then_inc(ld_tok, 16)
                    act.dma_start(bg[:], a["bg"]).then_inc(ld_tok, 16)
                    act.dma_start(gate_w[:], a["gate_w"]).then_inc(ld_tok, 16)
                    act.dma_start(b1[:], a["b1"]).then_inc(ld_tok, 16)
                    act.wait_ge(ld_const, 32)
                    nc.scalar.activation(gate[:], chan[:, C_ALPHA:C_ALPHA + 2], ACT.Tanh).then_inc(gate_ready, 1)
                    act.wait_ge(haar_psum, 1)
                    nc.scalar.copy(cw[:, 0:KC, D:2 * D].rearrange("p (g k) d -> p g k d", k=2),
                                   PS[:, 0:3, 0:2 * D].rearrange("p g (k d) -> p g k d", k=2)).then_inc(haar_ready, 1)
                    act.wait_ge(conv_psum, 1)
                    act.wait_ge(zeroed, 1)
                    for branch, pad, bias in ((0, pad_l, C_PLB), (1, pad_g, C_PGB)):
                        for n in range(2):
                            for h in range(2):
                                ins = nc.scalar.activation(inner(pad, h, n), grid(PS[0:HC, 4 * branch + 2 * h + n, :], 0),
                                                           ACT.Gelu, bias=col(bias, h))
                            ins.then_inc(pad_ready, 1)

                    def first_taps(r, n):
                        act.wait_ge(pad_ready, step(r, n))
                        if r:
                            act.wait_ge(pw_psum, step(r - 1, n))
                        for h, t, out in ((0, 0, dwo[:, 0, :]), (1, 0, dwo[:, 1, :]),
                                          *((1, t, tap[:, t - 1, :]) for t in range(1, PE_TAP0))):
                            ins = nc.scalar.activation(image_rows(out, 0, n), image_rows(PAD_OF[r][:, h, :], tap_offset(t), n),
                                                       ACT.Identity, scale=col(C_DW + 18 * r + 9 * h + t))
                        ins.then_inc(taps_ready, 1)

                    def evac_pw(r, out, func, bias, done, taps_next=False):
                        for n in range(2):
                            act.wait_ge(pw_psum, step(r, n))
                            for h in range(2):
                                ins = nc.scalar.activation(out(h, n), grid(PS[0:HC, 2 + 2 * h + n, :], 0), func,
                                                           bias=col(bias, h))
                            ins.then_inc(done, 1)
                            if taps_next:
                                first_taps(r + 1, n)

                    for n in range(2):
                        first_taps(0, n)

                    evac_pw(0, lambda h, n: grid(loc[:, h, :], n), ACT.Identity, C_PLP, loc_ready, True)
                    evac_pw(1, lambda h, n: grid(mid[:, h, :], n), ACT.Gelu, C_PGP, gg_ready)
                    for n in range(2):
                        first_taps(2, n)
                    evac_pw(2, lambda h, n: inner(pad_g, h, n), ACT.Relu, C_F1, pad_ready, True)
                    evac_pw(3, lambda h, n: grid(mid[:, h, :], n), ACT.Relu, C_F2, f2_relu, True)
                    for n in range(2):
                        act.wait_ge(dw_ready, step(NCONV - 1, n))
                        nc.scalar.copy(grid(flat[:, 0, :], n), cells(dwo[:, 0, :], n * CELLS // 2, B // 2)).then_inc(flat_ready, 1)

                @block.gpsimd
                def _(pool):
                    nc.gpsimd.memset(pad_l[:], 0.0)
                    nc.gpsimd.memset(pad_g[:], 0.0)
                    nc.gpsimd.memset(flat[:, :, NPOS:NPOS + 16], 0.0).then_inc(zeroed, 1)
                    pool.wait_ge(ld_const, 32)
                    for r in range(NCONV):
                        for t in range(PE_TAP0, 9):
                            ins = nc.gpsimd.tensor_scalar(diag[:, (9 - PE_TAP0) * r + t - PE_TAP0, :], ident[0:HC, 0:HC],
                                                          col(C_DW + 18 * r + 9 + t), None, ALU.mult)
                        ins.then_inc(diag_ready, 1)
                    for r in range(NCONV):
                        for n in range(2):
                            pool.wait_ge(taps_ready, step(r, n))
                            for t in range(1, PE_TAP0):
                                out = image_rows(dwo[:, 1, :], 0, n)
                                nc.gpsimd.tensor_tensor(out, out, image_rows(tap[:, t - 1, :], 0, n), ALU.add)\
                                    .then_inc(taps_added, 1)
                                pool.wait_ge(taps_added, (PE_TAP0 - 1) * (step(r, n) - 1) + t)

                @block.vector
                def _(dve):
                    ch = Chain(dve, tdve, 0, 0)
                    for s in range(2):
                        nc.vector.memset(kst[s][SROWS:128, :, :], 1.0)
                        ins = nc.vector.memset(va[s][:], 0.0)
                    ch.link(ins)
                    for s in range(2):
                        nc.vector.memset(va[s][:, 0:2, :, HD:HD + 1], 1.0)
                        for b in range(2):
                            nc.vector.memset(va[s][64 * b:64 * b + NB, 2 + b, :, HD:HD + 1], 1.0)
                    dve.wait_ge(ld_tok, 10 * 16)
                    nc.vector.tensor_copy(masks[:], masks_f[:])
                    dve.wait_ge(ld_const, 32)
                    nc.vector.tensor_copy(ident_bf[:], ident[:]).then_inc(casts, 1)
                    dve.wait_ge(gate_ready, 1)
                    ch.link(nc.vector.tensor_scalar(gate[:], gate[:], 1.0, 0.5, ALU.add, ALU.mult))
                    ch.link(nc.vector.tensor_tensor(qbias[:], chan[:, C_BQ:C_BQ + 2], chan[:, C_SCALE:C_SCALE + 2], ALU.mult))

                    def depthwise(r, n):
                        dve.wait_ge(taps_ready, step(r, n))
                        out = image_rows(dwo[:, 0, :], 0, n)
                        for t in range(1, 9):
                            ch.link(nc.vector.scalar_tensor_tensor(out=out, in0=image_rows(PAD_OF[r][:, 0, :], tap_offset(t), n),
                                                                   scalar=col(C_DW + 18 * r + t), in1=out,
                                                                   op0=ALU.mult, op1=ALU.add))
                        dve.wait_ge(taps_added, (PE_TAP0 - 1) * step(r, n))
                        dve.wait_ge(dw_psum, step(r, n))
                        mine = cells(dwo[:, 1, :], n * CELLS // 2, B // 2)
                        out = grid(flat[:, 1, :], n) if r == NCONV - 1 else mine
                        nc.vector.tensor_tensor(out, grid(PS[0:HC, n, :], 0), mine, ALU.add).then_inc(dw_ready, 1)

                    def fuse(n):
                        dve.wait_ge(loc_ready, n + 1)
                        dve.wait_ge(glob_psum, n + 1)
                        c = slice(NH * n, NH * n + NH)
                        for h in range(2):
                            ins = nc.vector.scalar_tensor_tensor(out=mid[:, h, c], in0=PS[0:HC, 2 + 2 * h + n, 0:NH],
                                                                 scalar=col(C_PGB2, h), in1=loc[:, h, c],
                                                                 op0=ALU.add, op1=ALU.subtract)
                        ch.link(ins)
                        for h in range(2):
                            ins = nc.vector.tensor_scalar(mid[:, h, c], mid[:, h, c], gate[:, h:h + 1], None, ALU.mult)
                        ch.link(ins)
                        for h in range(2):
                            ins = nc.vector.tensor_tensor(inner(pad_l, h, n), grid(mid[:, h, :], n), grid(loc[:, h, :], n),
                                                          ALU.add)
                        ins.then_inc(pad_ready, 1)

                    for r in range(2):
                        for n in range(2):
                            depthwise(r, n)
                    for n in range(2):
                        fuse(n)
                        depthwise(2, n)
                    for n in range(2):
                        depthwise(3, n)
                    for n in range(2):
                        dve.wait_ge(f2_relu, n + 1)
                        for h in range(2):
                            ins = nc.vector.tensor_tensor(inner(pad_l, h, n), grid(mid[:, h, :], n), grid(loc[:, h, :], n),
                                                          ALU.add)
                        ins.then_inc(pad_ready, 1)
                        depthwise(4, n)
                    dve.wait_ge(f3_psum, 1)
                    ps = PS[:, 4:8, 0:2 * D].rearrange("p g (k d) -> p g k d", k=2)
                    for g in range(4):
                        nc.vector.tensor_tensor(img_tok[:, 2 * g:2 * g + 2, :], ps[:, g], f3_bias[:].to_broadcast([128, 2, D]),
                                                ALU.add)

                @block.tensor
                def _(pe):
                    pe.wait_ge(ld_haar, 32)
                    for c in range(CIN):
                        for m in range(2):
                            for k in range(2):
                                ins = nc.tensor.matmul(PS[:, c, D * m:D * m + D], haar[:, k, 128 * m:128 * m + 128],
                                                       bands[:, 2 * c + k, :], start=(k == 0), stop=(k == 1))
                    ins.then_inc(haar_psum, 1)
                    pe.wait_ge(ld_cw, 16)
                    pe.wait_ge(haar_ready, 1)
                    for k in range(KC):
                        pe.wait_ge(ld_x[k], 16)
                        for m in range(4):
                            for n in range(2):
                                ins = nc.tensor.matmul(PS[0:HC, 2 * m + n, 0:NH], cw[:, k, HC * m:HC * m + HC],
                                                       cols[:, k, NH * n:NH * n + NH], start=(k == 0), stop=(k == KC - 1))
                    ins.then_inc(conv_psum, 1)

                    def depthwise(r, n):
                        pe.wait_ge(pad_ready, step(r, n))
                        pe.wait_ge(diag_ready, r + 1)
                        for t in range(PE_TAP0, 9):
                            ins = nc.tensor.matmul(PS[0:HC, n, 0:NH], diag[:, (9 - PE_TAP0) * r + t - PE_TAP0, :],
                                                   cells(PAD_OF[r][:, 1, :], tap_offset(t) + n * CELLS // 2, B // 2),
                                                   start=(t == PE_TAP0), stop=(t == 8))
                        ins.then_inc(dw_psum, 1)

                    def pointwise(w, n, src, done):
                        for m in range(2):
                            for k in range(2):
                                ins = nc.tensor.matmul(PS[0:HC, 2 + 2 * m + n, 0:NH], w_pw[:, w, k, HC * m:HC * m + HC],
                                                       src(k), start=(k == 0), stop=(k == 1))
                        ins.then_inc(done, 1)

                    pe.wait_ge(ld_tok, 10 * 16)
                    pe.wait_ge(pad_ready, step(1, 1))

                    def after(r, n):
                        pe.wait_ge(dw_ready, step(r, n))
                        if r == 1:
                            pe.wait_ge(loc_ready, n + 1)
                        pointwise(r, n, lambda k: cells(dwo[:, k, :], n * CELLS // 2, B // 2), pw_psum)

                    def second_global(n):
                        pe.wait_ge(gg_ready, n + 1)
                        pointwise(NCONV, n, lambda k: mid[:, k, NH * n:NH * n + NH], glob_psum)

                    for r in range(NCONV):
                        depthwise(r, 0)
                        if r == 2:
                            second_global(1)
                        if r < NCONV - 1:
                            after(r, 0)
                        depthwise(r, 1)
                        if r == 1:
                            second_global(0)
                        if r < NCONV - 1:
                            after(r, 1)
                    for i in range(B):
                        if i in (0, B // 2 - 1):
                            pe.wait_ge(flat_ready, 1 if i == 0 else 2)
                        q, b = divmod(i, 2)
                        for k in range(2):
                            ins = nc.tensor.matmul(PS[64 * b:64 * b + 64, 4 + q // 2, D * (q % 2):D * (q % 2) + D],
                                                   flat[:, k, NI * i:NI * i + 64], w_pw[:, NCONV - 1, k, :],
                                                   start=(k == 0), stop=(k == 1), skip_group_check=True)
                    ins.then_inc(f3_psum, 1)

        h0 = sb("h0", [128, 3, D])
        h1 = sb("h1", [128, 3, D])
        h1_keep = sb("h1_keep", [128, 3, D])
        h1_fin = sb("h1_fin", [128, 3, D])
        xn = [sb(f"xn{s}", [128, 3, D]) for s in range(2)]
        x2 = sb("x2", [128, 3, D])
        acc = sb("acc", [128, 3, D])
        fin = sb("fin", [128, 3, D])
        stat = sb("stat", [128, 2, 3, 6])
        mv = sb("mv", [128, 2, 3, 2])
        lsc = [sb(f"lsc{i}", [128, 4, 3]) for i in range(2)]
        xT = [sb(f"xT{s}", [HC, 2, XW]) for s in range(2)]
        x2T = sb("x2T", [HC, 2, XW])
        xbar = sb("xbar", [HC, 2, 2, 2])
        q32 = [sb(f"q32{s}", [HC, 2, 2, TP]) for s in range(2)]
        k32 = sb("k32", [HC, 2, 2, TP])
        rem = sb("rem", [HC, 2, 2, TP])
        qs = sb("qs", [HC, 2, 3, 2 * TP], BF16)
        ks = sb("ks", [HC, 2, 3, 2 * TP], BF16)
        qst = [sb(f"qst{s}", [128, HEADS, 2 * TP], BF16) for s in range(2)]
        kct = sb("kct", [128, 4, D])
        gsb = sb("gsb", [HC, 4, HC])
        mx = sb("mx", [128, 3, HEADS])
        mneg = sb("mneg", [128, 3, HEADS])
        mpart = sb("mpart", [128, 3, 3, HEADS])
        mbf = sb("mbf", [128, 3, HEADS], BF16)
        mrows = sb("mrows", [3 * HEADS, 2 * TP], BF16)
        probs = sb("probs", [128, PROB_UNITS, 3, T2])
        osb = sb("osb", [128, 3, XW])
        rs = sb("rs", [128, 3, HEADS])
        on = x2
        oT = sb("oT", [HC, 2, XW])
        xc = oT
        gl = sb("gl", [128, 3, E])
        gs = sb("gs", [128, 3, 2])
        cmp1 = sb("cmp1", [128, 3, E, E])
        cmp2 = sb("cmp2", [128, 3, E, E])
        comb = sb("comb", [128, 3, E])
        hid = [sb(f"hid{i}", [128, XW]) for i in range(2)]

        both = ("xn_ready xT_psum xT_ready q_psum q_f32 k_psum k_f32 v_psum v_ready q_split k_split "
                "q_stored k_stored q_stacked k_stacked s_psum s_used m_split mT_psum m_rows m_stacked e_psum e_done "
                "pv_psum o_ready oT_psum on_ready oc_psum oc_ready pr_psum pr_read res_ready").split()
        S = {(n, s): sem(f"{n}{s}") for n in both for s in range(2)}
        names = ("preset tok_ready txt_in img_in h1_kept xc_ready kc_psum kc_ready g_psum g_ready u_psum prod_ready ss_psum ss_read "
                 "qf_ready x2_ready x2T_psum x2T_ready gate_psum gate_used gl_ready ge_ready comb_ready "
                 "h_psum h_ready h_used y_used fin_ready fin_h1 stored passed").split()
        S.update({n: sem(n) for n in names + list(CHAIN_STEPS)})

        def plain_wait(eng):
            eng.sem_inc(S["passed"], 1)

        def at(n, per, k):
            return n * per + k

        def chain(eng, name, r):
            return Chain(eng, S[name], CHAIN_STEPS[name], r)

        def text(t):
            return t[:, :, 0:2 * NTXT].rearrange("p h (b j) -> p h b j", b=2)

        def images(t, n=NB):
            return t[:, :, 2 * NTXT:XW].rearrange("p h (b j) -> p h b j", b=2)[:, :, :, 0:n]

        def tile_cols(t, half, i):
            return t[:, half, 128 * i:128 * i + 128]

        def tile_psum(banks, i):
            return PS[:, banks[0], D * i:D * i + D] if i < 2 else PS[:, banks[1], 0:D]

        def row(r, n):
            return rows[:, r:r + 1, :].to_broadcast([128, n, D])

        FRONT = ((0, 1), (2, 3))


        class Moe:

            def __init__(self, eng, m, fill):
                self.eng, self.m, self.fill, self.done = eng, m, fill, 0

            def point(self, name, u=None):
                self.steps(self.fill[name] if u is None else self.fill[name][u])

            def steps(self, n):
                for step in range(self.done, min(self.done + n, MOE_STEPS)):
                    self.step(*divmod(step, 2))
                self.done = min(self.done + n, MOE_STEPS)

            def rest(self):
                self.steps(MOE_STEPS)

        class MoePe(Moe):

            def step(self, u, odd):
                pe, m = self.eng, self.m
                if odd:
                    if u:
                        self.second(u - 1)
                elif u == UNITS:
                    self.second(UNITS - 1)
                else:
                    if u >= 2:
                        pe.wait_ge(S["h_ready"], at(m, UNITS, u - 1))
                    for k in range(2):
                        ins = nc.tensor.matmul(PS[:, 4 + u % 2, 0:XN], w1[:, k, 128 * u:128 * u + 128],
                                               x2T[:, k, 0:XN], start=(k == 0), stop=(k == 1))
                    ins.then_inc(S["h_psum"], 1)

            def second(self, u):
                pe, m = self.eng, self.m
                e, j = divmod(u, FT)
                pe.wait_ge(S["h_ready"], at(m, UNITS, u + 1))
                if u and j == 0 or u == 0 and not (isinstance(m, int) and m == 0):
                    pe.wait_ge(S["y_used"], at(m, E, e))
                for i in range(3):
                    ins = nc.tensor.matmul(tile_psum((6, 7), i), hid[u % 2][:, 128 * i:128 * i + 128], w2[:, u, :],
                                           start=(j == 0 and i != 1), stop=(j == FT - 1), skip_group_check=True)
                ins.then_inc(S["h_used"], 1)

        class MoeAct(Moe):

            def step(self, u, odd):
                act, m = self.eng, self.m
                if not odd and u < UNITS:
                    act.wait_ge(S["h_psum"], at(m, UNITS, u + 1))
                    if u >= 2:
                        act.wait_ge(S["h_used"], at(m, UNITS, u - 1))
                    nc.scalar.activation(hid[u % 2][:, 0:XN], PS[:, 4 + u % 2, 0:XN], ACT.Relu,
                                         bias=b1[:, u:u + 1]).then_inc(S["h_ready"], 1)

        class MoeDve(Moe):

            def expert(self, e):
                dve, m = self.eng, self.m
                dve.wait_ge(S["h_used"], at(m, UNITS, FT * (e + 1)))
                for i in range(3):
                    ins = nc.vector.scalar_tensor_tensor(out=acc[:, i, :], in0=tile_psum((6, 7), i),
                                                         scalar=comb[:, i, e:e + 1], in1=acc[:, i, :],
                                                         op0=ALU.mult, op1=ALU.add)
                ins.then_inc(S["y_used"], 1)
                dve.wait_ge(S["y_used"], at(m, E, e + 1))

            def step(self, u, odd):
                if u and u % FT == 0 and (odd or u == UNITS):
                    self.expert(u // FT - 1)

            def start(self):
                dve, m = self.eng, self.m
                ch = chain(dve, "dve_bias", m)
                dve.wait_ge(S["comb_ready"], at(m, 1, 1))
                for e in range(E):
                    for i in range(3):
                        ins = nc.vector.scalar_tensor_tensor(out=acc[:, i, :], in0=rows[:, R_B2 + e, :],
                                                             scalar=comb[:, i, e:e + 1], in1=acc[:, i, :] if e else x2[:, i, :],
                                                             op0=ALU.mult, op1=ALU.add)
                    ch.link(ins)
                ch.end()

            def finish(self):
                dve, m = self.eng, self.m
                ch = chain(dve, "dve_moe", m)
                for i in range(3):
                    ins = nc.vector.bn_stats(stat[:, 1, i, :], acc[:, i, :])
                ch.link(ins)
                plain_wait(dve)
                for i in range(3):
                    ins = nc.vector.bn_aggr(mv[:, 1, i, :], stat[:, 1, i, :])
                ch.link(ins)
                ch.link(nc.vector.tensor_scalar(lsc[1][:, 0, :], mv[:, 1, :, 1], EPS, None, ALU.add))
                root(ch, lsc[1][:])
                dve.wait_ge(S["stored"], at(m, 80, 1))
                for i in range(3):
                    ins = nc.vector.tensor_scalar(fin[:, i, :], acc[:, i, :], mv[:, 1, i, 0:1], lsc[1][:, 2, i:i + 1],
                                                  ALU.subtract, ALU.mult)
                ch.link(ins)
                ch.link(nc.vector.tensor_tensor(fin[:], fin[:], row(R_L2G, 3), ALU.mult))
                ch.link(nc.vector.tensor_tensor(fin[:], fin[:], row(R_L2B, 3), ALU.add))
                dve.wait_ge(S["fin_h1"], at(m, 1, 1))
                nc.vector.tensor_tensor(fin[:], fin[:], h1_fin[:], ALU.add).then_inc(S["fin_ready"], 1)
                ch.end()

        class NoMoe:
            def rest(self):
                pass

            def point(self, name, u=None):
                pass

            def start(self):
                pass

            def finish(self):
                pass

        def moe_of(cls, eng, m, fill):
            return NoMoe() if m is None else cls(eng, m, fill)


        def pe_turn_in(pe, s, r):
            pe.wait_ge(S["xn_ready", s], at(r, 1, 1))
            for h in range(2):
                for i in range(3):
                    ins = nc.tensor.transpose(PS[0:HC, FRONT[s][h], 128 * i:128 * i + 128], xn[s][:, i, HC * h:HC * h + HC],
                                              ident[:])
            ins.then_inc(S["xT_psum", s], 1)

        def pe_project(pe, s, w, x, done):
            for m in range(2):
                for k in range(2):
                    ins = nc.tensor.matmul(PS[0:HC, FRONT[s][m], 0:XN], w_at[:, w, k, HC * m:HC * m + HC], x[:, k, 0:XN],
                                           start=(k == 0), stop=(k == 1))
            ins.then_inc(done, 1)

        def pe_tokens(banks, w, x, done):
            for i in range(3):
                for k in range(2):
                    ins = nc.tensor.matmul(tile_psum(banks, i), tile_cols(x, k, i), w_at[:, w, k, :],
                                           start=(k == 0), stop=(k == 1))
            ins.then_inc(done, 1)

        def pe_query(pe, s, r):
            pe.wait_ge(S["xT_ready", s], at(r, 1, 1))
            pe_project(pe, s, 4 * s, xT[s], S["q_psum", s])

        def pe_key(pe, s, r):
            if s:
                pe.wait_ge(S["xc_ready"], at(r, 1, 1))
            pe.wait_ge(S["q_f32", s], at(r, 1, 1))
            pe_project(pe, s, 4 * s + 1, xc if s else xT[0], S["k_psum", s])

        def pe_value(pe, s, r):
            pe.wait_ge(S["k_f32", s], at(r, 1, 1))
            pe_tokens(FRONT[s], 4 * s + 2, xT[s], S["v_psum", s])

        def pe_logits(pe, s, r, u, rows_, still, move, read, filled):
            for bank in range(3):
                if u:
                    pe.wait_ge(read, at(r, 3 * HH, 3 * u - 2 + bank))
                if bank < 2:
                    h = 2 * u + bank
                    for b in range(2):
                        ins = nc.tensor.matmul(PS[:, bank, T * b:T * b + T], still[0:rows_, h, TP * b:TP * b + NTXT],
                                               move[0:rows_, h, TP * b:TP * b + T], start=(b == 0), stop=(s == 1),
                                               skip_group_check=True)
                else:
                    for g in range(2):
                        for b in range(2):
                            ins = nc.tensor.matmul(PS[64 * b:64 * b + 64, 2, T * g:T * g + T],
                                                   still[0:rows_, 2 * u + g, TP * b + NTXT:TP * b + TP],
                                                   move[0:rows_, 2 * u + g, TP * b:TP * b + T], start=(g == 0),
                                                   stop=(s == 1),
                                                   skip_group_check=True)
                if s == 0:
                    own = PS[:, bank, 0:T2].rearrange("p (b j) -> p b j", b=2)
                    own, m = (own[:, :, 0:NTXT], masks[:, 0:2 * NTXT]) if bank < 2 else (own[:, :, NTXT:T], masks[:, 2 * NTXT:T2])
                    ins = nc.tensor.matmul(own, ident_bf[:], m.rearrange("p (b j) -> p b j", b=2), start=False, stop=True,
                                           skip_group_check=True)
                ins.then_inc(filled, 1)

        def pe_max_pass(pe, s, r, moe):
            pe.wait_ge(S["q_stacked", s], at(r, 16 * len(Q_RUNS), 16 * len(Q_RUNS)))
            pe.wait_ge(S["k_stacked", s], at(r, 16 * len(K_RUNS), 16 * len(K_RUNS)))
            for u in range(HH):
                pe_logits(pe, s, r, u, SROWS, qst[s], kst[s], S["s_used", s], S["s_psum", s])
                moe.point(("max", s), u)

        def pe_max_rows(pe, s, r):
            pe.wait_ge(S["m_split", s], at(r, 1, 1))
            plain_wait(pe)
            for i in range(3):
                src = mpart[:, i, :, :].rearrange("p c h -> p (c h)")
                ins = nc.tensor.transpose(PS[0:3 * HEADS, 3, 128 * i:128 * i + 128], src, ident[:])
            ins.then_inc(S["mT_psum", s], 1)

        def pe_exp_pass(pe, s, r, moe):
            pe.wait_ge(S["s_used", s], at(r, 3 * HH, 3 * HH))
            pe.wait_ge(S["m_stacked", s], at(r, 48, 48))
            for u in range(HH):
                pe_logits(pe, s, r, u, SROWS + 3, kst[s], qst[s], S["e_done", s], S["e_psum", s])
                moe.point(("exp", s), u)
                if u % 2 == 0 and u:
                    pe_values(pe, s, r, u // 2 - 1)
            pe_values(pe, s, r, HH // 2 - 1)

        def pe_values(pe, s, r, g):
            pe.wait_ge(S["e_done", s], at(r, 3 * HH, 6 * g + 6))
            if g:
                pe.wait_ge(S["o_ready", s], at(r, 3, g))
            for b in range(2):
                for i in range(2):
                    for q in range(4):
                        h = 4 * g + q
                        slot = h // 2 % PROB_UNITS
                        pr = probs[:, slot, h % 2, T * b:T * b + T] if i == 0 else \
                            probs[:, slot, 2, T * (h % 2):T * (h % 2) + T]
                        ins = nc.tensor.matmul(PS[32 * q:32 * q + 32, 3, T * b:T * b + T], va[s][:, 2 * i + b, h, :],
                                               pr, start=(i == 0), stop=(i == 1), skip_group_check=True)
            ins.then_inc(S["pv_psum", s], 1)

        def pe_out(pe, s, r, moe):
            pe.wait_ge(S["o_ready", s], at(r, 3, 3))
            for i in range(3):
                for g in range(3):
                    ins = nc.tensor.transpose(PS[:, i, 128 * g:128 * g + 128], osb[:, g, 128 * i:128 * i + 128], ident[:])
            ins.then_inc(S["oT_psum", s], 1)
            moe.point(("turn", s))
            pe.wait_ge(S["on_ready", s], at(r, 1, 1))
            for h in range(2):
                for i in range(3):
                    ins = nc.tensor.transpose(PS[0:HC, h, 128 * i:128 * i + 128], on[:, i, HC * h:HC * h + HC], ident[:])
            ins.then_inc(S["oc_psum", s], 1)
            moe.point(("back", s))
            pe.wait_ge(S["oc_ready", s], at(r, 1, 1))
            pe_tokens((2, 3), 4 * s + 3, oT, S["pr_psum", s])

        def pe_deviation(pe, b, moe):
            pe_tokens((0, 1), 5, xc, S["kc_psum"])
            moe.point("kc")
            pe.wait_ge(S["kc_ready"], at(b, 1, 1))
            pe.wait_ge(S["v_ready", 1], at(b, 1, 1))
            for c in range(2):
                for h in range(2):
                    for i in range(2):
                        x = kct[:, 2 * i + c, HC * h:HC * h + HC]
                        o = HC * (2 * h + c)
                        ins = nc.tensor.matmul(PS[0:HC, 2, o:o + HC], x, x, start=(i == 0), stop=(i == 1))
            ins.then_inc(S["g_psum"], 1)
            moe.point("g")
            pe.wait_ge(S["g_ready"], at(b, 1, 1))
            for h in range(2):
                for c in range(2):
                    ins = nc.tensor.matmul(PS[0:HC, h, T * c:T * c + T], gsb[:, 2 * h + c, :], q32[1][:, h, c, 0:T],
                                           start=True, stop=True)
            ins.then_inc(S["u_psum"], 1)
            moe.point("u")
            pe.wait_ge(S["prod_ready"], at(b, 1, 1))
            for h in range(2):
                ins = nc.tensor.matmul(PS[0:HC, (2, 3)[h], 0:T2], same_head[:], rem[:, h, :, 0:T], start=True, stop=True)
            ins.then_inc(S["ss_psum"], 1)

        def pe_round(pe, a, b, nxt, m, fill):
            moe = moe_of(MoePe, pe, m, fill)
            moe.point("start")
            if b is not None:
                if m is not None:
                    pe.wait_ge(S["gate_used"], at(b, 1, 0))
                pe_turn_in(pe, 1, b)
                moe.point("norm")
                pe_query(pe, 1, b)
                moe.point("query")
                pe_key(pe, 1, b)
                moe.point("key")
                pe_value(pe, 1, b)
                moe.point("value")
                if a is not None:
                    pe.wait_ge(S["v_ready", 0], at(a, 1, 1))
                pe_deviation(pe, b, moe)
                moe.point("ss")
                pe.wait_ge(S["ss_read"], at(b, 1, 1))
            if a is not None:
                if b is None:
                    pe.wait_ge(S["v_ready", 0], at(a, 1, 1))
                pe_max_pass(pe, 0, a, moe)
                moe.point(("split", 0))
                pe_max_rows(pe, 0, a)
                moe.point(("rows", 0))
                pe_exp_pass(pe, 0, a, moe)
                moe.point(("out", 0))
                pe.wait_ge(S["e_done", 0], at(a, 3 * HH, 3 * HH))
            if b is not None:
                pe_max_pass(pe, 1, b, moe)
                moe.point(("split", 1))
                if a is not None:
                    pe.wait_ge(S["o_ready", 0], at(a, 3, 3))
                pe_max_rows(pe, 1, b)
                pe.wait_ge(S["m_rows", 1], at(b, 1, 1))
            if a is not None:
                pe_out(pe, 0, a, moe)
                moe.point(("rows", 1))
                pe.wait_ge(S["pr_read", 0], at(a, 1, 1))
            if b is not None:
                pe_exp_pass(pe, 1, b, moe)
                moe.point(("out", 1))
                pe.wait_ge(S["e_done", 1], at(b, 3 * HH, 3 * HH))
                pe_out(pe, 1, b, moe)
            if nxt is not None:
                pe_turn_in(pe, 0, nxt)
                moe.point("next turn")
                moe.point("next norm")
                pe_query(pe, 0, nxt)
                moe.point("next query")
                pe_key(pe, 0, nxt)
            moe.rest()
            if b is not None:
                pe.wait_ge(S["x2_ready"], at(b, 1, 1))
                for h in range(2):
                    for i in range(3):
                        ins = nc.tensor.transpose(PS[0:HC, (2, 3)[h], 128 * i:128 * i + 128], x2[:, i, HC * h:HC * h + HC],
                                                  ident[:])
                ins.then_inc(S["x2T_psum"], 1)
            if nxt is not None:
                pe_value(pe, 0, nxt)
            if b is not None:
                pe.wait_ge(S["x2T_ready"], at(b, 1, 1))
                for i in range(3):
                    for k in range(2):
                        ins = nc.tensor.matmul(PS[:, 2, E * i:E * i + E], tile_cols(x2T, k, i), gate_w[:, k, :],
                                               start=(k == 0), stop=(k == 1))
                ins.then_inc(S["gate_psum"], 1)


        def by_token(bank, half=slice(0, HC)):
            return (PS[half, bank, 0:2 * NTXT].rearrange("p (b j) -> p b j", b=2),
                    PS[half, bank, 2 * NTXT:XW].rearrange("p (b j) -> p b j", b=2)[:, :, 0:NB])

        def act_turn_in(act, s, r):
            act.wait_ge(S["xT_psum", s], at(r, 1, 1))
            src = PS[0:HC, 0:2, 0:XW] if s == 0 else PS[0:HC, 2:4, 0:XW]
            nc.scalar.copy(xT[s][:], src).then_inc(S["xT_ready", s], 1)

        def act_query(act, s, r):
            act.wait_ge(S["q_psum", s], at(r, 1, 1))
            for h in range(2):
                for src, c in zip(by_token(FRONT[s][h]), (slice(0, NTXT), slice(NTXT, T))):
                    if s == 0:
                        ins = nc.scalar.activation(q32[0][:, h, :, c], src, ACT.Identity, bias=qbias[:, h:h + 1],
                                                   scale=chan[:, C_SCALE + h:C_SCALE + h + 1])
                    else:
                        ins = nc.scalar.activation(q32[1][:, h, :, c], src, ACT.Identity,
                                                   bias=chan[:, C_FBQ + h:C_FBQ + h + 1])
            ins.then_inc(S["q_f32", s], 1)

        def act_key(act, s, r, before):
            act.wait_ge(S["k_psum", s], at(r, 1, 1))
            if before is not None:
                act.wait_ge(S["k_split", 1 - s], at(before, 1, 1))
            for h in range(2):
                for src, c in zip(by_token(FRONT[s][h]), (slice(0, NTXT), slice(NTXT, T))):
                    if s == 0:
                        ins = nc.scalar.activation(k32[:, h, :, c], src, ACT.Identity, bias=chan[:, C_BK + h:C_BK + h + 1])
                    else:
                        ins = nc.scalar.copy(k32[:, h, :, c], src)
            ins.then_inc(S["k_f32", s], 1)

        def act_max_rows(act, s, r):
            act.wait_ge(S["mT_psum", s], at(r, 1, 1))
            v = mrows[:].rearrange("p (b j) -> p b j", b=2)
            nc.scalar.copy(v[:, :, 0:NTXT], PS[0:3 * HEADS, 3, 0:256].rearrange("p (b j) -> p b j", b=2))
            nc.scalar.copy(v[:, :, NTXT:TP], PS[0:3 * HEADS, 3, 256:384].rearrange("p (b j) -> p b j", b=2))\
                .then_inc(S["m_rows", s], 1)

        def act_exp_pass(act, s, r, moe):
            for u in range(HH):
                if u == PROB_UNITS:
                    act.wait_ge(S["pv_psum", s], at(r, 3, 1))
                for bank in range(3):
                    act.wait_ge(S["e_psum", s], at(r, 3 * HH, 3 * u + bank + 1))
                    nc.scalar.activation(probs[:, u % PROB_UNITS, bank, :], PS[:, bank, 0:T2], ACT.Exp)\
                        .then_inc(S["e_done", s], 1)
                moe.point(("exp", s), u)
                if u % 2 == 0 and u:
                    act_values(act, s, r, u // 2 - 1)
            act_values(act, s, r, HH // 2 - 1)

        def act_values(act, s, r, g):
            act.wait_ge(S["pv_psum", s], at(r, 3, g + 1))
            o = PS[:, 3, 0:T2].rearrange("p (b j) -> p b j", b=2)
            nc.scalar.copy(osb[:, g, 0:2 * NTXT].rearrange("p (b j) -> p b j", b=2), o[:, :, 0:NTXT])
            nc.scalar.copy(osb[:, g, 2 * NTXT:XW].rearrange("p (b j) -> p b j", b=2)[:, :, 0:NB], o[:, :, NTXT:T])\
                .then_inc(S["o_ready", s], 1)

        def act_out(act, s, r, moe):
            moe.point(("turn", s))
            act.wait_ge(S["oc_psum", s], at(r, 1, 1))
            nc.scalar.copy(oT[:], PS[0:HC, 0:2, 0:XW]).then_inc(S["oc_ready", s], 1)
            moe.point(("back", s))

        def act_deviation(act, b, moe):
            act.wait_ge(S["kc_psum"], at(b, 1, 1))
            nc.scalar.copy(kct[:, 0:2, :].rearrange("p i d -> p (i d)"), PS[:, 0, 0:2 * D])
            nc.scalar.copy(kct[0:NB, 2, :], PS[0:NB, 1, 0:D])
            nc.scalar.copy(kct[64:64 + NB, 3, :], PS[64:64 + NB, 1, 0:D]).then_inc(S["kc_ready"], 1)
            moe.point("kc")
            moe.point("g")
            moe.point("u")
            act.wait_ge(S["ss_psum"], at(b, 1, 1))
            ch = chain(act, "act_deviation", b)
            z = rem[:, :, :, 0:T]
            nc.scalar.activation(z, PS[0:HC, 2:4, 0:T2].rearrange("p h (b j) -> p h b j", b=2), ACT.Ln, bias=1e-18,
                                 scale=1.0 / (T - 1)).then_inc(S["ss_read"], 1)
            act.wait_ge(S["ss_read"], at(b, 1, 1))
            ch.link(nc.scalar.activation(z, z, ACT.Exp, scale=0.5))
            ch.link(nc.scalar.activation(z, z, ACT.Ln, bias=EPS / HD ** -0.5))
            nc.scalar.activation(z, z, ACT.Exp, scale=-1.0).then_inc(S["qf_ready"], 1)
            ch.end()

        def act_round(act, a, b, nxt, m, fill):
            moe = moe_of(MoeAct, act, m, fill)
            moe.point("start")
            if b is not None:
                act_turn_in(act, 1, b)
                moe.point("norm")
                act_query(act, 1, b)
                moe.point("query")
                act_key(act, 1, b, a)
                moe.point("key")
                moe.point("value")
                act_deviation(act, b, moe)
                moe.point("ss")
            if a is not None:
                for u in range(HH):
                    moe.point(("max", 0), u)
                moe.point(("split", 0))
                act_max_rows(act, 0, a)
                moe.point(("rows", 0))
                act_exp_pass(act, 0, a, moe)
                moe.point(("out", 0))
            if b is not None:
                for u in range(HH):
                    moe.point(("max", 1), u)
                moe.point(("split", 1))
                act_max_rows(act, 1, b)
            if a is not None:
                act_out(act, 0, a, moe)
                moe.point(("rows", 1))
            if b is not None:
                act_exp_pass(act, 1, b, moe)
                moe.point(("out", 1))
            if b is not None:
                act_out(act, 1, b, moe)
            if nxt is not None:
                act_turn_in(act, 0, nxt)
                moe.point("next turn")
                moe.point("next norm")
                act_query(act, 0, nxt)
                moe.point("next query")
                act_key(act, 0, nxt, b)
            moe.rest()
            if b is not None:
                act.wait_ge(S["x2T_psum"], at(b, 1, 1))
                nc.scalar.copy(x2T[:], PS[0:HC, 2:4, 0:XW]).then_inc(S["x2T_ready"], 1)
                act.wait_ge(S["gl_ready"], at(b, 1, 1))
                nc.scalar.activation(gl[:], gl[:], ACT.Exp).then_inc(S["ge_ready"], 1)


        def dve_norm(dve, ch, x, y, done, gain=None):
            for i in range(3):
                ins = nc.vector.bn_stats(stat[:, 0, i, :], x[:, i, :])
            ch.link(ins)
            plain_wait(dve)
            for i in range(3):
                ins = nc.vector.bn_aggr(mv[:, 0, i, :], stat[:, 0, i, :])
            ch.link(ins)
            ch.link(nc.vector.tensor_scalar(lsc[0][:, 0, :], mv[:, 0, :, 1], EPS, None, ALU.add))
            root(ch, lsc[0][:])
            for i in range(3):
                ins = nc.vector.tensor_scalar(y[:, i, :], x[:, i, :], mv[:, 0, i, 0:1], lsc[0][:, 2, i:i + 1],
                                              ALU.subtract, ALU.mult)
            if gain is not None:
                ch.link(ins)
                ch.link(nc.vector.tensor_tensor(y[:], y[:], row(gain, 3), ALU.mult))
                ins = nc.vector.tensor_tensor(y[:], y[:], row(gain + 1, 3), ALU.add)
            ins.then_inc(done, 1)

        def dve_split(ch, x, parts, done):
            v = [parts[:, :, c].rearrange("p h (b j) -> p h b j", b=2)[:, :, :, 0:T] for c in range(3)]
            ch.link(nc.vector.tensor_copy(v[0], x[:, :, :, 0:T]))
            ch.link(nc.vector.tensor_tensor(rem[:, :, :, 0:T], x[:, :, :, 0:T], v[0], ALU.subtract))
            ch.link(nc.vector.tensor_copy(v[1], rem[:, :, :, 0:T]))
            nc.vector.tensor_tensor(v[2], rem[:, :, :, 0:T], v[1], ALU.subtract).then_inc(done, 1)

        def dve_value(dve, s, r):
            dve.wait_ge(S["v_psum", s], at(r, 1, 1))
            bv = R_FBV if s else R_BV
            bias = rows[:, bv:bv + 1, :].rearrange("p i (h d) -> p i h d", d=HD)
            nc.vector.tensor_tensor(va[s][:, 0:2, :, 0:HD], PS[:, FRONT[s][0], 0:2 * D].rearrange("p (i h d) -> p i h d", i=2, d=HD),
                                    bias.to_broadcast([128, 2, HEADS, HD]), ALU.add)
            for b in range(2):
                t = slice(64 * b, 64 * b + NB)
                ins = nc.vector.tensor_tensor(va[s][t, 2 + b, :, 0:HD],
                                              PS[t, FRONT[s][1], 0:D].rearrange("p (h d) -> p h d", d=HD),
                                              rows[t, bv, :].rearrange("p (h d) -> p h d", d=HD), ALU.add)
            ins.then_inc(S["v_ready", s], 1)

        def dve_front0(dve, r):
            ch = chain(dve, "dve_front0", r)
            dve.wait_ge(S["txt_in"], at(r, 64, 64))
            dve.wait_ge(S["img_in"], at(r, 2, 2))
            dve_norm(dve, ch, h0, xn[0], S["xn_ready", 0])

            def splits(before):
                dve.wait_ge(S["q_f32", 0], at(r, 1, 1))
                if before is not None:
                    dve.wait_ge(S["q_stored", 1], at(before, 16, 16))
                dve_split(ch, q32[0], qs, S["q_split", 0])
                dve.wait_ge(S["q_split", 0], at(r, 1, 1))
                dve.wait_ge(S["k_f32", 0], at(r, 1, 1))
                if before is not None:
                    dve.wait_ge(S["k_stored", 1], at(before, 16, 16))
                dve_split(ch, k32, ks, S["k_split", 0])
                ch.end()
            return splits

        def tok_norm(dve, lo, hi):
            ch = chain(dve, "dve_tok", 1 if lo else 0)
            for q in range(lo, hi):
                ins = nc.vector.bn_stats(tstat[:, q, :], img_tok[:, q, :])
            ch.link(ins)
            for q in range(lo, hi):
                ins = nc.vector.bn_aggr(tmv[:, q, :], tstat[:, q, :])
            ch.link(ins)
            sc = tsc[:, :, lo:hi]
            ch.link(nc.vector.tensor_scalar(sc[:, 0, :], tmv[:, lo:hi, 1], EPS, None, ALU.add))
            root(ch, sc)
            for q in range(lo, hi):
                ins = nc.vector.tensor_scalar(img_tok[:, q, :], img_tok[:, q, :], tmv[:, q, 0:1], tsc[:, 2, q:q + 1],
                                              ALU.subtract, ALU.mult)
            ch.link(ins)
            x = img_tok[:, lo:hi, :]
            ch.link(nc.vector.tensor_tensor(x, x, tok_gain[:, 0:1, :].to_broadcast([128, hi - lo, D]), ALU.mult))
            nc.vector.tensor_tensor(x, x, tok_gain[:, 1:2, :].to_broadcast([128, hi - lo, D]), ALU.add)\
                .then_inc(S["tok_ready"], 1)
            ch.end()

        def dve_norm1(dve, r):
            ch = chain(dve, "dve_norm1", r)
            dve.wait_ge(S["res_ready", 0], at(r, 1, 1))
            dve_norm(dve, ch, h1, xn[1], S["xn_ready", 1])
            ch.end()

        def dve_front1(dve, r, a, moe):
            ch = chain(dve, "dve_front1", r)
            dve.wait_ge(S["xT_ready", 1], at(r, 1, 1))
            nc.vector.tensor_reduce(xbar[:, 0], text(xT[1]), AX.X, ALU.add)
            ch.link(nc.vector.tensor_reduce(xbar[:, 1], images(xT[1]), AX.X, ALU.add))
            ch.link(nc.vector.tensor_tensor(xbar[:, 0], xbar[:, 0], xbar[:, 1], ALU.add))
            ch.link(nc.vector.tensor_scalar(xbar[:, 0], xbar[:, 0], 1.0 / T, None, ALU.mult))
            mean = xbar[:, 0].unsqueeze(3)
            nc.vector.tensor_tensor(text(xc), text(xT[1]), mean.to_broadcast([HC, 2, 2, NTXT]), ALU.subtract)
            nc.vector.tensor_tensor(images(xc, 64), images(xT[1], 64), mean.to_broadcast([HC, 2, 2, 64]),
                                    ALU.subtract).then_inc(S["xc_ready"], 1)
            moe.start()
            moe.point("norm")
            moe.point("query")
            dve.wait_ge(S["k_f32", 1], at(r, 1, 1))
            if a is not None:
                dve.wait_ge(S["k_stored", 0], at(a, 16, 16))
            dve_split(ch, k32, ks, S["k_split", 1])
            moe.point("key")
            dve_value(dve, 1, r)
            moe.point("value")
            moe.point("kc")
            dve.wait_ge(S["g_psum"], at(r, 1, 1))
            nc.vector.tensor_tensor(gsb[:], PS[0:HC, 2, 0:4 * HC].rearrange("p (i c) -> p i c", i=4),
                                    same_head[:].unsqueeze(1).to_broadcast([HC, 4, HC]), ALU.mult).then_inc(S["g_ready"], 1)
            moe.point("g")
            dve.wait_ge(S["u_psum"], at(r, 1, 1))
            dve.wait_ge(S["k_split", 1], at(r, 1, 1))
            nc.vector.tensor_tensor(rem[:, :, :, 0:T], PS[0:HC, 0:2, 0:T2].rearrange("p h (b j) -> p h b j", b=2),
                                    q32[1][:, :, :, 0:T], ALU.mult).then_inc(S["prod_ready"], 1)
            moe.point("u")

            def query(a):
                dve.wait_ge(S["qf_ready"], at(r, 1, 1))
                ch.link(nc.vector.scalar_tensor_tensor(out=q32[1][:, :, :, 0:T], in0=q32[1][:, :, :, 0:T],
                                                       scalar=chan[:, C_GAMMA:C_GAMMA + 1], in1=rem[:, :, :, 0:T],
                                                       op0=ALU.mult, op1=ALU.mult))
                if a is not None:
                    dve.wait_ge(S["q_stored", 0], at(a, 16, 16))
                dve_split(ch, q32[1], qs, S["q_split", 1])
                ch.end()
            return query

        def dve_max_pass(dve, s, r, moe):
            for u in range(HH):
                for g in range(3):
                    dve.wait_ge(S["s_psum", s], at(r, 3 * HH, 3 * u + g + 1))
                    out = mx[:, 0:2, 2 * u + g] if g < 2 else mx[:, 2, 2 * u:2 * u + 2]
                    nc.vector.tensor_reduce(out, PS[:, g, 0:T2].rearrange("p (b j) -> p b j", b=2), AX.X, ALU.max)\
                        .then_inc(S["s_used", s], 1)
                moe.point(("max", s), u)
            ch = chain(dve, f"dve_max{s}", r)
            dve.wait_ge(S["s_used", s], at(r, 3 * HH, 3 * HH))
            ch.link(nc.vector.tensor_scalar(mneg[:], mx[:], -1.0, None, ALU.mult))
            for c in range(3):
                ch.link(nc.vector.tensor_copy(mbf[:], mneg[:]))
                ins = nc.vector.tensor_copy(mpart[:, :, c, :], mbf[:])
                if c < 2:
                    ch.link(ins)
                    ch.link(nc.vector.tensor_tensor(mneg[:], mneg[:], mbf[:], ALU.subtract))
            ins.then_inc(S["m_split", s], 1)
            ch.end()

        def dve_out(dve, s, r, moe):
            ch = chain(dve, f"dve_out{s}", r)
            dve.wait_ge(S["oT_psum", s], at(r, 1, 1))
            o = PS[:, 0:3, 0:384].rearrange("p i (h c) -> p i h c", c=32)
            ch.link(nc.vector.reciprocal(rs[:].unsqueeze(3), o[:, :, :, HD:HD + 1]))
            nc.vector.tensor_tensor(on[:].rearrange("p i (h d) -> p i h d", d=HD), o[:, :, :, 0:HD],
                                    rs[:].unsqueeze(3).to_broadcast([128, 3, HEADS, HD]), ALU.mult)\
                .then_inc(S["on_ready", s], 1)
            moe.point(("turn", s))
            moe.point(("back", s))
            dve.wait_ge(S["pr_psum", s], at(r, 1, 1))
            out, res, bo = (x2, xn[1], R_BO) if s else (h1, h0, R_BP)
            if s == 0 and not (isinstance(r, int) and r == 0):
                dve.wait_ge(S["h1_kept"], at(r, 1, 0))
            for i, (lo, hi) in enumerate(((0, 2), (2, 3))):
                src = PS[:, (2, 3)[i], 0:(hi - lo) * D].rearrange("p (i d) -> p i d", d=D)
                ins = nc.vector.tensor_tensor(out[:, lo:hi, :], src, row(bo, hi - lo), ALU.add)
            ins.then_inc(S["pr_read", s], 1)
            dve.wait_ge(S["pr_read", s], at(r, 1, 1))
            nc.vector.tensor_tensor(out[:], out[:], res[:], ALU.add).then_inc(S["res_ready", s], 1)
            ch.end()

        def dve_gate(dve, b, ch):
            dve.wait_ge(S["gate_psum"], at(b, 1, 1))
            nc.vector.tensor_tensor(gl[:], PS[:, 2, 0:3 * E].rearrange("p (i e) -> p i e", e=E),
                                    bg[:].unsqueeze(1).to_broadcast([128, 3, E]), ALU.add).then_inc(S["gate_used"], 1)
            dve.wait_ge(S["gate_used"], at(b, 1, 1))
            ch.link(nc.vector.tensor_reduce(gs[:, :, 0], gl[:], AX.X, ALU.max))
            nc.vector.tensor_tensor(gl[:], gl[:], gs[:, :, 0:1].to_broadcast([128, 3, E]), ALU.subtract)\
                .then_inc(S["gl_ready"], 1)
            dve.wait_ge(S["ge_ready"], at(b, 1, 1))
            ch.link(nc.vector.tensor_reduce(gs[:, :, 0], gl[:], AX.X, ALU.add))
            ch.link(nc.vector.reciprocal(gs[:, :, 1], gs[:, :, 0]))
            ch.link(nc.vector.tensor_tensor(gl[:], gl[:], gs[:, :, 1:2].to_broadcast([128, 3, E]), ALU.mult))
            mine, other = gl[:].unsqueeze(3).to_broadcast([128, 3, E, E]), gl[:].unsqueeze(2).to_broadcast([128, 3, E, E])
            ch.link(nc.vector.tensor_tensor(cmp1[:], other, mine, ALU.is_gt))
            ch.link(nc.vector.tensor_tensor(cmp2[:], other, mine, ALU.is_equal))
            ch.link(nc.vector.tensor_tensor(cmp2[:], cmp2[:],
                                            lower[:].rearrange("p (i e) -> p i e", e=E).unsqueeze(1).to_broadcast([128, 3, E, E]),
                                            ALU.mult))
            ch.link(nc.vector.tensor_tensor(cmp1[:], cmp1[:], cmp2[:], ALU.add))
            ch.link(nc.vector.tensor_reduce(comb[:], cmp1[:], AX.X, ALU.add))
            ch.link(nc.vector.tensor_scalar(comb[:], comb[:], 1.5, None, ALU.is_lt))
            nc.vector.tensor_tensor(comb[:], comb[:], gl[:], ALU.mult).then_inc(S["comb_ready"], 1)
            ch.end()

        def dve_round(dve, a, b, nxt, m, fill):
            moe = moe_of(MoeDve, dve, m, fill)
            moe.point("start")
            if b is not None:
                query = dve_front1(dve, b, a, moe)
                moe.point("ss")
            else:
                moe.start()
            if a is not None:
                dve_max_pass(dve, 0, a, moe)
                moe.point(("split", 0))
            if b is not None:
                query(a)
            if a is not None:
                moe.point(("rows", 0))
                for u in range(HH):
                    moe.point(("exp", 0), u)
                moe.point(("out", 0))
            if b is not None:
                dve_max_pass(dve, 1, b, moe)
                moe.point(("split", 1))
            if a is not None:
                dve_out(dve, 0, a, moe)
                moe.point(("rows", 1))
            if b is not None:
                for u in range(HH):
                    moe.point(("exp", 1), u)
                moe.point(("out", 1))
            if nxt is not None:
                splits = dve_front0(dve, nxt)
            if b is not None:
                dve_out(dve, 1, b, moe)
                if nxt is not None:
                    moe.point("next turn")
                ch = chain(dve, "dve_x2", b)
                dve.wait_ge(S["res_ready", 1], at(b, 1, 1))
                dve_norm(dve, ch, x2, x2, S["x2_ready"], R_L1G)
            if nxt is not None:
                moe.point("next norm")
            if a is not None:
                dve_norm1(dve, a)
            if nxt is not None:
                moe.point("next query")
                splits(b)
            moe.rest()
            if nxt is not None:
                dve_value(dve, 0, nxt)
            if b is not None:
                dve_gate(dve, b, ch)
            moe.finish()


        def image(pool, r):
            for b in range(2):
                t = slice(64 * b, 64 * b + NI)
                nc.gpsimd.tensor_copy(h0[t, 2, :], img_tok[t, r, :]).then_inc(S["img_in"], 1)
                pool.wait_ge(S["img_in"], at(r, 2, b + 1))
                plain_wait(pool)

        def pool_round(pool, a, b, nxt, m, _):
            if m is not None:
                pool.wait_ge(S["h1_kept"], at(m, 1, 1))
                pool.wait_ge(S["stored"], at(m, 80, 1))
                plain_wait(pool)
                nc.gpsimd.tensor_copy(h1_fin[:], h1_keep[:]).then_inc(S["fin_h1"], 1)
            if b is not None:
                pool.wait_ge(S["res_ready", 0], at(b, 1, 1))
                if m is not None:
                    pool.wait_ge(S["fin_h1"], at(m, 1, 1))
                plain_wait(pool)
                nc.gpsimd.tensor_copy(h1_keep[:], h1[:]).then_inc(S["h1_kept"], 1)
            if nxt is not None:
                pool.wait_ge(S["res_ready", 0], at(a, 1, 1))
                plain_wait(pool)
                image(pool, nxt)


        def load_text(sp, r):
            for b in range(2):
                sp.dma_start(h0[:, b, :], a["txt"][r, b]).then_inc(S["txt_in"], 16)
                sp.dma_start(h0[64 * b + NI:64 * b + NB, 2, :], a["cls"]).then_inc(S["txt_in"], 16)

        def stack(sp, s, r, which):
            x, scr, st = (qs, scr_q[s], qst[s]) if which == "q" else (ks, scr_k[s], kst[s])
            sp.wait_ge(S[f"{which}_split", s], at(r, 1, 1))
            sp.dma_start(scr.rearrange("h c d (g j) -> (d g) h c j", g=HH), x[:]).then_inc(S[f"{which}_stored", s], 16)
            sp.wait_ge(S[f"{which}_stored", s], at(r, 16, 16))
            for t, c, n in K_RUNS if which == "k" else Q_RUNS:
                sp.dma_start(st[HD * t:HD * (t + n), :, :].rearrange("p (h g) j -> p h (g j)", h=2),
                             scr[:, c:c + n].rearrange("h c d x -> (c d) h x")).then_inc(S[f"{which}_stacked", s], 16)

        def stack_max(sp, s, r):
            sp.wait_ge(S["m_rows", s], at(r, 1, 1))
            for c in range(3):
                sp.dma_start(qst[s][SROWS + c:SROWS + c + 1, :, :], mrows[HEADS * c:HEADS * c + HEADS, :])\
                    .then_inc(S["m_stacked", s], 16)

        def store_pair(sp, m):
            sp.wait_ge(S["fin_ready"], at(m, 1, 1))
            out = a["out"][m]
            sp.dma_start(out[:, NB:T, :].rearrange("b t d -> t b d"), fin[:, 0:2, :]).then_inc(S["stored"], 16)
            for b in range(2):
                sp.dma_start(out[b, 1:NB, :], fin[64 * b:64 * b + NI, 2, :]).then_inc(S["stored"], 16)
                sp.dma_start(out[b, 0:1, :], fin[64 * b + NI:64 * b + NB, 2, :]).then_inc(S["stored"], 16)

        def sp_round(sp, a, b, nxt, m, _):
            if b is not None:
                stack(sp, 1, b, "k")
            if a is not None:
                stack_max(sp, 0, a)
            if b is not None:
                stack(sp, 1, b, "q")
                stack_max(sp, 1, b)
            if nxt is not None:
                sp.wait_ge(S["res_ready", 0], at(a, 1, 1))
                load_text(sp, nxt)
                stack(sp, 0, nxt, "q")
                stack(sp, 0, nxt, "k")
            if m is not None:
                store_pair(sp, m)

        def rounds(eng, one_round):
            one_round(eng, 0, None, 1, None, FILL)
            one_round(eng, 1, 0, 2, None, FILL)
            with eng.Fori(1, PAIRS - 2) as p:
                one_round(eng, p + 1, p, p + 2, p - 1, FILL)
            one_round(eng, PAIRS - 1, PAIRS - 2, None, PAIRS - 3, FILL_A7)
            one_round(eng, None, PAIRS - 1, None, PAIRS - 2, FILL_B7)
            one_round(eng, None, None, None, PAIRS - 1, FILL)

        with nc.Block() as block:
            @block.sync
            def _(sp):
                sp.wait_ge(S["preset"], 2)
                load_text(sp, 0)
                stack(sp, 0, 0, "q")
                stack(sp, 0, 0, "k")
                rounds(sp, sp_round)
                sp.wait_ge(S["stored"], at(PAIRS, 80, 1))

            @block.tensor
            def _(pe):
                pe.wait_ge(ld_attn, 16)
                pe.wait_ge(ld_moe, 32)
                pe.wait_ge(casts, 1)
                pe.wait_ge(S["preset"], 2)
                pe_turn_in(pe, 0, 0)
                pe_query(pe, 0, 0)
                pe_key(pe, 0, 0)
                pe_value(pe, 0, 0)
                rounds(pe, pe_round)

            @block.scalar
            def _(act):
                act_turn_in(act, 0, 0)
                act_query(act, 0, 0)
                act_key(act, 0, 0, None)
                rounds(act, act_round)

            @block.vector
            def _(dve):
                for x in (qs, ks):
                    v = x[:].rearrange("p h c (b j) -> p (h c b) j", b=2)[:, :, T:TP]
                    ins = nc.vector.memset(v, 0.0)
                ins.then_inc(S["preset"], 1)
                nc.vector.memset(rs[:], 0.0).then_inc(S["stored"], 1)
                tok_norm(dve, 0, 1)
                splits = dve_front0(dve, 0)
                tok_norm(dve, 1, PAIRS)
                splits(None)
                dve_value(dve, 0, 0)
                rounds(dve, dve_round)

            @block.gpsimd
            def _(pool):
                nc.gpsimd.memset(h0[:, 2, :], 0.0)
                nc.gpsimd.memset(kct[:], 0.0)
                nc.gpsimd.memset(osb[:, :, 2 * NTXT:XW], 1.0)
                nc.gpsimd.memset(hid[0][:, XN:XW], 0.0)
                nc.gpsimd.memset(hid[1][:, XN:XW], 0.0).then_inc(S["preset"], 1)
                pool.wait_ge(S["preset"], 2)
                pool.wait_ge(S["tok_ready"], 1)
                image(pool, 0)
                pool.wait_ge(S["tok_ready"], 2)
                rounds(pool, pool_round)



def _haar():
    isq2 = float(np.float32(0.7071067811865476))
    f = np.arange(256)
    y, x = np.divmod(np.arange(256), 16)
    h = np.full((256, 256), isq2 ** 8)
    for level in range(4):
        digit = (f >> (2 * (3 - level))) & 3
        w_hi, h_hi = digit >> 1, digit & 1
        h = h * np.where((w_hi[:, None] & (x[None] >> level) & 1) == 1, -1.0, 1.0)
        h = h * np.where((h_hi[:, None] & (y[None] >> level) & 1) == 1, -1.0, 1.0)
    return h.astype(np.float32)


def _layout(i):
    f = {k: np.asarray(v) for k, v in i.items()}

    def halves(v):
        return np.reshape(v, (2, HC)).T

    def chunk(m, r=HC):
        return np.reshape(m, (-1, r, m.shape[-1])).transpose(1, 0, 2)

    turn = np.arange(D).reshape(2, HH, HD).transpose(0, 2, 1).reshape(-1)
    o = {}
    o["x_cols"] = chunk(f["x"].reshape(B, CIN, G7, PATCH, G7, PATCH).transpose(1, 3, 5, 0, 2, 4).reshape(-1, NPOS), 128)
    o["pl_cols"] = chunk(f["L0_tok_pl_w"].reshape(D, -1).T, 128)
    o["pg_bands"] = chunk(f["L0_tok_pg_w1"].reshape(D, 256, CIN).transpose(2, 1, 0).reshape(-1, D), 128)
    o["haar"] = chunk(_haar(), 128)
    o["ident"] = np.eye(128, dtype=np.float32)
    t = {}
    chan = np.zeros((HC, NCH), np.float32)
    scale = np.repeat(f["L0_attn_scale"], HD)
    bqkv = f["L0_attn_b_qkv"].reshape(3, D)
    for c, v in ((C_PLB, f["L0_tok_pl_b"]), (C_PGB, f["L0_tok_pg_b1"]), (C_PLP, f["L0_tok_pl_pwb"]),
                 (C_PGP, f["L0_tok_pg_pwb"]), (C_PGB2, f["L0_tok_pg_b2"]), (C_ALPHA, f["L0_tok_alpha"].reshape(D)),
                 (C_F1, f["L0_tok_f1_pwb"]), (C_F2, f["L0_tok_f2_pwb"]), (C_BQ, bqkv[0][turn]), (C_BK, bqkv[1][turn]),
                 (C_SCALE, scale[turn]), (C_FBQ, f["L0_ffn_bq"][turn]),
                 (C_GAMMA, np.broadcast_to(f["L0_ffn_gamma"], (D,)))):
        chan[:, c:c + 2] = halves(v)
    for r, name in enumerate(("pl", "pg", "f1", "f2", "f3")):
        w = f[f"L0_tok_{name}_dw"].reshape(2, HC, 9).transpose(1, 0, 2).reshape(HC, 18)
        chan[:, C_DW + 18 * r:C_DW + 18 * r + 18] = w
    o["chan"] = chan
    pws = [f[f"L0_tok_{n}_pw"].reshape(D, D).T for n in ("pl", "pg", "f1", "f2", "f3")] + [f["L0_tok_pg_w2"].reshape(D, D).T]
    o["w_pw"] = np.stack([chunk(w) for w in pws], 1)
    wqkv = f["L0_attn_w_qkv"]
    ws = [wqkv[:, 0:D][:, turn], wqkv[:, D:2 * D][:, turn], wqkv[:, 2 * D:], f["L0_attn_w_proj"],
          f["L0_ffn_Wq"].T[:, turn], f["L0_ffn_Wk"].T[:, turn], f["L0_ffn_Wv"].T, f["L0_ffn_Wo"].T]
    o["w_at"] = np.stack([chunk(w) for w in ws], 1)
    o["f3_bias"] = np.broadcast_to(f["L0_tok_f3_pwb"].reshape(1, 1, D), (128, 1, D))
    o["tok_gain"] = np.broadcast_to(np.stack([f["L0_tok_ln_g"], f["L0_tok_ln_b"]])[None], (128, 2, D))
    rows = [bqkv[2], f["L0_attn_b_proj"], f["L0_ffn_bv"],
            f["L0_ffn_bo"], f["L0_ffn_ln1_g"], f["L0_ffn_ln1_b"], f["L0_ffn_ln2_g"], f["L0_ffn_ln2_b"], *f["L0_ffn_b2"]]
    o["rows"] = np.broadcast_to(np.stack(rows)[None], (128, NROW, D))
    masks = np.zeros((128, T2), np.float32)
    for j in range(128):
        masks[j, [j, NTXT + j]] = BIG
    for b in range(2):
        for j in range(NI):
            masks[64 * b + j, [2 * NTXT + j, 2 * NTXT + NB + j]] = BIG
    o["masks"] = masks
    head = np.arange(HC) % HH
    o["same_head"] = (head[:, None] == head[None]).astype(np.float32)
    low = np.tril(np.ones((E, E), np.float32), -1)
    o["lower"] = np.broadcast_to(low.reshape(1, -1), (128, E * E))
    o["bg"] = np.broadcast_to(f["L0_ffn_bg"][None], (128, E))
    o["gate_w"] = chunk(f["L0_ffn_Wg"].T)
    o["b1"] = f["L0_ffn_b1"].reshape(UNITS, 128).T
    o["w1"] = chunk(f["L0_ffn_W1"].transpose(1, 0, 2).reshape(D, E * FF))
    o["w2"] = chunk(f["L0_ffn_W2"].reshape(E * FF, D), 128)
    o["cls"] = f["L0_tok_cls"].reshape(1, D)
    o["txt"] = f["txt"].reshape(PAIRS, 2, NTXT, D)
    return {k: np.ascontiguousarray(v) for k, v in o.items()}


def kernel(**inputs):
    import concourse.bacc as _bacc
    from concourse.bass_utils import run_bass_kernel_spmd as _run

    nc = _bacc.Bacc("TRN2", target_bir_lowering=False, num_devices=1)
    arrays = _layout(inputs)
    aps = {k: nc.dram_tensor(f"in_{k}", v.shape, F32, kind="ExternalInput").ap() for k, v in arrays.items()}
    aps["out"] = nc.dram_tensor("out", (PAIRS, 2, T, D), F32, kind="ExternalOutput").ap()
    build(nc, aps)
    r = _run(nc, [{f"in_{k}": v for k, v in arrays.items()}], core_ids=[0])
    return r.results[0]["out"].reshape(B, T, D)
```
